# Optimizing a Trainium2 kernel written in Bass

```python
import numpy as np
import jax
import jax.numpy as jnp

def _softmax(x, axis=-1):
    return jax.nn.softmax(x, axis=axis)

def _gelu(x):
    return jax.nn.gelu(x, approximate=True)

def _silu(x):
    return jax.nn.silu(x)

def _sigmoid(x):
    return jax.nn.sigmoid(x)

def _layernorm(x, axis=-1, eps=1e-05):
    m = jnp.mean(x, axis=axis, keepdims=True)
    v = jnp.var(x, axis=axis, keepdims=True)
    return (x - m) / jnp.sqrt(v + eps)

def _scatter_add(tgt, idx, src, axis=0):
    return tgt.at[idx].add(src)

def _segment_sum(src, seg, n):
    return jax.ops.segment_sum(src, seg, n)
kernel_name = 'mk_gnn_resnorm_d2_gnn_r64_0732ed'

def setup_inputs(seed: int=0):
    np.random.seed(seed)
    _w = jnp.asarray

    def _rec_inputs():
        import jax
        import jax.numpy as jnp
        _gk = jax.random.key(seed)
        x = -0.000202 + 1 * jax.random.normal(jax.random.fold_in(_gk, 1), (100000, 64), jnp.float32)
        src = jax.random.randint(jax.random.fold_in(_gk, 2), (50000,), 0, 100000, jnp.int32)
        dst = jnp.minimum((100000 * jax.random.uniform(jax.random.fold_in(_gk, 3), (50000,)) ** 2.0).astype(jnp.int32), 99999)
        _o = jnp.argsort(dst, stable=True)
        src = src[_o]
        dst = dst[_o]
        edge_attr_32 = -5.3897e-05 + 0.999841 * jax.random.normal(jax.random.fold_in(_gk, 12), (50000, 32), jnp.float32)
        return (x, src, dst, edge_attr_32)
    x, src, dst, edge_attr_32 = _rec_inputs()

    def _L0_gnn_setup():
        import jax, jax.numpy as jnp
        import numpy as np
        N_NODES = 100000

        def _inv_sqrt_deg(counts):
            return jnp.where(counts > 0, jax.lax.rsqrt(jnp.maximum(counts, 1.0)), 0.0)

        def _graph_conv(x, src, dst, out_norm_src, in_norm_dst, W, b):
            xn = x * out_norm_src[:, None]
            msg = xn[src]
            agg = jax.ops.segment_sum(msg, dst, num_segments=N_NODES)
            agg = agg * in_norm_dst[:, None]
            return agg @ W + b
        key = jax.random.key(seed)
        ks = jax.random.split(key, 7)
        E = 25000
        d_in, d_hid, d_out = (64, 64, 64)
        x = jax.random.normal(ks[0], (N_NODES, d_in), dtype=jnp.float32)
        edge_src = jax.random.randint(ks[1], (E,), 0, N_NODES, dtype=jnp.int64)
        edge_dst = jax.random.randint(ks[2], (E,), 0, N_NODES, dtype=jnp.int64)
        W1 = jax.random.normal(ks[3], (d_in, d_hid), dtype=jnp.float32) * (1.0 / np.sqrt(d_in))
        b1 = jnp.zeros((d_hid,), dtype=jnp.float32)
        W2 = jax.random.normal(ks[4], (d_hid, d_out), dtype=jnp.float32) * (1.0 / np.sqrt(d_hid))
        b2 = jnp.zeros((d_out,), dtype=jnp.float32)
        return {'x': x, 'edge_src': edge_src, 'edge_dst': edge_dst, 'W1': W1, 'b1': b1, 'W2': W2, 'b2': b2}
    _L0_gnn_all = _L0_gnn_setup()
    _L0_gnn_in = {k: v for k, v in _L0_gnn_all.items() if k in ('W1', 'b1', 'W2', 'b2')}
    del _L0_gnn_all

    def _L1_gnn_setup():
        import jax, jax.numpy as jnp
        import numpy as np
        N = 50000
        E = 12500
        DIN = 64
        DE = 32
        HID = 32
        DOUT = 64

        def _lin_init(key, fan_in, fan_out):
            return jax.random.normal(key, (fan_in, fan_out), dtype=jnp.float32) / np.sqrt(fan_in)

        def _transformer_conv(x, src, dst, eattr, Wq, bq, Wk, bk, Wv, bv, We, Ws, bs, H, C, concat):
            n = x.shape[0]
            q = (x @ Wq + bq).reshape(n, H, C)
            k = (x @ Wk + bk).reshape(n, H, C)
            v = (x @ Wv + bv).reshape(n, H, C)
            e = (eattr @ We).reshape(-1, H, C)
            kj = k[src] + e
            alpha = jnp.sum(q[dst] * kj, axis=-1) / jnp.sqrt(jnp.float32(C))
            m = jax.ops.segment_max(alpha, dst, num_segments=n)
            a = jnp.exp(alpha - m[dst])
            s = jax.ops.segment_sum(a, dst, num_segments=n)
            a = a / (s[dst] + 1e-16)
            vj = v[src] + e
            out = jax.ops.segment_sum(a[..., None] * vj, dst, num_segments=n)
            out = out.reshape(n, H * C) if concat else jnp.mean(out, axis=1)
            return out + x @ Ws + bs
        key = jax.random.key(seed)
        ks = list(jax.random.split(key, 64))
        inp = {}
        inp['x'] = jax.random.normal(ks[0], (N, DIN), dtype=jnp.float32)
        inp['edge_attr'] = jax.random.normal(ks[1], (E, DE), dtype=jnp.float32)
        inp['edge_index'] = jax.random.randint(ks[2], (2, E), 0, N, dtype=jnp.int32)
        dims = [(DIN, 2, HID, 2 * HID), (2 * HID, 2, HID, 2 * HID), (2 * HID, 1, DOUT, DOUT)]
        ki = 3
        for l, (din, H, C, dskip) in enumerate(dims):
            HC = H * C
            inp[f'Wq{l}'] = _lin_init(ks[ki], din, HC)
            ki += 1
            inp[f'bq{l}'] = jnp.zeros((HC,), jnp.float32)
            inp[f'Wk{l}'] = _lin_init(ks[ki], din, HC)
            ki += 1
            inp[f'bk{l}'] = jnp.zeros((HC,), jnp.float32)
            inp[f'Wv{l}'] = _lin_init(ks[ki], din, HC)
            ki += 1
            inp[f'bv{l}'] = jnp.zeros((HC,), jnp.float32)
            inp[f'We{l}'] = _lin_init(ks[ki], DE, HC)
            ki += 1
            inp[f'Ws{l}'] = _lin_init(ks[ki], din, dskip)
            ki += 1
            inp[f'bs{l}'] = jnp.zeros((dskip,), jnp.float32)
        inp['prelu_a'] = jnp.asarray(0.25, dtype=jnp.float32)
        return inp
    _L1_gnn_all = _L1_gnn_setup()
    _L1_gnn_in = {k: v for k, v in _L1_gnn_all.items() if k in ('Wq0', 'bq0', 'Wk0', 'bk0', 'Wv0', 'bv0', 'We0', 'Ws0', 'bs0', 'Wq1', 'bq1', 'Wk1', 'bk1', 'Wv1', 'bv1', 'We1', 'Ws1', 'bs1', 'Wq2', 'bq2', 'Wk2', 'bk2', 'Wv2', 'bv2', 'We2', 'Ws2', 'bs2', 'prelu_a')}
    del _L1_gnn_all
    return {'x': x, 'src': src, 'dst': dst, 'edge_attr_32': edge_attr_32, 'L0_gnn_W1': _L0_gnn_in['W1'], 'L0_gnn_b1': _L0_gnn_in['b1'], 'L0_gnn_W2': _L0_gnn_in['W2'], 'L0_gnn_b2': _L0_gnn_in['b2'], 'L1_gnn_Wq0': _L1_gnn_in['Wq0'], 'L1_gnn_bq0': _L1_gnn_in['bq0'], 'L1_gnn_Wk0': _L1_gnn_in['Wk0'], 'L1_gnn_bk0': _L1_gnn_in['bk0'], 'L1_gnn_Wv0': _L1_gnn_in['Wv0'], 'L1_gnn_bv0': _L1_gnn_in['bv0'], 'L1_gnn_We0': _L1_gnn_in['We0'], 'L1_gnn_Ws0': _L1_gnn_in['Ws0'], 'L1_gnn_bs0': _L1_gnn_in['bs0'], 'L1_gnn_Wq1': _L1_gnn_in['Wq1'], 'L1_gnn_bq1': _L1_gnn_in['bq1'], 'L1_gnn_Wk1': _L1_gnn_in['Wk1'], 'L1_gnn_bk1': _L1_gnn_in['bk1'], 'L1_gnn_Wv1': _L1_gnn_in['Wv1'], 'L1_gnn_bv1': _L1_gnn_in['bv1'], 'L1_gnn_We1': _L1_gnn_in['We1'], 'L1_gnn_Ws1': _L1_gnn_in['Ws1'], 'L1_gnn_bs1': _L1_gnn_in['bs1'], 'L1_gnn_Wq2': _L1_gnn_in['Wq2'], 'L1_gnn_bq2': _L1_gnn_in['bq2'], 'L1_gnn_Wk2': _L1_gnn_in['Wk2'], 'L1_gnn_bk2': _L1_gnn_in['bk2'], 'L1_gnn_Wv2': _L1_gnn_in['Wv2'], 'L1_gnn_bv2': _L1_gnn_in['bv2'], 'L1_gnn_We2': _L1_gnn_in['We2'], 'L1_gnn_Ws2': _L1_gnn_in['Ws2'], 'L1_gnn_bs2': _L1_gnn_in['bs2'], 'L1_gnn_prelu_a': _L1_gnn_in['prelu_a']}

def reference(x, src, dst, edge_attr_32, L0_gnn_W1, L0_gnn_b1, L0_gnn_W2, L0_gnn_b2, L1_gnn_Wq0, L1_gnn_bq0, L1_gnn_Wk0, L1_gnn_bk0, L1_gnn_Wv0, L1_gnn_bv0, L1_gnn_We0, L1_gnn_Ws0, L1_gnn_bs0, L1_gnn_Wq1, L1_gnn_bq1, L1_gnn_Wk1, L1_gnn_bk1, L1_gnn_Wv1, L1_gnn_bv1, L1_gnn_We1, L1_gnn_Ws1, L1_gnn_bs1, L1_gnn_Wq2, L1_gnn_bq2, L1_gnn_Wk2, L1_gnn_bk2, L1_gnn_Wv2, L1_gnn_bv2, L1_gnn_We2, L1_gnn_Ws2, L1_gnn_bs2, L1_gnn_prelu_a):
    import jax
    import jax.numpy as jnp

    def _L0_gnn_ref(x, edge_src, edge_dst, W1, b1, W2, b2):
        import jax, jax.numpy as jnp
        import numpy as np
        N_NODES = 100000

        def _inv_sqrt_deg(counts):
            return jnp.where(counts > 0, jax.lax.rsqrt(jnp.maximum(counts, 1.0)), 0.0)

        def _graph_conv(x, src, dst, out_norm_src, in_norm_dst, W, b):
            xn = x * out_norm_src[:, None]
            msg = xn[src]
            agg = jax.ops.segment_sum(msg, dst, num_segments=N_NODES)
            agg = agg * in_norm_dst[:, None]
            return agg @ W + b
        ones = jnp.ones(edge_src.shape, dtype=x.dtype)
        out_deg = jax.ops.segment_sum(ones, edge_src, num_segments=N_NODES)
        in_deg = jax.ops.segment_sum(ones, edge_dst, num_segments=N_NODES)
        src_norm = _inv_sqrt_deg(out_deg)
        dst_norm = _inv_sqrt_deg(in_deg)
        h = jax.nn.relu(_graph_conv(x, edge_src, edge_dst, src_norm, dst_norm, W1, b1))
        h = jax.nn.relu(_graph_conv(h, edge_src, edge_dst, src_norm, dst_norm, W2, b2))
        return h

    def _L1_gnn_ref(x, edge_attr, edge_index, Wq0, bq0, Wk0, bk0, Wv0, bv0, We0, Ws0, bs0, Wq1, bq1, Wk1, bk1, Wv1, bv1, We1, Ws1, bs1, Wq2, bq2, Wk2, bk2, Wv2, bv2, We2, Ws2, bs2, prelu_a):
        import jax, jax.numpy as jnp
        import numpy as np
        N = 50000
        E = 12500
        DIN = 64
        DE = 32
        HID = 32
        DOUT = 64

        def _lin_init(key, fan_in, fan_out):
            return jax.random.normal(key, (fan_in, fan_out), dtype=jnp.float32) / np.sqrt(fan_in)

        def _transformer_conv(x, src, dst, eattr, Wq, bq, Wk, bk, Wv, bv, We, Ws, bs, H, C, concat):
            n = x.shape[0]
            q = (x @ Wq + bq).reshape(n, H, C)
            k = (x @ Wk + bk).reshape(n, H, C)
            v = (x @ Wv + bv).reshape(n, H, C)
            e = (eattr @ We).reshape(-1, H, C)
            kj = k[src] + e
            alpha = jnp.sum(q[dst] * kj, axis=-1) / jnp.sqrt(jnp.float32(C))
            m = jax.ops.segment_max(alpha, dst, num_segments=n)
            a = jnp.exp(alpha - m[dst])
            s = jax.ops.segment_sum(a, dst, num_segments=n)
            a = a / (s[dst] + 1e-16)
            vj = v[src] + e
            out = jax.ops.segment_sum(a[..., None] * vj, dst, num_segments=n)
            out = out.reshape(n, H * C) if concat else jnp.mean(out, axis=1)
            return out + x @ Ws + bs
        src, dst = (edge_index[0], edge_index[1])
        h = _transformer_conv(x, src, dst, edge_attr, Wq0, bq0, Wk0, bk0, Wv0, bv0, We0, Ws0, bs0, 2, HID, True)
        h = jnp.where(h >= 0, h, prelu_a * h)
        h = _transformer_conv(h, src, dst, edge_attr, Wq1, bq1, Wk1, bk1, Wv1, bv1, We1, Ws1, bs1, 2, HID, True)
        h = jnp.where(h >= 0, h, prelu_a * h)
        h = _transformer_conv(h, src, dst, edge_attr, Wq2, bq2, Wk2, bk2, Wv2, bv2, We2, Ws2, bs2, 1, DOUT, False)
        return h
    edge_index = jnp.stack([src, dst])
    x = _layernorm(x + _L0_gnn_ref(x, src, dst, L0_gnn_W1, L0_gnn_b1, L0_gnn_W2, L0_gnn_b2), axis=-1)
    x = _layernorm(x + _L1_gnn_ref(x, edge_attr_32, edge_index, L1_gnn_Wq0, L1_gnn_bq0, L1_gnn_Wk0, L1_gnn_bk0, L1_gnn_Wv0, L1_gnn_bv0, L1_gnn_We0, L1_gnn_Ws0, L1_gnn_bs0, L1_gnn_Wq1, L1_gnn_bq1, L1_gnn_Wk1, L1_gnn_bk1, L1_gnn_Wv1, L1_gnn_bv1, L1_gnn_We1, L1_gnn_Ws1, L1_gnn_bs1, L1_gnn_Wq2, L1_gnn_bq2, L1_gnn_Wk2, L1_gnn_bk2, L1_gnn_Wv2, L1_gnn_bv2, L1_gnn_We2, L1_gnn_Ws2, L1_gnn_bs2, L1_gnn_prelu_a), axis=-1)
    return x

_drawn_inputs = setup_inputs


def setup_inputs(seed=0):
    import zlib

    import numpy as np

    out = dict(_drawn_inputs(seed))
    spreads = {'L0_gnn_b1': (0.0, 0.409),
     'L0_gnn_b2': (0.0, 0.1),
     'L1_gnn_bq0': (0.0, 0.8),
     'L1_gnn_bk0': (0.0, 0.8),
     'L1_gnn_bv0': (0.0, 0.472),
     'L1_gnn_bs0': (0.0, 0.1),
     'L1_gnn_bq1': (0.0, 0.8),
     'L1_gnn_bk1': (0.0, 0.8),
     'L1_gnn_bv1': (0.0, 0.326),
     'L1_gnn_bs1': (0.0, 0.1),
     'L1_gnn_bq2': (0.0, 0.8),
     'L1_gnn_bk2': (0.0, 0.8),
     'L1_gnn_bv2': (0.0, 0.1),
     'L1_gnn_bs2': (0.0, 0.1)}
    factors = {}
    for name, (base, spread) in spreads.items():
        noise = np.random.default_rng([zlib.crc32(name.encode()), seed]).standard_normal(out[name].shape)
        drawn = base * np.exp(spread * noise) if base else spread * noise
        out[name] = jnp.asarray(drawn.astype(out[name].dtype))
    for name, factor in factors.items():
        out[name] = (out[name] * factor).astype(out[name].dtype)
    return out
```

```python
import math
from contextlib import ExitStack

import concourse.bass as bass
from concourse import mybir

F32 = mybir.dt.float32
F16 = mybir.dt.float16
I32 = mybir.dt.int32
ALU = mybir.AluOpType
ACT = mybir.ActivationFunctionType
AX = mybir.AxisListType.X

P = 128
D = 64
DE = 32
N_NODES, N_EDGES = 100000, 50000
T = 7
SL = T + 1
EC = 392
CH = EC // T
PAIRS = CH // 2
NN = 2 * EC
NPAD, EPAD = P * NN, P * EC
XW = D + 4
XC = 28
BIG = 1.0e30
EPS = 1e-5
HC = T * D
FS = D * SL
HEADS = (2, 2, 1)
assert EC % (2 * T) == 0 and NPAD > N_NODES and EPAD > N_EDGES and NN % (2 * XC) == 0

REVERSE = (False, True, False, True, False)


W_LOADED = 16 * (3 * 10 + 2 * 3 + 1)


class Order:

    def __init__(self, eng, s):
        self.eng, self.s, self.n = eng, s, 0

    def __call__(self, instruction):
        self.n += 1
        instruction.then_inc(self.s, 1)
        self.eng.wait_ge(self.s, self.n)


def gnn_kernel(nc, x, src, dst, eaT, W1, b1, W2, b2, layers, prelu_a, out):
    with ExitStack() as ctx:
        def sb(name, shape, dt=F32):
            return ctx.enter_context(nc.sbuf_tensor(name, shape, dt))

        def sem(name):
            return ctx.enter_context(nc.semaphore(name))

        def sems(names):
            return {n: sem(n) for n in names.split()}

        def dram(name, shape, dt=F32):
            return nc.dram_tensor(name, shape, dt).ap()

        ext = dram("ext", (NPAD, XW))
        xd_rows = dram("xd_rows", (EPAD, D))
        tab_h1 = dram("tab_h1", (EPAD + P, D))
        tab = [dram(f"tab{k}", (NPAD + EPAD, D)) for k in range(3)]
        agg_blk = dram("agg_blk", (P * CH, FS))
        hd_blk = [dram(f"hd_blk{k}", (P * CH, FS)) for k in range(3)]

        def rows(t, lo=0, n=EPAD):
            return t[lo:lo + n, :].rearrange("(p c) f -> p (c f)", p=P)

        def blocks(t):
            return t.rearrange("(p c) f -> p (c f)", p=P)

        def shared(name, early, late):
            def words(spec):
                return -(-math.prod(spec[1][1:]) * (2 if spec[2:] == (F16,) else 4) // 4)

            whole = sb(name, [P, max(sum(map(words, s)) for s in (early, late))])
            got = {}
            for specs in (early, late):
                at = 0
                for spec in specs:
                    ap = whole[0:spec[1][0], at:at + words(spec)]
                    if spec[2:] == (F16,):
                        ap = ap.bitcast(F16)
                    if len(spec[1]) == 3:
                        ap = ap.rearrange("p (a b) -> p a b", b=spec[1][2])
                    got[spec[0]] = ap
                    at += words(spec)
            return got

        two_of = lambda names, shape: [(f"{n}{b}", shape) for n in names.split() for b in range(2)]
        B = shared("nodes_or_dense", [(f"tn{k}", [P, NN]) for k in range(5)], two_of("x1d t1d t2d od", [P, T, D]))
        B |= shared("ext_or_attention", two_of("extb", [P, XC, XW]),
                    two_of("qs", [P, T, 2 * D]) + [("prod", [P, T, D]), ("cF", [P, FS]), ("hp", [P, FS])])
        B |= shared("aux_or_rows", [("aux", [P, NN, 4])], two_of("hnew", [P, T, D]) + [(f"u{k}", [P, T, D]) for k in (1, 2, 3)])
        B |= shared("onehots_or_sums", [(f"oh{b}_{k}", [P, P + NN], F16) for b in range(2) for k in range(2)],
                    [("m_all", [P, CH + 1, 2 * SL]), ("s_all", [P, CH + 1, 2 * SL])])
        x1d, t1d, t2d, od, extb, qs, hnew = ([B[n + "0"], B[n + "1"]] for n in "x1d t1d t2d od extb qs hnew".split())
        tn = [B[f"tn{k}"] for k in range(5)]
        oh = [[B[f"oh{b}_{k}"] for k in range(2)] for b in range(2)]
        aux, prod, cF, hp, u1, u2, u3, m_all, s_all = (B[n] for n in "aux prod cF hp u1 u2 u3 m_all s_all".split())

        ident = sb("ident", [P, P])
        below = sb("below", [P, P])
        io_lo = sb("io_lo", [P, NN], F16)
        io_hi = sb("io_hi", [P, P], F16)
        io_node = sb("io_node", [P, NN])
        io_part = sb("io_part", [P, 1])
        io_blk = sb("io_blk", [P, CH, SL])
        io_row = [sb(f"io_row{d}", [P, CH, SL]) for d in range(2)]
        ones = sb("ones", [P, NN])
        zero16 = sb("zero16", [P, EC], F16)
        wqs = [sb(f"wqs{k}", [D + 1, 2 * D]) for k in range(3)]
        wkv = [sb(f"wkv{k}", [D + DE + 1, 2 * D]) for k in range(3)]
        wgc = [sb(f"wgc{k}", [D + 1, D]) for k in range(2)]
        relu_b = [sb(f"relu_b{k}", [P, D]) for k in range(2)]
        slope = sb("slope", [P, 3])
        eps_t = sb("eps_t", [P, 1])

        mask8 = [sb(f"mask8_{d}", [P, CH, SL]) for d in range(2)]
        new = [sb(f"new_{d}", [P, EC]) for d in range(2)]
        pen16 = [sb(f"pen16_{d}", [P, CH, 2, SL]) for d in range(2)]
        fmask = [sb(f"fmask_{d}", [P, CH, SL]) for d in range(2)]
        slotm = [sb(f"slotm_{d}", [P, SL]) for d in range(2)]
        cont_all = [sb(f"cont_all_{d}", [P, 1]) for d in range(2)]
        fixed = [sb(f"fixed_{d}", [P, 2]) for d in range(2)]
        inn = [sb(f"inn_{d}", [P, EC]) for d in range(2)]
        fixi = [sb(f"fixi_{d}", [P, 4], I32) for d in range(2)]
        fixo = sb("fixo", [P, 1], I32)
        norm_e = sb("norm_e", [P, EC])
        norm_r = sb("norm_r", [P, EC])
        idx_f = sb("idx_f", [P, 3, EC])

        stage_i = [sb(f"stage_i{k}", [P, EC], I32) for k in range(4)]
        ef = sb("ef", [P, 4, EC])
        gi = [sb(f"gi{k}", [P, EC], I32) for k in range(4)]
        GI = {1: 0, 2: 1, 3: 2, 4: 1}

        qi = sb("qi", [P, EC], I32)
        te = [sb(f"te{k}", [P, EC]) for k in range(3)]
        hl = [[sb(f"hl{k}_{j}", [P, EC]) for j in range(2)] for k in range(2)]
        offs = sb("offs", [P, 2])

        tails = sb("tails", [P, 4, D])
        ft = sb("ft", [D, 4, P])
        fd = sb("fd", [D, 2, P])
        fe = sb("fe", [D, 2, P])
        fr = sb("fr", [D, 3, P + 1])
        fc = sb("fc", [D, 3, P])
        carry = sb("carry", [P, 3, D])
        fb = sb("fb", [P, FS])
        fh = sb("fh", [P, FS])
        fx1 = sb("fx1", [P, FS])
        fxd = sb("fxd", [P, D])
        fbm = sb("fbm", [P, D, SL])
        pre = sb("pre", [P, 4, D])
        fsel = sb("fsel", [P, CH, SL])
        fsc = sb("fsc", [P, 8])
        fm2 = sb("fm2", [P, D])
        fdd = sb("fdd", [P, 2, D])
        fee = sb("fee", [P, 2, D])
        fz = sb("fz", [P, 6, D])
        fT = sb("fT", [D + 1, P])
        frow = sb("frow", [P, D])
        fln = {"xc": sb("lnf_xc", [P, 1, D]), "sq": sb("lnf_sq", [P, 1, D]),
               **{k: sb(f"lnf_{k}", [P, 1]) for k in ("sum", "mean", "ss", "std", "rstd")}}

        gs = [sb(f"gs{b}", [P, T, XW]) for b in range(2)]
        idxb = [sb(f"idxb{b}", [P, T], I32) for b in range(2)]
        oidxb = [sb(f"oidxb{b}", [P, T], I32) for b in range(2)]
        hrow = [sb(f"hrow{b}", [P, T, D]) for b in range(2)]
        hd = [sb(f"hd{b}", [P, FS]) for b in range(2)]
        maskF = [sb(f"maskF{b}", [P, FS]) for b in range(2)]
        msgF = sb("msgF", [P, FS])
        aggF = [sb(f"aggF{b}", [P, FS]) for b in range(2)]
        hdT = sb("hdT", [D + 1, T * P])
        kvin = [sb(f"kvin{b}", [D + DE + 1, T * P]) for b in range(2)]
        alpha8 = sb("alpha8", [P, 2 * SL])
        d8 = sb("d8", [P, 2, 2 * SL])
        e8 = sb("e8", [P, 2, 2 * SL])
        r8 = sb("r8", [P, 2 * SL])
        x1b = [sb(f"x1b{b}", [P, FS]) for b in range(2)]
        xin = [sb(f"xin{b}", [P, T, D]) for b in range(2)]
        nT = sb("nT", [D + 1, T * P])
        neg = sb("neg", [P, T, D])
        yd = sb("yd", [P, T, D])
        mask8f = [m[:, :, :].rearrange("p c s -> p (c s)") for m in mask8]

        def ln_buffers(name):
            return {"xc": sb(name + "_xc", [P, T, D]), "sq": sb(name + "_sq", [P, T, D]),
                    **{k: sb(f"{name}_{k}", [P, T]) for k in ("sum", "mean", "ss", "std", "rstd")}}

        def ln_sems(name):
            return sems(" ".join(f"{name}_{k}" for k in "sum mean centred squared spread std rstd out".split()))

        lnb = {k: ln_buffers(k) for k in ("lnd", "lne")}
        LS = {k: ln_sems(k) for k in ("LD", "LE", "LF")}

        ps = [ctx.enter_context(nc.psum_tensor(f"ps{k}", [P, 1024], F32)) for k in range(4)]
        psA, psB, psC, psD = ps

        S = sems("waits_passed idx_copied oidx_copied w_loaded edges_loaded pool_consts onehots_ready onehots_used counts_done norm_done "
                 "totals_ready offset_done aux_done sqrt_in deg_tail degT deg_carry deg_back inn_in inn_std "
                 "idx_made idx_stored consts_stored relu_made "
                 "ext_aux gc_extract gc_idx gc_maskF gc_msg gc_carry gc_agg gc_z gc_zT gc_zTc gc_mm gc_relu gc_y "
                 "d_y d_tr d_trc d_mm d_neg d_pre d_res "
                 "t_maskF t_hp t_hpc t_hd t_trh t_hdT t_trg t_gT t_q t_kv t_qs t_prod t_alpha t_acar t_m t_d0 t_d t_e "
                 "t_scar t_s t_r0 t_r t_av t_avc t_agg t_u1 t_u2 t_u3 t_hn t_cF t_y "
                 "fx_tail fx_tailT fx_d fx_e fx_carry fx_back fx_z fx_zT fx_zTc fx_mm fx_relu fx_row fx_hT fx_hTr fx_ho "
                 "fx_gather fx_scatter round_open rounds_dve "
                 "dve_order pe_order act_order pool_order")
        ld = {k: [sem(f"{k}{b}") for b in range(2)] for k in
              "ld_h ld_ea ld_x1 ld_xd ld_dx ld_xin gat scat st_xd st_agg st_hn st_hd st_ext st_d".split()}

        def settle(eng):
            if eng.engine in (mybir.EngineType.SP, mybir.EngineType.Pool, mybir.EngineType.PE):
                eng.sem_inc(S["waits_passed"], 1)

        def need(eng, s, v):
            if isinstance(v, int) and v <= 0:
                return
            eng.wait_ge(s, v)
            if not isinstance(v, int):
                settle(eng)

        def pairs(eng, n, body):
            body(0)
            with eng.Fori(1, n - 1) as i:
                body(i)
            body(n - 1)

        def fj(t):
            return t[:, :].rearrange("p (f s) -> p s f", s=SL)[:, 1:SL, :]

        def slot(t, s):
            return t[:, :].rearrange("p (f s) -> p f s", s=SL)[:, :, s]

        def bc(ap, n):
            return ap.unsqueeze(2).broadcast_to([ap.shape[0], ap.shape[1], n])

        def mem(ap, rev):
            return ap[:, ::-1] if rev else ap

        def col0(c, rev):
            return (EC - T) - c * T if rev else c * T

        block = ctx.enter_context(nc.Block())
        LB = 16 * PAIRS

        @block.sync
        def _(sp):
            e2 = dst[1:1 + EPAD].rearrange("(p c) -> p c", p=P)
            sp.dma_start(stage_i[0][:, :], src.rearrange("(p c) -> p c", p=P)).then_inc(S["edges_loaded"], 16)
            sp.dma_start(stage_i[1][:, :], e2).then_inc(S["edges_loaded"], 16)
            sp.dma_start(stage_i[2][:, :], dst[0:EPAD].rearrange("(p c) -> p c", p=P)).then_inc(S["edges_loaded"], 16)
            sp.dma_start(stage_i[3][:, :], dst[2:2 + EPAD].rearrange("(p c) -> p c", p=P)).then_inc(S["edges_loaded"], 16)
            for k, (Wq, bq, Wk, bk, Wv, bv, We, Ws, bs) in enumerate(layers):
                for t, r0, c0, w in ((wqs[k], 0, 0, Wq), (wqs[k], 0, D, Ws), (wkv[k], 0, 0, Wk), (wkv[k], 0, D, Wv),
                                     (wkv[k], D, 0, We), (wkv[k], D, D, We)):
                    sp.dma_start(t[r0:r0 + w.shape[0], c0:c0 + D], w).then_inc(S["w_loaded"], 16)
                for t, r0, c0, w in ((wqs[k], D, 0, bq), (wqs[k], D, D, bs), (wkv[k], D + DE, 0, bk), (wkv[k], D + DE, D, bv)):
                    sp.dma_start(t[r0:r0 + 1, c0:c0 + D], w.unsqueeze(0)).then_inc(S["w_loaded"], 16)
            for k, (w, bb) in enumerate(((W1, b1), (W2, b2))):
                sp.dma_start(wgc[k][0:D, :], w).then_inc(S["w_loaded"], 16)
                sp.dma_start(wgc[k][D:D + 1, :], bb.unsqueeze(0)).then_inc(S["w_loaded"], 16)
                sp.dma_start(relu_b[k][:, :], bb.unsqueeze(0).broadcast_to([P, D])).then_inc(S["w_loaded"], 16)
            sp.dma_start(slope[:, 0:1], prelu_a.unsqueeze(0).broadcast_to([P, 1])).then_inc(S["w_loaded"], 16)

            def xd_body(i):
                for b in range(2):
                    c = 2 * i + b
                    need(sp, ld["gat"][b], 16 * T * (i + 1))
                    sp.dma_start(rows(xd_rows)[:, bass.ds(c * HC, HC)], x1b[b][:, 0:HC]).then_inc(ld["st_xd"][b], 16)

            pairs(sp, PAIRS, xd_body)

            def ext_store(eng, c, er):
                b = c % 2
                eng.wait_ge(S["ext_aux"], c + 1)
                eng.wait_ge(ld["ld_dx"][b], 16 * (c // 2 + 1))
                eng.dma_start(er[:, c * XC * XW:(c + 1) * XC * XW], extb[b][:, :, :].rearrange("p c f -> p (c f)")
                              ).then_inc(ld["st_ext"][b], 16)

            xr, er = rows(x, 0, NPAD), ext.rearrange("(p c) f -> p (c f)", p=P)
            for c in range(NN // XC):
                b = c % 2
                need(sp, ld["st_ext"][b], 16 * (c // 2))
                sp.dma_start(extb[b][:, :, 0:D], xr[:, c * XC * D:(c + 1) * XC * D].rearrange("p (c f) -> p c f", f=D)
                             ).then_inc(ld["ld_dx"][b], 16)
                if c >= 1:
                    ext_store(sp, c - 1, er)
            ext_store(sp, NN // XC - 1, er)
            sp.wait_ge(S["relu_made"], 1)
            sp.dma_start(tab_h1[EPAD:EPAD + P, :], relu_b[0][:, :]).then_inc(S["consts_stored"], 16)
            for b in range(2):
                sp.wait_ge(ld["st_ext"][b], 16 * (NN // XC // 2))
            sp.wait_ge(S["consts_stored"], 16)
            for b in range(2):
                sp.wait_ge(ld["st_xd"][b], LB)

            def gc_loads(r, i, b):
                c = 2 * i + b
                need(sp, S["d_y"], r * CH + c - 1)
                sp.dma_start(xin[b][:, :, :].rearrange("p t f -> p (t f)"),
                             xr[:, bass.ds((r * CH + c) * HC, HC)]).then_inc(ld["ld_xin"][b], 16)
                if r == 1:
                    need(sp, S["gc_y"], c - 1)
                    sp.dma_start(hrow[b][:, :, :].rearrange("p t f -> p (t f)"),
                                 rows(xd_rows)[:, bass.ds(col0(c, True) * D, HC)]).then_inc(ld["ld_xd"][b], 16)

            def gc_stores(r, i, b):
                c = 2 * i + b
                n = r * CH + c + 1
                need(sp, S["gc_agg"], n)
                sp.dma_start(blocks(agg_blk)[:, bass.ds(c * FS, FS)], aggF[b][:, :]).then_inc(ld["st_agg"][b], 16)
                flat = lambda t: t[:, :, :].rearrange("p t f -> p (t f)")
                if r == 0:
                    need(sp, S["gc_relu"], n)
                    sp.dma_start(rows(tab_h1)[:, bass.ds(c * HC, HC)], flat(hnew[b])).then_inc(ld["st_hn"][b], 16)
                else:
                    need(sp, LS["LE"]["LE_out"], c + 1)
                    sp.dma_start(rows(tab[0], NPAD)[:, bass.ds(col0(c, True) * D, HC)], flat(hnew[b])
                                 ).then_inc(ld["st_hn"][b], 16)
                dcols = bass.ds((r * CH + c) * HC, HC)
                need(sp, LS["LD"]["LD_out"], 2 * n - 1)
                sp.dma_start(rows(tab[0], 0, NPAD)[:, dcols], flat(x1d[b])).then_inc(ld["st_d"][b], 16)
                need(sp, S["d_pre"], 2 * n - 1)
                sp.dma_start(rows(tab[1], 0, NPAD)[:, dcols], flat(t1d[b])).then_inc(ld["st_d"][b], 16)
                need(sp, S["d_pre"], 2 * n)
                sp.dma_start(rows(tab[2], 0, NPAD)[:, dcols], flat(t2d[b])).then_inc(ld["st_d"][b], 16)
                need(sp, LS["LD"]["LD_out"], 2 * n)
                sp.dma_start(rows(out, 0, NPAD)[:, dcols], flat(od[b])).then_inc(ld["st_d"][b], 16)

            def opened(r):
                sp.wait_ge(S["fx_scatter"], 16 * r)
                for b in range(2):
                    sp.wait_ge(ld["st_hn"][b], LB * r)

            for r in range(2):
                if r:
                    opened(r)
                for b in range(2):
                    gc_loads(r, 0, b)

                def gc_body(i):
                    for b in range(2):
                        if not (isinstance(i, int) and i == PAIRS - 1):
                            gc_loads(r, i + 1, b)
                        gc_stores(r, i, b)

                pairs(sp, PAIRS, gc_body)

            def t_loads(l, i, b):
                c = 2 * i + b
                g = l * CH + c
                rev = REVERSE[2 + l]
                need(sp, S["t_hp"], g - 1)
                sp.dma_start(hrow[b][:, :, :].rearrange("p t f -> p (t f)"),
                             rows(tab[l], NPAD)[:, bass.ds(col0(c, rev) * D, HC)]).then_inc(ld["ld_h"][b], 16)
                need(sp, S["t_kv"], g - 1)
                sp.dma_start(kvin[b][D:D + DE, :], eaT[:, bass.ds(col0(c, rev) * P, T * P)]).then_inc(ld["ld_ea"][b], 16)
                if l == 2:
                    need(sp, S["t_y"], c - 1)
                    sp.dma_start(x1b[b][:, :], blocks(hd_blk[0])[:, bass.ds(c * FS, FS)]).then_inc(ld["ld_x1"][b], 16)

            def t_stores(l, i, b):
                c = 2 * i + b
                n = l * CH + c + 1
                rev = REVERSE[2 + l]
                need(sp, S["t_hd"], n)
                sp.dma_start(blocks(hd_blk[l])[:, bass.ds(c * FS, FS)], hd[b][:, :]).then_inc(ld["st_hd"][b], 16)
                need(sp, S["t_agg"], n)
                sp.dma_start(blocks(agg_blk)[:, bass.ds(c * FS, FS)], aggF[b][:, :]).then_inc(ld["st_agg"][b], 16)
                if l < 2:
                    need(sp, S["t_hn"], n)
                    sp.dma_start(rows(tab[l + 1], NPAD)[:, bass.ds(col0(c, rev) * D, HC)],
                                 hnew[b][:, :, :].rearrange("p t f -> p (t f)")).then_inc(ld["st_hn"][b], 16)

            for l in range(3):
                opened(2 + l)
                for b in range(2):
                    t_loads(l, 0, b)

                def t_body(i):
                    for b in range(2):
                        if not (isinstance(i, int) and i == PAIRS - 1):
                            t_loads(l, i + 1, b)
                        t_stores(l, i, b)

                pairs(sp, PAIRS, t_body)
            for b in range(2):
                sp.wait_ge(ld["st_hd"][b], 3 * LB)
                sp.wait_ge(ld["st_agg"][b], 5 * LB)
                sp.wait_ge(ld["st_hn"][b], 4 * LB)
                sp.wait_ge(ld["st_d"][b], 4 * 2 * LB)
                sp.wait_ge(ld["scat"][b], T * LB)
            sp.wait_ge(S["fx_scatter"], 16 * 5)

        @block.gpsimd
        def _(pool):
            order = Order(pool, S["pool_order"])
            order(pool.memset(ident[:, :], 0.0))
            order(pool.affine_select(out=ident[:, :], in_=ident[:, :], compare_op=ALU.not_equal, fill=1.0, base=0,
                                     pattern=[[-1, P]], channel_multiplier=1))
            order(pool.memset(below[:, :], 1.0))
            order(pool.affine_select(out=below[:, :], in_=below[:, :], compare_op=ALU.is_ge, fill=0.0, base=-1,
                                     pattern=[[1, P]], channel_multiplier=-1))
            loose = dict(allow_small_or_imprecise_dtypes=True)
            order(pool.iota(io_lo[:, :], [[1, NN]], base=0, channel_multiplier=0, **loose))
            order(pool.iota(io_hi[:, :], [[1, P]], base=0, channel_multiplier=0, **loose))
            order(pool.iota(io_node[:, :], [[1, NN]], base=0, channel_multiplier=NN, **loose))
            order(pool.iota(io_part[:, :], [[1, 1]], base=0, channel_multiplier=1, **loose))
            order(pool.iota(io_blk[:, :, :], [[1, CH], [0, SL]], base=0, channel_multiplier=CH, **loose))
            order(pool.iota(io_row[0][:, :, :], [[T, CH], [1, SL]], base=-1, channel_multiplier=EC, **loose))
            order(pool.iota(io_row[1][:, :, :], [[-T, CH], [-1, SL]], base=EC, channel_multiplier=EC, **loose))
            for t in (hdT, nT, fT):
                order(pool.memset(t[D:D + 1, :], 1.0))
            for b in range(2):
                order(pool.memset(kvin[b][D + DE:D + DE + 1, :], 1.0))
            pool.memset(eps_t[:, :], EPS).then_inc(S["pool_consts"], 1)

            def copy_idx(phase, c, b, idx, before):
                need(pool, ld["gat"][b], before)
                pool.tensor_copy(idxb[b][:, :], idx[:, bass.ds(c * T, T)]).then_inc(S["idx_copied"], 1)

            def gathers(phase, i, b, idx, table, bound, to, width):
                c = 2 * i + b
                base = phase * T * LB
                need(pool, S["idx_copied"], phase * CH + c + 1)
                for t in range(T):
                    if t == T - 1 and not (isinstance(i, int) and i == PAIRS - 1 and b == 1):
                        copy_idx(phase, c + 1, 1 - b, idx, base + 16 * T * (i + b))
                    pool.indirect_dma_start(out=to(b, t)[:, 0:width], out_offset=None, in_=table,
                                            in_offset=bass.IndirectOffsetOnAxis(ap=idxb[b][:, t:t + 1], axis=0),
                                            bounds_check=bound, oob_is_err=False).then_inc(ld["gat"][b], 16)

            def opened(r):
                for b in range(2):
                    need(pool, ld["st_hn"][b], LB * min(r, 4))
                need(pool, S["fx_scatter"], 16 * r)

            def fix_gather(r, table, bound, col, to):
                pool.indirect_dma_start(out=to, out_offset=None, in_=table,
                                        in_offset=bass.IndirectOffsetOnAxis(ap=fixi[REVERSE[r]][:, col:col + 1], axis=0),
                                        bounds_check=bound, oob_is_err=False).then_inc(S["fx_gather"], 16)

            def fix(r):
                for b in range(2):
                    pool.wait_ge(ld["st_agg"][b], LB * (r + 1))
                fix_gather(r, agg_blk, P * CH - 1, 0, fb[:, :])
                if r == 1:
                    fix_gather(r, xd_rows, EPAD - 1, 1, fxd[:, :])
                if r >= 2:
                    for b in range(2):
                        pool.wait_ge(ld["st_hd"][b], LB * (r - 1))
                    fix_gather(r, hd_blk[r - 2], P * CH - 1, 0, fh[:, :])
                if r == 4:
                    fix_gather(r, hd_blk[0], P * CH - 1, 0, fx1[:, :])
                for b in range(2):
                    pool.wait_ge(ld["st_hn"][b], LB * min(r + 1, 4))
                    need(pool, ld["scat"][b], T * LB if r == 4 else 0)
                pool.wait_ge(S["fx_row"], r + 1)
                if r == 0:
                    to, bound, at = tab_h1, EPAD + P - 1, fixi[0][:, 2:3]
                elif r < 4:
                    to, bound, at = tab[r - 1], NPAD + EPAD - 1, fixi[REVERSE[r]][:, 3:4]
                else:
                    to, bound, at = out, NPAD - 1, fixo[:, 0:1]
                pool.indirect_dma_start(out=to, out_offset=bass.IndirectOffsetOnAxis(ap=at, axis=0), in_=frow[:, :],
                                        in_offset=None, bounds_check=bound, oob_is_err=False
                                        ).then_inc(S["fx_scatter"], 16)

            pool.wait_ge(S["edges_loaded"], 64)
            copy_idx(0, 0, 0, stage_i[1], 0)

            def xd_body(i):
                for b in range(2):
                    need(pool, ld["st_xd"][b], 16 * i)
                    gathers(0, i, b, stage_i[1], x, NPAD - 1, lambda b, t: x1b[b][:, t * D:(t + 1) * D], D)

            pairs(pool, PAIRS, xd_body)

            for b in range(2):
                pool.wait_ge(ld["st_ext"][b], 16 * (NN // XC // 2))
            pool.wait_ge(S["consts_stored"], 16)
            for r in range(2):
                opened(r)
                if r:
                    pool.wait_ge(S["idx_made"], 1)
                idx = stage_i[0] if r == 0 else gi[GI[r]]
                table, bound, width = (ext, NPAD - 1, XW) if r == 0 else (tab_h1, EPAD + P - 1, D)
                copy_idx(1 + r, 0, 0, idx, (1 + r) * T * LB)

                def gc_body(i):
                    for b in range(2):
                        need(pool, S["gc_msg"], r * CH + 2 * i + b - 1)
                        gathers(1 + r, i, b, idx, table, bound, lambda b, t: gs[b][:, t, :], width)

                pairs(pool, PAIRS, gc_body)
                fix(r)

            for b in range(2):
                pool.wait_ge(ld["st_d"][b], 4 * 2 * LB)
            for l in range(3):
                r = 2 + l
                opened(r)
                idx = gi[GI[r]]
                copy_idx(1 + r, 0, 0, idx, (1 + r) * T * LB)

                def scatters(i, b):
                    c = 2 * i + b
                    need(pool, S["oidx_copied"], c + 1)
                    need(pool, LS["LE"]["LE_out"], CH + c + 1)
                    for t in range(T):
                        pool.indirect_dma_start(out=out, out_offset=bass.IndirectOffsetOnAxis(ap=oidxb[b][:, t:t + 1], axis=0),
                                                in_=hnew[b][:, t, :], in_offset=None, bounds_check=NPAD - 1,
                                                oob_is_err=False).then_inc(ld["scat"][b], 16)

                def copy_oidx(i, b):
                    need(pool, ld["scat"][b], 16 * T * i)
                    pool.tensor_copy(oidxb[b][:, :], gi[3][:, bass.ds((2 * i + b) * T, T)]).then_inc(S["oidx_copied"], 1)

                def t_body(i):
                    for b in range(2):
                        first = isinstance(i, int) and i == 0 and b == 0
                        if l == 2 and not first:
                            copy_oidx(i - 1 + b, 1 - b)
                        need(pool, S["t_trg"], l * CH + 2 * i + b - 1)
                        gathers(1 + r, i, b, idx, tab[l], NPAD + EPAD - 1, lambda b, t: gs[b][:, t, :], D)
                        if l == 2 and not first:
                            scatters(i - 1 + b, 1 - b)

                pairs(pool, PAIRS, t_body)
                if l == 2:
                    copy_oidx(PAIRS - 1, 1)
                    scatters(PAIRS - 1, 1)
                fix(r)
            pool.wait_ge(S["fx_scatter"], 16 * 5)

        @block.tensor
        def _(pe):
            def onehot_products(k, b, lhs, rhs, start, stop):
                for h in range(2):
                    m = pe.matmul(ps[k][:, h * 512:h * 512 + EC], lhs, rhs(h), start=start, stop=stop,
                                  skip_group_check=True)
                return m

            pe.wait_ge(S["onehots_ready"], 1)
            for k in range(2):
                onehot_products(k, 0, zero16[:, 0:P], lambda h: zero16[:, :], True, False)

            def count(i):
                for b in range(2):
                    pe.wait_ge(S["onehots_ready"], 2 + 2 * i + b)
                    for k in range(2):
                        m = onehot_products(k, b, oh[b][k][:, 0:P],
                                            lambda h, k=k, b=b: oh[b][k][:, P + h * EC:P + (h + 1) * EC], False, False)
                    m.then_inc(S["onehots_used"], 1)

            pairs(pe, EC // 2, count)
            for k in range(2):
                m = onehot_products(k, 0, zero16[:, 0:P], lambda h: zero16[:, :], False, True)
            m.then_inc(S["counts_done"], 1)
            pe.wait_ge(S["totals_ready"], 1)
            pe.matmul(psC[:, 0:1], below[:, :], offs[:, 0:1], start=True, stop=True).then_inc(S["offset_done"], 1)

            def turn(n, src3, count, dst, rows_, done):
                for k in range(count):
                    t = pe.transpose(dst[0:src3(k).shape[1], k * rows_:(k + 1) * rows_], src3(k), ident[0:rows_, 0:rows_])
                t.then_inc(done, 1)

            for d in range(2):
                pe.wait_ge(S["deg_tail"], d + 1)
                turn(d, lambda k: tails[:, 3 * k, :], 2, psC, P, S["degT"])
                pe.wait_ge(S["deg_carry"], d + 1)
                pe.transpose(psC[:, 0:D], fc[:, 0, :], ident[0:D, 0:D]).then_inc(S["deg_back"], 1)

            pe.wait_ge(S["w_loaded"], W_LOADED)

            def fix(r):
                t_round = r >= 2
                n = r + 1
                ks = range(4) if t_round else (0, 3)
                pe.wait_ge(S["fx_tail"], n)
                for k in ks:
                    t = pe.transpose(psA[0:D, k * P:(k + 1) * P], tails[:, k, :], ident[:, :])
                t.then_inc(S["fx_tailT"], 1)
                pe.wait_ge(S["fx_carry"], n)
                for k in range(3 if t_round else 1):
                    t = pe.transpose(psA[:, k * D:(k + 1) * D], fc[:, k, :], ident[0:D, 0:D])
                t.then_inc(S["fx_back"], 1)
                pe.wait_ge(S["fx_z"], n)
                pe.transpose(psB[0:D, 0:P], fz[:, 0, :], ident[:, :]).then_inc(S["fx_zT"], 1)
                pe.wait_ge(S["fx_zTc"], n)
                w = wqs[r - 2] if t_round else wgc[r]
                pe.matmul(psC[:, 0:w.shape[1]], fT[:, :], w[:, :], start=True, stop=True).then_inc(S["fx_mm"], 1)
                if 1 <= r <= 3:
                    pe.wait_ge(S["fx_hT"], r)
                    for k in range(2):
                        t = pe.transpose(psA[0:D, k * P:(k + 1) * P], tails[:, k, :], ident[:, :])
                    t.then_inc(S["fx_hTr"], 1)
                    pe.wait_ge(S["fx_ho"], r)
                    pe.transpose(psB[:, 0:D], fc[:, 0, :], ident[0:D, 0:D]).then_inc(S["fx_hTr"], 1)

            def transposes(to, tile, done):
                settle(pe)
                for t in range(T):
                    m = pe.transpose(to[0:D, t * P:(t + 1) * P], tile(t), ident[:, :])
                m.then_inc(done, 1)

            def products(to, width, lhs, w, done):
                for t in range(T):
                    m = pe.matmul(to[:, t * width:(t + 1) * width], lhs(t), w, start=True, stop=True)
                m.then_inc(done, 1)

            nTt = lambda t: nT[:, t * P:(t + 1) * P]

            def gc_step(r, i, b):
                n = r * CH + 2 * i + b + 1
                pe.wait_ge(S["gc_z"], n)
                transposes(psA, lambda t: u1[:, t, :], S["gc_zT"])
                pe.wait_ge(S["gc_zTc"], n)
                if r:
                    need(pe, S["gc_relu"], n - 1)
                products(psC, D, lambda t: hdT[:, t * P:(t + 1) * P], wgc[r][:, :], S["gc_mm"])
                for k, (src_t, s, m) in enumerate(((x1d, LS["LD"]["LD_out"], 2 * n - 1), (t1d, S["d_pre"], 2 * n - 1),
                                                   (t2d, S["d_pre"], 2 * n))):
                    pe.wait_ge(s, m)
                    transposes(psB, lambda t: src_t[b][:, t, :], S["d_tr"])
                    pe.wait_ge(S["d_trc"], 3 * (n - 1) + k + 1)
                    if k == 0:
                        need(pe, S["d_res"], n - 1)
                    products(psD, D, nTt, wqs[k][:, D:2 * D], S["d_mm"])

            for r in range(2):
                def gc_body(i):
                    for b in range(2):
                        gc_step(r, i, b)

                pairs(pe, PAIRS, gc_body)
                fix(r)

            for l in range(3):
                def t_body(i):
                    for b in range(2):
                        c = 2 * i + b
                        n = l * CH + c + 1
                        pe.wait_ge(S["t_hd"], n)
                        hv = hd[b][:, :].rearrange("p (f s) -> p s f", s=SL)
                        transposes(psB, lambda t: hv[:, t + 1, :], S["t_trh"])
                        pe.wait_ge(ld["gat"][b], (3 + l) * T * LB + 16 * T * (i + 1))
                        need(pe, S["t_gT"], n - 1)
                        transposes(psA, lambda t: gs[b][:, t, 0:D], S["t_trg"])
                        pe.wait_ge(S["t_hdT"], n)
                        need(pe, S["t_qs"], n - 1)
                        products(psD, 2 * D, lambda t: hdT[:, t * P:(t + 1) * P], wqs[l][:, :], S["t_q"])
                        pe.wait_ge(S["t_gT"], n)
                        pe.wait_ge(ld["ld_ea"][b], l * LB + 16 * (i + 1))
                        need(pe, S["t_av"], n - 1)
                        at = (lambda t: T - 1 - t) if REVERSE[2 + l] else (lambda t: t)
                        products(psC, 2 * D, lambda t: kvin[b][:, at(t) * P:(at(t) + 1) * P], wkv[l][:, :], S["t_kv"])

                pairs(pe, PAIRS, t_body)
                fix(2 + l)

        @block.scalar
        def _(act):
            def ln_square(L, n, w, B):
                act.wait_ge(L[B + "_centred"], n)
                act.activation(w["sq"][:, :, :], w["xc"][:, :, :], ACT.Square).then_inc(L[B + "_squared"], 1)

            def ln_std(L, n, w, B):
                act.wait_ge(L[B + "_spread"], n)
                act.activation(w["std"][:, :], w["ss"][:, :], ACT.Sqrt, scale=1.0 / D, bias=eps_t[:, 0:1]
                               ).then_inc(L[B + "_std"], 1)

            act.wait_ge(S["sqrt_in"], 1)
            act.activation(tn[0][:, :], tn[0][:, :], ACT.Sqrt).then_inc(S["norm_done"], 1)
            for d in range(2):
                act.wait_ge(S["inn_in"], d + 1)
                act.activation(te[1][:, :], te[0][:, :], ACT.Sqrt).then_inc(S["inn_std"], 1)

            def fill_mask(c, b, d, done):
                act.copy(maskF[b][:, :].rearrange("p (f s) -> p f s", s=SL),
                         mask8f[d][:, bass.ds(c * SL, SL)].unsqueeze(1).broadcast_to([P, D, SL])).then_inc(done, 1)

            def fix(r):
                t_round = r >= 2
                n = r + 1
                if t_round:
                    act.wait_ge(S["fx_d"], 2 * (r - 1) - 1)
                    act.activation(fe[:, :, :], fd[:, :, :], ACT.Exp).then_inc(S["fx_e"], 1)
                    act.wait_ge(S["fx_d"], 2 * (r - 1))
                    act.activation(fee[:, :, :], fdd[:, :, :], ACT.Exp).then_inc(S["fx_e"], 1)
                act.wait_ge(S["fx_zT"], n)
                act.copy(fT[0:D, :], psB[0:D, 0:P]).then_inc(S["fx_zTc"], 1)
                if not t_round:
                    act.wait_ge(S["fx_mm"], n)
                    act.activation(fz[:, 1, :], psC[:, 0:D], ACT.Relu).then_inc(S["fx_relu"], 1)
                if r in (1, 4):
                    k = 1 if r == 1 else 2
                    ln_square(LS["LF"], k, fln, "LF")
                    ln_std(LS["LF"], k, fln, "LF")

            def gc_step(r, i, b):
                c = 2 * i + b
                n = r * CH + c + 1
                L = LS["LD"]
                need(act, S["gc_agg"], n - 2)
                fill_mask(c, b, int(REVERSE[r]), S["gc_maskF"])
                ln_square(L, 2 * n - 1, lnb["lnd"], "LD")
                ln_std(L, 2 * n - 1, lnb["lnd"], "LD")
                act.wait_ge(S["gc_zT"], n)
                act.copy(hdT[0:D, :], psA[0:D, 0:T * P]).then_inc(S["gc_zTc"], 1)
                act.wait_ge(S["gc_mm"], n)
                ps3 = psC[:, 0:HC].rearrange("p (t f) -> p t f", f=D)
                if r == 0:
                    need(act, ld["st_hn"][b], 16 * i)
                    act.activation(hnew[b][:, :, :], ps3, ACT.Relu).then_inc(S["gc_relu"], 1)
                else:
                    need(act, S["gc_y"], c)
                    act.activation(u2[:, :, :], ps3, ACT.Relu).then_inc(S["gc_relu"], 1)
                for k in range(3):
                    act.wait_ge(S["d_tr"], 3 * (n - 1) + k + 1)
                    act.copy(nT[0:D, :], psB[0:D, 0:T * P]).then_inc(S["d_trc"], 1)
                    if k == 2:
                        break
                    act.wait_ge(S["d_mm"], 3 * (n - 1) + k + 1)
                    act.activation(neg[:, :, :], psD[:, 0:HC].rearrange("p (t f) -> p t f", f=D), ACT.Relu,
                                   scale=-1.0).then_inc(S["d_neg"], 1)
                    if r == 1:
                        (ln_square, ln_std)[k](LS["LE"], c + 1, lnb["lne"], "LE")
                ln_square(L, 2 * n, lnb["lnd"], "LD")
                ln_std(L, 2 * n, lnb["lnd"], "LD")

            for r in range(2):
                def gc_body(i):
                    for b in range(2):
                        gc_step(r, i, b)

                pairs(act, PAIRS, gc_body)
                fix(r)

            def t_mask(l, c, b, n):
                need(act, S["t_hd"], n - 2)
                fill_mask(c, b, int(REVERSE[2 + l]), S["t_maskF"])

            def t_hdT(n, b):
                act.wait_ge(S["t_trh"], n)
                need(act, S["t_q"], n - 1)
                act.copy(hdT[0:D, :], psB[0:D, 0:T * P]).then_inc(S["t_hdT"], 1)

            def t_inputs(l, n, b):
                act.wait_ge(S["t_trg"], n)
                need(act, S["t_kv"], n - 2)
                tiles = lambda ap: ap.rearrange("p (t e) -> p t e", t=T)
                act.copy(mem(tiles(kvin[b][0:D, :]), REVERSE[2 + l]), tiles(psA[0:D, 0:T * P])).then_inc(S["t_gT"], 1)
                act.wait_ge(S["t_q"], n)
                need(act, S["t_u2"], n - 2)
                act.copy(qs[b][:, :, :].rearrange("p t f -> p (t f)"), psD[:, 0:T * 2 * D]).then_inc(S["t_qs"], 1)

            for l in range(3):
                H = HEADS[l]
                t_mask(l, 0, 0, l * CH + 1)
                t_mask(l, 1, 1, l * CH + 2)
                t_hdT(l * CH + 1, 0)
                t_inputs(l, l * CH + 1, 0)

                def t_body(i):
                    for b in range(2):
                        c = 2 * i + b
                        n = l * CH + c + 1
                        last = isinstance(i, int) and i == PAIRS - 1
                        act.wait_ge(S["t_d"], n)
                        act.activation(e8[:, :, 0:H * SL], d8[:, :, 0:H * SL], ACT.Exp).then_inc(S["t_e"], 1)
                        need(act, S["t_agg"], n - 1)
                        act.wait_ge(S["t_e"], n)
                        act.copy(cF[:, :].rearrange("p (h c s) -> p h c s", h=H, s=SL),
                                 e8[:, 0, 0:H * SL].rearrange("p (h s) -> p h s", h=H).unsqueeze(2)
                                 .broadcast_to([P, H, D // H, SL])).then_inc(S["t_cF"], 1)
                        if not (last and b == 1):
                            t_hdT(n + 1, 1 - b)
                            t_inputs(l, n + 1, 1 - b)
                        if not last:
                            t_mask(l, c + 2, b, n + 2)
                        if l == 2:
                            ln_square(LS["LE"], CH + c + 1, lnb["lne"], "LE")
                            ln_std(LS["LE"], CH + c + 1, lnb["lne"], "LE")

                pairs(act, PAIRS, t_body)
                fix(2 + l)

        @block.vector
        def _(v):
            order = Order(v, S["dve_order"])

            def ln_centre(L, n, w, B, y, F=None):
                v.tensor_reduce(w["sum"][:, :], y, AX, ALU.add).then_inc(L[B + "_sum"], 1)
                v.wait_ge(L[B + "_sum"], n)
                v.tensor_scalar(w["mean"][:, :], w["sum"][:, :], 1.0 / D, None, ALU.mult).then_inc(L[B + "_mean"], 1)
                v.wait_ge(L[B + "_mean"], n)
                v.tensor_tensor(w["xc"][:, :, :], y, bc(w["mean"][:, :], D), ALU.subtract).then_inc(L[B + "_centred"], 1)

            def ln_spread(L, n, w, B):
                v.wait_ge(L[B + "_squared"], n)
                v.tensor_reduce(w["ss"][:, :], w["sq"][:, :, :], AX, ALU.add).then_inc(L[B + "_spread"], 1)

            def ln_scale(L, n, w, B, to):
                v.wait_ge(L[B + "_std"], n)
                v.reciprocal(w["rstd"][:, :], w["std"][:, :]).then_inc(L[B + "_rstd"], 1)
                v.wait_ge(L[B + "_rstd"], n)
                v.tensor_tensor(to, w["xc"][:, :, :], bc(w["rstd"][:, :], D), ALU.mult).then_inc(L[B + "_out"], 1)

            v.wait_ge(S["edges_loaded"], 64)
            v.wait_ge(S["pool_consts"], 1)
            for k in range(4):
                order(v.tensor_copy(ef[:, k, :], stage_i[k][:, :]))
            for k in range(2):
                hi, lo = hl[k][0][:, :], hl[k][1][:, :]
                e, q, t = ef[:, k, :], te[0][:, :], te[1][:, :]
                order(v.tensor_scalar(q, e, 1.0 / NN, None, ALU.mult))
                order(v.tensor_copy(qi[:, :], q))
                order(v.tensor_copy(hi, qi[:, :]))
                order(v.scalar_tensor_tensor(out=lo, in0=hi, scalar=-float(NN), in1=e, op0=ALU.mult, op1=ALU.add))
                for op, sign in ((ALU.is_lt, 1.0), (ALU.is_ge, -1.0)):
                    order(v.tensor_scalar(t, lo, 0.0 if sign > 0 else float(NN), None, op))
                    order(v.scalar_tensor_tensor(out=hi, in0=t, scalar=-sign, in1=hi, op0=ALU.mult, op1=ALU.add))
                    order(v.scalar_tensor_tensor(out=lo, in0=t, scalar=sign * NN, in1=lo, op0=ALU.mult, op1=ALU.add))
            v.memset(zero16[:, :], 0.0).then_inc(S["onehots_ready"], 1)

            def onehots(i):
                for b in range(2):
                    j = 2 * i + b
                    need(v, S["onehots_used"], j - 1)
                    for k in range(2):
                        v.tensor_scalar(oh[b][k][:, P:P + NN], io_lo[:, :], hl[k][1][:, bass.ds(j, 1)], None, ALU.is_equal)
                        m = v.tensor_scalar(oh[b][k][:, 0:P], io_hi[:, :], hl[k][0][:, bass.ds(j, 1)], None, ALU.is_equal)
                    m.then_inc(S["onehots_ready"], 1)

            pairs(v, EC // 2, onehots)

            counts = [ps[k][:, :].rearrange("p (h w) -> p h w", h=2)[:, :, 0:EC] for k in range(2)]
            two = lambda t: t[:, :].rearrange("p (h w) -> p h w", h=2)
            root, indeg, has, cum, first = tn
            v.wait_ge(S["counts_done"], 1)
            v.tensor_scalar(two(root), counts[0], 1.0, None, ALU.max).then_inc(S["sqrt_in"], 1)
            order(v.tensor_copy(two(indeg), counts[1]))
            order(v.memset(ones[:, :], 1.0))
            order(v.tensor_tensor_scan(cum[:, :], ones[:, :], indeg[:, :], 0.0, ALU.mult, ALU.add))
            v.tensor_copy(offs[:, 0:1], cum[:, NN - 1:NN]).then_inc(S["totals_ready"], 1)
            order(v.tensor_scalar(has[:, :], indeg[:, :], 0.5, None, ALU.is_ge))
            v.wait_ge(S["norm_done"], 1)
            order(v.reciprocal(aux[:, :, 0], root[:, :]))
            v.wait_ge(S["offset_done"], 1)
            order(v.tensor_copy(offs[:, 1:2], psC[:, 0:1]))
            order(v.tensor_scalar(cum[:, :], cum[:, :], offs[:, 1:2], -1.0, ALU.add, ALU.add))
            order(v.scalar_tensor_tensor(out=first[:, :], in0=cum[:, :], scalar=1.0, in1=indeg[:, :], op0=ALU.add, op1=ALU.subtract))
            order(v.tensor_scalar(offs[:, 0:1], io_part[:, :], float(EPAD), None, ALU.add))
            order(v.tensor_scalar(root[:, :], cum[:, :], offs[:, 0:1], None, ALU.subtract))
            order(v.tensor_tensor(root[:, :], root[:, :], has[:, :], ALU.mult))
            order(v.tensor_scalar(aux[:, :, 1], root[:, :], offs[:, 0:1], None, ALU.add))
            for k, pos in ((2, cum), (3, first)):
                order(v.scalar_tensor_tensor(out=root[:, :], in0=pos[:, :], scalar=float(NPAD), in1=io_node[:, :],
                                             op0=ALU.add, op1=ALU.subtract))
                order(v.tensor_tensor(root[:, :], root[:, :], has[:, :], ALU.mult))
                order(v.tensor_tensor(aux[:, :, k], root[:, :], io_node[:, :], ALU.add))
            for c in range(NN // XC):
                b = c % 2
                need(v, ld["st_ext"][b], 16 * (c // 2))
                v.tensor_copy(extb[b][:, :, D:XW], aux[:, c * XC:(c + 1) * XC, :]).then_inc(S["ext_aux"], 1)

            v.wait_ge(S["w_loaded"], W_LOADED)
            for l in range(3):
                order(v.tensor_scalar(wqs[l][:, 0:D], wqs[l][:, 0:D], float((D // HEADS[l]) ** -0.5), None, ALU.mult))
            order(v.tensor_scalar(slope[:, 1:2], slope[:, 0:1], -1.0, None, ALU.add))
            order(v.tensor_scalar(slope[:, 2:3], slope[:, 0:1], -1.0, 1.0, ALU.mult, ALU.add))
            order(v.tensor_scalar(relu_b[1][:, :], relu_b[1][:, :], 0.0, None, ALU.max))
            v.tensor_scalar(relu_b[0][:, :], relu_b[0][:, :], 0.0, None, ALU.max).then_inc(S["relu_made"], 1)

            order(v.memset(m_all[:, :, :], 0.0))
            order(v.memset(s_all[:, :, :], 0.0))
            order(v.memset(fr[:, :, :], 0.0))
            order(v.tensor_tensor(hl[0][0][:, :], ef[:, 1, :], ef[:, 2, :], ALU.is_equal))
            order(v.tensor_tensor(hl[0][1][:, :], ef[:, 1, :], ef[:, 3, :], ALU.is_equal))
            go, end, lead = hl[1][0], hl[1][1], te[2]
            chunks = lambda t: t[:, :].rearrange("p (c t) -> p c t", t=T)
            flat8 = lambda t: t[:, :, :].rearrange("p c s -> p (c s)")

            def total(to, in0, in1):
                order(v.tensor_tensor(fsel[:, :, :], in0, in1, ALU.mult))
                order(v.tensor_reduce(to, flat8(fsel), AX, ALU.add))

            def carry_over(d, k):
                order(v.tensor_tensor_scan(fr[:, k, 1:P + 1], ft[:, 3, :], ft[:, k, :], 0.0, ALU.mult, ALU.add))

            for d in range(2):
                order(v.tensor_copy(go[:, :], mem(hl[0][d][:, :], d)))
                order(v.tensor_scalar(end[:, :], mem(hl[0][1 - d][:, :], d), -1.0, 1.0, ALU.mult, ALU.add))
                order(v.tensor_scalar(new[d][:, :], go[:, :], -1.0, 1.0, ALU.mult, ALU.add))
                order(v.memset(mask8[d][:, :, :], 0.0))
                order(v.tensor_copy(mask8[d][:, :, 1:SL], chunks(go)))
                order(v.memset(pen16[d][:, :, :, :], -BIG))
                for h in range(2):
                    order(v.tensor_scalar(pen16[d][:, :, h, 1:SL], chunks(new[d]), -BIG, None, ALU.mult))
                order(v.memset(te[0][:, :], 0.0))
                order(v.tensor_tensor_scan(lead[:, :], go[:, :], te[0][:, :], 1.0, ALU.mult, ALU.add))
                order(v.tensor_copy(cont_all[d][:, :], lead[:, EC - 1:EC]))
                order(v.memset(fmask[d][:, :, :], 0.0))
                order(v.tensor_tensor(fmask[d][:, :, 1:SL], chunks(lead), chunks(end), ALU.mult))
                order(v.tensor_reduce(fixed[d][:, 0:1], flat8(fmask[d]), AX, ALU.add))
                order(v.tensor_scalar(fixed[d][:, 1:2], fixed[d][:, 0:1], -1.0, 1.0, ALU.mult, ALU.add))
                order(v.tensor_reduce(slotm[d][:, :], fmask[d][:, :, :].rearrange("p c s -> p s c"), AX, ALU.add))
                total(fsc[:, 0:1], fmask[d][:, :, :], io_blk[:, :, :])
                total(fsc[:, 1:2], fmask[d][:, :, :], io_row[d][:, :, :])
                order(v.scalar_tensor_tensor(out=fsc[:, 2:3], in0=fixed[d][:, 1:2], scalar=float(EPAD + P), in1=fsc[:, 1:2],
                                             op0=ALU.mult, op1=ALU.add))
                order(v.scalar_tensor_tensor(out=fsc[:, 3:4], in0=fixed[d][:, 1:2], scalar=float(EPAD), in1=fsc[:, 1:2],
                                             op0=ALU.mult, op1=ALU.add))
                order(v.tensor_scalar(fsc[:, 3:4], fsc[:, 3:4], float(NPAD), None, ALU.add))
                order(v.tensor_copy(fixi[d][:, :], fsc[:, 0:4]))
                if d == 0:
                    order(v.tensor_tensor(fsel[:, :, 1:SL], fmask[0][:, :, 1:SL], ef[:, 1, :].rearrange("p (c t) -> p c t", t=T), ALU.mult))
                    order(v.memset(fsel[:, :, 0:1], 0.0))
                    order(v.tensor_reduce(fsc[:, 0:1], flat8(fsel), AX, ALU.add))
                    order(v.scalar_tensor_tensor(out=fsc[:, 0:1], in0=fixed[0][:, 1:2], scalar=float(NPAD), in1=fsc[:, 0:1],
                                                 op0=ALU.mult, op1=ALU.add))
                    order(v.tensor_copy(fixo[:, :], fsc[:, 0:1]))
                order(v.tensor_tensor_scan(te[0][:, :], go[:, :], ones[:, 0:EC], 0.0, ALU.mult, ALU.add))
                order(v.tensor_copy(tails[:, 0, :], te[0][:, EC - 1:EC].broadcast_to([P, D])))
                v.tensor_copy(tails[:, 3, :], cont_all[d][:, :].broadcast_to([P, D])).then_inc(S["deg_tail"], 1)
                v.wait_ge(S["degT"], d + 1)
                order(v.tensor_copy(ft[:, 0, :], mem(psC[0:D, 0:P], d)))
                order(v.tensor_copy(ft[:, 3, :], mem(psC[0:D, P:2 * P], d)))
                carry_over(d, 0)
                v.tensor_copy(fc[:, 0, :], mem(fr[:, 0, 0:P], d)).then_inc(S["deg_carry"], 1)
                v.wait_ge(S["deg_back"], d + 1)
                order(v.tensor_copy(carry[:, 0, :], psC[:, 0:D]))
                v.tensor_tensor_scan(te[0][:, :], go[:, :], ones[:, 0:EC], carry[:, 0, 0:1], ALU.mult, ALU.add
                                     ).then_inc(S["inn_in"], 1)
                v.wait_ge(S["inn_std"], d + 1)
                order(v.reciprocal(inn[d][:, :], te[1][:, :]))
            order(v.scalar_tensor_tensor(out=te[0][:, :], in0=hl[0][1][:, :], scalar=float(NPAD), in1=ef[:, 1, :],
                                         op0=ALU.mult, op1=ALU.add))
            order(v.tensor_copy(gi[3][:, :], te[0][:, :]))
            order(v.memset(d8[:, 0, :], -BIG))
            order(v.memset(d8[:, 1, :], 0.0))

            GATHERED = (1, 3, 5, 7, 10)

            def pick(to, blk, d, done=None):
                order(v.tensor_tensor(fbm[:, :, :], blk[:, :].rearrange("p (f s) -> p f s", s=SL),
                                      slotm[d][:, :].unsqueeze(1).broadcast_to([P, D, SL]), ALU.mult))
                m = v.tensor_reduce(to, fbm[:, :, :], AX, ALU.add)
                m.then_inc(done, 1) if done else order(m)

            def fix(r):
                d = int(REVERSE[r])
                n = r + 1
                t_round = r >= 2
                l = r - 2
                H = HEADS[l] if t_round else 1
                heads = lambda ap: bc(ap, D // H)
                hc = lambda ap: ap.rearrange("p (h c) -> p h c", h=H)
                last = lambda t: t[:, CH, 0:H * SL].rearrange("p (h s) -> p h s", s=SL)[:, :, SL - 1]
                if t_round:
                    v.wait_ge(S["t_agg"], CH * (l + 1))
                    v.wait_ge(S["t_s"], CH * (l + 1))
                    order(v.tensor_copy(hc(tails[:, 1, :]), heads(last(s_all))))
                    order(v.tensor_copy(hc(tails[:, 2, :]), heads(last(m_all))))
                else:
                    v.wait_ge(S["gc_agg"], CH * (r + 1))
                order(v.tensor_copy(tails[:, 0, :], slot(aggF[1], SL - 1)))
                v.tensor_copy(tails[:, 3, :], cont_all[d][:, :].broadcast_to([P, D])).then_inc(S["fx_tail"], 1)
                v.wait_ge(S["fx_tailT"], n)
                for k in (range(4) if t_round else (0, 3)):
                    order(v.tensor_copy(ft[:, k, :], mem(psA[0:D, k * P:(k + 1) * P], d)))
                if t_round:
                    M, Mprev = fr[:, 2, 1:P + 1], fr[:, 2, 0:P]
                    order(v.tensor_scalar(fd[:, 0, :], ft[:, 3, :], BIG, -BIG, ALU.mult, ALU.add))
                    order(v.tensor_tensor_scan(M, fd[:, 0, :], ft[:, 2, :], 0.0, ALU.add, ALU.max))
                    order(v.tensor_tensor(fd[:, 1, :], Mprev, M, ALU.subtract))
                    order(v.tensor_tensor(fd[:, 0, :], fd[:, 0, :], fd[:, 1, :], ALU.add))
                    v.tensor_tensor(fd[:, 1, :], ft[:, 2, :], M, ALU.subtract).then_inc(S["fx_d"], 1)
                    v.wait_ge(S["fx_e"], 2 * l + 1)
                    for k in range(2):
                        order(v.tensor_tensor(ft[:, k, :], ft[:, k, :], fe[:, 1, :], ALU.mult))
                        order(v.tensor_tensor_scan(fr[:, k, 1:P + 1], fe[:, 0, :], ft[:, k, :], 0.0, ALU.mult, ALU.add))
                    v.tensor_copy(fc[:, :, :], fr[:, :, 0:P][:, :, ::-1] if d else fr[:, :, 0:P]).then_inc(S["fx_carry"], 1)
                else:
                    carry_over(d, 0)
                    v.tensor_copy(fc[:, 0, :], mem(fr[:, 0, 0:P], d)).then_inc(S["fx_carry"], 1)
                v.wait_ge(S["fx_back"], n)
                nk = 3 if t_round else 1
                order(v.tensor_copy(carry[:, 0:nk, :], psA[:, 0:nk * D].rearrange("p (k f) -> p k f", f=D)))
                v.wait_ge(S["fx_gather"], 16 * GATHERED[r])
                pick(pre[:, 0, :], fb, d)
                if not t_round:
                    order(v.memset(fsel[:, :, 0:1], 0.0))
                    order(v.tensor_tensor(fsel[:, :, 1:SL], fmask[d][:, :, 1:SL], chunks(inn[d]), ALU.mult))
                    order(v.tensor_reduce(fsc[:, 0:1], flat8(fsel), AX, ALU.add))
                    order(v.tensor_tensor(fz[:, 2, :], carry[:, 0, :], pre[:, 0, :], ALU.add))
                    v.tensor_scalar(fz[:, 0, :], fz[:, 2, :], fsc[:, 0:1], None, ALU.mult).then_inc(S["fx_z"], 1)
                    v.wait_ge(S["fx_relu"], n)
                    need(v, S["fx_scatter"], 16 * r)
                    if r == 0:
                        v.tensor_copy(frow[:, :], fz[:, 1, :]).then_inc(S["fx_row"], 1)
                        v.wait_ge(S["fx_row"], 1)
                        return
                    order(v.tensor_tensor(fz[:, 2, :], fz[:, 1, :], fxd[:, :], ALU.add))
                    y = fz[:, 2:3, :]
                else:
                    pick(fz[:, 0, :], fh, d, S["fx_z"])
                    for k, t in ((1, s_all), (2, m_all)):
                        for h in range(H):
                            total(fsc[:, h:h + 1], fmask[d][:, :, :], t[:, 1:CH + 1, h * SL:(h + 1) * SL])
                        order(v.tensor_copy(hc(pre[:, k, :]), heads(fsc[:, 0:H])))
                    order(v.tensor_tensor(fm2[:, :], carry[:, 2, :], pre[:, 2, :], ALU.max))
                    order(v.tensor_tensor(fdd[:, 0, :], carry[:, 2, :], fm2[:, :], ALU.subtract))
                    v.tensor_tensor(fdd[:, 1, :], pre[:, 2, :], fm2[:, :], ALU.subtract).then_inc(S["fx_d"], 1)
                    v.wait_ge(S["fx_e"], 2 * l + 2)
                    for k in range(2):
                        order(v.tensor_tensor(fz[:, 1 + k, :], carry[:, k, :], fee[:, 0, :], ALU.mult))
                        order(v.tensor_tensor(fz[:, 3, :], pre[:, k, :], fee[:, 1, :], ALU.mult))
                        order(v.tensor_tensor(fz[:, 1 + k, :], fz[:, 1 + k, :], fz[:, 3, :], ALU.add))
                    order(v.tensor_scalar(fz[:, 2, :], fz[:, 2, :], 1e-16, None, ALU.add))
                    order(v.reciprocal(fz[:, 2, :], fz[:, 2, :]))
                    order(v.tensor_tensor(fz[:, 1, :], fz[:, 1, :], fz[:, 2, :], ALU.mult))
                    v.wait_ge(S["fx_mm"], n)
                    order(v.tensor_tensor(fz[:, 1, :], fz[:, 1, :], psC[:, D:2 * D], ALU.add))
                    need(v, S["fx_scatter"], 16 * r)
                    if l < 2:
                        order(v.tensor_scalar(fz[:, 2, :], fz[:, 1, :], 0.0, slope[:, 1:2], ALU.min, ALU.mult))
                        v.tensor_tensor(frow[:, :], fz[:, 2, :], fz[:, 1, :], ALU.add).then_inc(S["fx_row"], 1)
                        v.wait_ge(S["fx_row"], n)
                    else:
                        pick(fz[:, 3, :], fx1, d)
                        order(v.tensor_tensor(fz[:, 1, :], fz[:, 1, :], fz[:, 3, :], ALU.add))
                        y = fz[:, 1:2, :]
                if r in (1, 4):
                    k = 1 if r == 1 else 2
                    L = LS["LF"]
                    ln_centre(L, k, fln, "LF", y)
                    ln_spread(L, k, fln, "LF")
                    ln_scale(L, k, fln, "LF", fz[:, 4:5, :])
                    v.wait_ge(L["LF_out"], k)
                    v.tensor_copy(frow[:, :], fz[:, 4, :]).then_inc(S["fx_row"], 1)
                    v.wait_ge(S["fx_row"], n)
                if r == 4:
                    return
                order(v.tensor_scalar(tails[:, 0, :], frow[:, :], fixed[d][:, 0:1], None, ALU.mult))
                v.tensor_copy(tails[:, 1, :], fixed[d][:, 1:2].broadcast_to([P, D])).then_inc(S["fx_hT"], 1)
                v.wait_ge(S["fx_hTr"], 2 * r - 1)
                for k in range(2):
                    order(v.tensor_copy(ft[:, k, :], mem(psA[0:D, k * P:(k + 1) * P], not d)))
                order(v.tensor_tensor_scan(fr[:, 0, 1:P + 1], ft[:, 1, :], ft[:, 0, :], 0.0, ALU.mult, ALU.add))
                v.tensor_copy(fc[:, 0, :], mem(fr[:, 0, 0:P], not d)).then_inc(S["fx_ho"], 1)
                v.wait_ge(S["fx_hTr"], 2 * r)
                need(v, ld["st_hd"][1], LB * (r - 1))
                order(v.tensor_copy(slot(hd[1], SL - 1), psB[:, 0:D]))

            def gc_step(r, i, b):
                c = 2 * i + b
                n = r * CH + c + 1
                d = int(REVERSE[r])
                L, w = LS["LD"], lnb["lnd"]
                cols = bass.ds(c * T, T)
                v.wait_ge(ld["ld_xin"][b], r * LB + 16 * (i + 1))
                v.tensor_tensor(yd[:, :, :], xin[b][:, :, :], relu_b[1][:, :].unsqueeze(1).broadcast_to([P, T, D]), ALU.add
                                ).then_inc(S["d_y"], 1)
                v.wait_ge(S["d_y"], n)
                ln_centre(L, 2 * n - 1, w, "LD", yd[:, :, :])
                v.wait_ge(ld["gat"][b], (1 + r) * T * LB + 16 * T * (i + 1))
                if r == 0:
                    v.tensor_copy(idx_f[:, :, cols], gs[b][:, :, D + 1:XW].rearrange("p t k -> p k t")).then_inc(S["gc_extract"], 1)
                    v.tensor_copy(norm_e[:, cols], gs[b][:, :, D]).then_inc(S["gc_extract"], 1)
                    norm = gs[b][:, :, D]
                else:
                    norm = norm_r[:, cols]
                v.tensor_tensor(fj(msgF), gs[b][:, :, 0:D], bc(norm, D), ALU.mult).then_inc(S["gc_msg"], 1)
                v.tensor_copy(slot(msgF, 0), slot(aggF[1 - b], SL - 1)).then_inc(S["gc_carry"], 1)
                ln_spread(L, 2 * n - 1, w, "LD")
                v.wait_ge(S["gc_maskF"], n)
                v.wait_ge(S["gc_carry"], n)
                need(v, ld["st_agg"][b], r * LB + 16 * i)
                v.tensor_tensor_scan(aggF[b][:, :], maskF[b][:, :], msgF[:, :], 0.0, ALU.mult, ALU.add).then_inc(S["gc_agg"], 1)
                need(v, ld["st_d"][b], 64 * (r * PAIRS + i))
                ln_scale(L, 2 * n - 1, w, "LD", x1d[b][:, :, :])
                v.wait_ge(S["gc_agg"], n)
                need(v, S["gc_zT"], n - 1)
                v.tensor_tensor(u1[:, :, :], fj(aggF[b]), bc(inn[d][:, cols], D), ALU.mult).then_inc(S["gc_z"], 1)
                for k in range(2):
                    if r == 1 and k == 0:
                        v.wait_ge(S["gc_relu"], n)
                        v.wait_ge(ld["ld_xd"][b], 16 * (i + 1))
                        v.tensor_tensor(u3[:, :, :], mem(u2[:, :, :], True), hrow[b][:, :, :], ALU.add).then_inc(S["gc_y"], 1)
                        v.wait_ge(S["gc_y"], c + 1)
                        ln_centre(LS["LE"], c + 1, lnb["lne"], "LE", u3[:, :, :])
                    v.wait_ge(S["d_neg"], 2 * (n - 1) + k + 1)
                    v.scalar_tensor_tensor(out=(t1d, t2d)[k][b][:, :, :], in0=neg[:, :, :], scalar=slope[:, 2:3],
                                           in1=psD[:, 0:HC].rearrange("p (t f) -> p t f", f=D), op0=ALU.mult, op1=ALU.add
                                           ).then_inc(S["d_pre"], 1)
                    if r == 1 and k == 0:
                        ln_spread(LS["LE"], c + 1, lnb["lne"], "LE")
                if r == 1:
                    need(v, ld["st_hn"][b], LB + 16 * i)
                    ln_scale(LS["LE"], c + 1, lnb["lne"], "LE", hnew[b][:, :, :])
                v.wait_ge(S["d_mm"], 3 * n)
                v.tensor_tensor(yd[:, :, :], x1d[b][:, :, :], psD[:, 0:HC].rearrange("p (t f) -> p t f", f=D), ALU.add
                                ).then_inc(S["d_res"], 1)
                v.wait_ge(S["d_res"], n)
                ln_centre(L, 2 * n, w, "LD", yd[:, :, :])
                ln_spread(L, 2 * n, w, "LD")
                ln_scale(L, 2 * n, w, "LD", od[b][:, :, :])

            for r in range(2):
                if r:
                    v.wait_ge(ld["st_agg"][1], LB * r)
                order(v.memset(slot(aggF[1], SL - 1), 0.0))

                def gc_body(i):
                    for b in range(2):
                        gc_step(r, i, b)

                pairs(v, PAIRS, gc_body)
                if r == 0:
                    v.wait_ge(S["gc_extract"], 2 * CH)
                    order(v.tensor_copy(norm_r[:, :], norm_e[:, ::-1]))
                    order(v.tensor_copy(gi[0][:, :], idx_f[:, 0, :][:, ::-1]))
                    order(v.tensor_copy(gi[1][:, :], idx_f[:, 2, :]))
                    v.tensor_copy(gi[2][:, :], idx_f[:, 1, :][:, ::-1]).then_inc(S["idx_made"], 1)
                fix(r)

            mf = m_all[:, :, :].rearrange("p c s -> p (c s)")
            sf = s_all[:, :, :].rearrange("p c s -> p (c s)")
            k3 = psC[:, 0:T * 2 * D].rearrange("p (t f) -> p t f", f=2 * D)

            def hd_prepare(l, i, b):
                c = 2 * i + b
                d = int(REVERSE[2 + l])
                v.wait_ge(ld["ld_h"][b], l * LB + 16 * (i + 1))
                v.tensor_tensor(fj(hp), mem(hrow[b][:, :, :], d), bc(new[d][:, bass.ds(c * T, T)], D), ALU.mult
                                ).then_inc(S["t_hp"], 1)

            def hd_carry(b):
                v.tensor_copy(slot(hp, 0), slot(hd[1 - b], SL - 1)).then_inc(S["t_hpc"], 1)

            def hd_scan(l, i, b):
                n = l * CH + 2 * i + b + 1
                v.wait_ge(S["t_maskF"], n)
                v.wait_ge(S["t_hpc"], n)
                need(v, S["t_trh"], n - 2)
                need(v, ld["st_hd"][b], l * LB + 16 * i)
                v.tensor_tensor_scan(hd[b][:, :], maskF[b][:, :], hp[:, :], 0.0, ALU.mult, ALU.add).then_inc(S["t_hd"], 1)

            def t_step(l, i, b):
                c = 2 * i + b
                n = l * CH + c + 1
                d = int(REVERSE[2 + l])
                H = HEADS[l]
                HS = H * SL
                more = not (isinstance(i, int) and i == PAIRS - 1 and b == 1)
                nxt = (l, i + b, 1 - b)
                hs = lambda ap: ap.rearrange("p (h s) -> p h s", s=SL)
                over = lambda ap: ap.unsqueeze(2).broadcast_to([P, H, D // H, T])
                wide = lambda t, lo, hi: t[:, :].rearrange("p (h c s) -> p h c s", h=H, s=SL)[:, :, :, lo:hi]
                m_old, m_new = mf[:, bass.ds(c * 2 * SL, HS)], mf[:, bass.ds((c + 1) * 2 * SL, HS)]
                s_old, s_new = sf[:, bass.ds(c * 2 * SL, HS)], sf[:, bass.ds((c + 1) * 2 * SL, HS)]
                pen = pen16[d][:, :, :, :].rearrange("p c h s -> p (c h s)")[:, bass.ds(c * 2 * SL, HS)]
                v.wait_ge(S["t_qs"], n)
                v.wait_ge(S["t_kv"], n)
                v.tensor_tensor(prod[:, :, :], qs[b][:, :, 0:D], k3[:, :, 0:D], ALU.mult).then_inc(S["t_prod"], 1)
                if more:
                    hd_prepare(*nxt)
                v.wait_ge(S["t_prod"], n)
                v.tensor_reduce(hs(alpha8[:, 0:HS])[:, :, 1:SL].rearrange("p h t -> p t h"),
                                prod[:, :, :].rearrange("p t (h c) -> p t h c", h=H), AX, ALU.add).then_inc(S["t_alpha"], 1)
                v.tensor_copy(hs(alpha8[:, 0:HS])[:, :, 0], hs(m_old)[:, :, SL - 1]).then_inc(S["t_acar"], 1)
                if more:
                    hd_carry(1 - b)
                v.wait_ge(S["t_acar"], n)
                v.tensor_tensor_scan(m_new, pen, alpha8[:, 0:HS], 0.0, ALU.add, ALU.max).then_inc(S["t_m"], 1)
                if more:
                    hd_scan(*nxt)
                v.wait_ge(S["t_m"], n)
                v.tensor_tensor(hs(d8[:, 0, 0:HS])[:, :, 1:SL], hs(m_new)[:, :, 0:T], hs(m_new)[:, :, 1:SL], ALU.subtract
                                ).then_inc(S["t_d0"], 1)
                v.tensor_tensor(hs(d8[:, 1, 0:HS])[:, :, 1:SL], hs(alpha8[:, 0:HS])[:, :, 1:SL], hs(m_new)[:, :, 1:SL],
                                ALU.subtract)
                v.wait_ge(S["t_d0"], n)
                v.tensor_tensor(hs(d8[:, 0, 0:HS])[:, :, 1:SL], hs(d8[:, 0, 0:HS])[:, :, 1:SL], hs(pen)[:, :, 1:SL], ALU.add
                                ).then_inc(S["t_d"], 1)
                v.tensor_copy(slot(msgF, 0), slot(aggF[1 - b], SL - 1)).then_inc(S["t_avc"], 1)
                v.wait_ge(S["t_e"], n)
                v.tensor_copy(hs(e8[:, 1, 0:HS])[:, :, 0], hs(s_old)[:, :, SL - 1]).then_inc(S["t_scar"], 1)
                v.tensor_tensor(wide(msgF, 1, SL), k3[:, :, D:2 * D].rearrange("p t (h c) -> p h c t", h=H),
                                over(hs(e8[:, 1, 0:HS])[:, :, 1:SL]), ALU.mult).then_inc(S["t_av"], 1)
                v.wait_ge(S["t_scar"], n)
                v.tensor_tensor_scan(s_new, e8[:, 0, 0:HS], e8[:, 1, 0:HS], 0.0, ALU.mult, ALU.add).then_inc(S["t_s"], 1)
                v.wait_ge(S["t_cF"], n)
                v.wait_ge(S["t_av"], n)
                v.wait_ge(S["t_avc"], n)
                need(v, ld["st_agg"][b], (2 + l) * LB + 16 * i)
                v.tensor_tensor_scan(aggF[b][:, :], cF[:, :], msgF[:, :], 0.0, ALU.mult, ALU.add).then_inc(S["t_agg"], 1)
                v.wait_ge(S["t_s"], n)
                v.tensor_scalar(r8[:, 0:HS], s_new, 1e-16, None, ALU.add).then_inc(S["t_r0"], 1)
                v.wait_ge(S["t_r0"], n)
                v.reciprocal(r8[:, 0:HS], r8[:, 0:HS]).then_inc(S["t_r"], 1)
                v.wait_ge(S["t_r"], n)
                v.wait_ge(S["t_agg"], n)
                v.tensor_tensor(u1[:, :, :].rearrange("p t (h c) -> p h c t", h=H), wide(aggF[b], 1, SL),
                                over(hs(r8[:, 0:HS])[:, :, 1:SL]), ALU.mult).then_inc(S["t_u1"], 1)
                v.wait_ge(S["t_u1"], n)
                v.tensor_tensor(u2[:, :, :], u1[:, :, :], qs[b][:, :, D:2 * D], ALU.add).then_inc(S["t_u2"], 1)
                v.wait_ge(S["t_u2"], n)
                if l < 2:
                    v.tensor_scalar(u3[:, :, :], u2[:, :, :], 0.0, slope[:, 1:2], ALU.min, ALU.mult).then_inc(S["t_u3"], 1)
                    need(v, ld["st_hn"][b], (2 + l) * LB + 16 * i)
                    v.wait_ge(S["t_u3"], n)
                    v.tensor_tensor(mem(hnew[b][:, :, :], d), u3[:, :, :], u2[:, :, :], ALU.add).then_inc(S["t_hn"], 1)
                else:
                    v.wait_ge(ld["ld_x1"][b], 16 * (i + 1))
                    v.tensor_tensor(u3[:, :, :], u2[:, :, :], fj(x1b[b]), ALU.add).then_inc(S["t_y"], 1)
                    v.wait_ge(S["t_y"], c + 1)
                    L, w = LS["LE"], lnb["lne"]
                    ln_centre(L, CH + c + 1, w, "LE", u3[:, :, :])
                    ln_spread(L, CH + c + 1, w, "LE")
                    need(v, ld["scat"][b], 16 * T * i)
                    if isinstance(i, int) and i == 0:
                        v.wait_ge(ld["st_hn"][b], 4 * LB)
                    ln_scale(L, CH + c + 1, w, "LE", hnew[b][:, :, :])

            for l in range(3):
                v.wait_ge(ld["st_agg"][1], LB * (2 + l))
                order(v.memset(slot(aggF[1], SL - 1), 0.0))
                hd_prepare(l, 0, 0)
                hd_carry(0)
                hd_scan(l, 0, 0)

                def t_body(i):
                    for b in range(2):
                        t_step(l, i, b)

                pairs(v, PAIRS, t_body)
                fix(2 + l)


_L = [f"L1_gnn_{w}{k}" for k in range(3) for w in ("Wq", "bq", "Wk", "bk", "Wv", "bv", "We", "Ws", "bs")]
_INS = ["x", "src", "dst", "edge_attr_32", "L0_gnn_W1", "L0_gnn_b1", "L0_gnn_W2", "L0_gnn_b2", *_L, "L1_gnn_prelu_a"]


def kernel(**inputs):
    import numpy as np
    import concourse.bacc as bacc
    from concourse.bass_utils import run_bass_kernel_spmd

    given = {k: np.asarray(v) for k, v in inputs.items()}
    given["x"] = np.pad(given["x"], ((0, NPAD - N_NODES), (0, 0)))
    given["src"] = np.pad(given["src"], (0, EPAD - N_EDGES), constant_values=N_NODES)
    given["dst"] = np.pad(given["dst"], (1, EPAD - N_EDGES), constant_values=(-1, N_NODES))
    given["dst"] = np.pad(given["dst"], (0, 1), constant_values=N_NODES + 1)
    ea = np.pad(given["edge_attr_32"], ((0, EPAD - N_EDGES), (0, 0)))
    given["edge_attr_32"] = ea.reshape(P, EC, DE).transpose(2, 1, 0).reshape(DE, EC * P)
    given["L1_gnn_prelu_a"] = given["L1_gnn_prelu_a"].reshape(1)

    nc = bacc.Bacc("TRN2", target_bir_lowering=False, num_devices=1)
    arrays, aps = {}, {}
    for name in _INS:
        a = np.ascontiguousarray(given[name])
        arrays[f"in_{name}"] = a
        aps[name] = nc.dram_tensor(f"in_{name}", a.shape, mybir.dt.from_np(a.dtype), kind="ExternalInput").ap()
    out = nc.dram_tensor("out_0", (NPAD, D), F32, kind="ExternalOutput").ap()
    layers = [[aps[n] for n in _L[9 * k:9 * k + 9]] for k in range(3)]
    gnn_kernel(nc, aps["x"], aps["src"], aps["dst"], aps["edge_attr_32"], aps["L0_gnn_W1"], aps["L0_gnn_b1"],
               aps["L0_gnn_W2"], aps["L0_gnn_b2"], layers, aps["L1_gnn_prelu_a"], out)
    r = run_bass_kernel_spmd(nc, [arrays], core_ids=[0])
    return r.results[0]["out_0"][0:N_NODES]
```

```python
import math
from contextlib import ExitStack

import concourse.bass as bass
from concourse import mybir

F32 = mybir.dt.float32
F16 = mybir.dt.float16
BF16 = mybir.dt.bfloat16
I32 = mybir.dt.int32
ALU = mybir.AluOpType
ACT = mybir.ActivationFunctionType
AX = mybir.AxisListType.X

P = 128
D = 64
DE = 32
N_NODES, N_EDGES = 100000, 50000
T = 7
SL = T + 1
EC = 392
CH = EC // T
PAIRS = CH // 2
QUADS = CH // 4
NN = 2 * EC
NPAD, EPAD = P * NN, P * EC
XW = D + 4
XC = 28
BIG = 1.0e30
EPS = 1e-5
HC = T * D
FS = D * SL
HEADS = (2, 2, 1)
assert EC % (2 * T) == 0 and NPAD > N_NODES and EPAD > N_EDGES and NN % (2 * XC) == 0

REVERSE = (False, True, False, True, False)


W_LOADED = 16 * (3 * 10 + 2 * 3 + 1 + 5 * 3)


class Step:

    def __init__(self, r, i, j, lag=0):
        self.r, k = r, j - lag
        self.c = 4 * i + k
        self.g = r * CH + self.c
        self.n = self.g + 1
        self.b, self.q = k % 2, k % 4
        self.h = r * PAIRS + 2 * i + k // 2
        self.k = r * QUADS + i + k // 4
        self.fixed = isinstance(i, int)
        self.edges = not self.fixed or 0 <= self.c < CH
        self.dense = not self.fixed or 0 <= self.g < 2 * CH


class Order:

    def __init__(self, eng, s):
        self.eng, self.s, self.n = eng, s, 0

    def __call__(self, instruction):
        self.n += 1
        instruction.then_inc(self.s, 1)
        self.eng.wait_ge(self.s, self.n)


def gnn_kernel(nc, x, src, dst, eaT, W1, b1, W2, b2, layers, prelu_a, out):
    with ExitStack() as ctx:
        def sb(name, shape, dt=F32):
            return ctx.enter_context(nc.sbuf_tensor(name, shape, dt))

        def sem(name):
            return ctx.enter_context(nc.semaphore(name))

        def sems(names):
            return {n: sem(n) for n in names.split()}

        def dram(name, shape, dt=F32):
            return nc.dram_tensor(name, shape, dt).ap()

        ext = dram("ext", (NPAD, XW))
        xd_rows = dram("xd_rows", (EPAD, D))
        tab_h1 = dram("tab_h1", (EPAD + P, D))
        tab = [dram(f"tab{k}", (NPAD + EPAD, D)) for k in range(3)]
        agg_blk = dram("agg_blk", (P * CH, FS))
        hd_blk = [dram(f"hd_blk{k}", (P * CH, FS)) for k in range(3)]

        def rows(t, lo=0, n=EPAD):
            return t[lo:lo + n, :].rearrange("(p c) f -> p (c f)", p=P)

        def blocks(t):
            return t.rearrange("(p c) f -> p (c f)", p=P)

        def shared(name, early, late):
            def words(spec):
                return -(-math.prod(spec[1][1:]) * (2 if spec[2:] == (F16,) else 4) // 4)

            whole = sb(name, [P, max(sum(map(words, s)) for s in (early, late))])
            got = {}
            for specs in (early, late):
                at = 0
                for spec in specs:
                    ap = whole[0:spec[1][0], at:at + words(spec)]
                    if spec[2:] == (F16,):
                        ap = ap.bitcast(F16)
                    if len(spec[1]) == 3:
                        ap = ap.rearrange("p (a b) -> p a b", b=spec[1][2])
                    got[spec[0]] = ap
                    at += words(spec)
            return got

        two_of = lambda names, shape: [(f"{n}{b}", shape) for n in names.split() for b in range(2)]
        B = shared("nodes_or_dense", [(f"tn{k}", [P, NN]) for k in range(5)], [(f"x1d{q}", [P, T, D]) for q in range(4)] + two_of("t1d t2d", [P, T, D]))
        B |= shared("ext_or_attention", two_of("extb", [P, XC, XW]),
                    two_of("qs", [P, T, 2 * D]) + [("prod", [P, T, D]), ("cF", [P, FS]), ("hp", [P, FS])])
        B |= shared("aux_or_rows", [("aux", [P, NN, 4])], two_of("hnew", [P, T, D]) + [(f"u{k}", [P, T, D]) for k in (1, 2, 3)])
        B |= shared("onehots_or_sums", [(f"oh{b}_{k}", [P, P + NN], F16) for b in range(2) for k in range(2)],
                    [("m_all", [P, CH + 1, 2 * SL]), ("s_all", [P, CH + 1, 2 * SL])])
        B |= shared("degrees_or_dense",
                    [(f"hl{k}_{j}", [P, EC]) for k in range(2) for j in range(2)] + [(f"te{k}", [P, EC]) for k in range(3)]
                    + [("ef", [P, 4, EC]), ("io_node", [P, NN]), ("ones", [P, NN]), ("io_blk", [P, CH, SL])]
                    + [(f"io_row{d}", [P, CH, SL]) for d in range(2)],
                    [(f"nT{k}", [P, 4 * P]) for k in range(3)] + [("zT", [P, 4 * P])] + two_of("neg yd", [P, T, D])
                    + [(f"{k}_{j}", [P, T, D]) for k in ("lna", "lnb", "lne") for j in ("xc", "sq")])
        hl = [[B[f"hl{k}_{j}"] for j in range(2)] for k in range(2)]
        te, nT = ([B[f"{n}{k}"] for k in range(3)] for n in ("te", "nT"))
        neg, yd, io_row = ([B[f"{n}{k}"] for k in range(2)] for n in ("neg", "yd", "io_row"))
        ef, io_node, ones, io_blk, zT = (B[n] for n in "ef io_node ones io_blk zT".split())
        t1d, t2d, extb, qs, hnew = ([B[n + "0"], B[n + "1"]] for n in "t1d t2d extb qs hnew".split())
        x1d = [B[f"x1d{q}"] for q in range(4)]
        tn = [B[f"tn{k}"] for k in range(5)]
        oh = [[B[f"oh{b}_{k}"] for k in range(2)] for b in range(2)]
        aux, prod, cF, hp, u1, u2, u3, m_all, s_all = (B[n] for n in "aux prod cF hp u1 u2 u3 m_all s_all".split())

        ident = sb("ident", [P, P])
        below = sb("below", [P, P])
        io_lo = sb("io_lo", [P, NN], F16)
        io_hi = sb("io_hi", [P, P], F16)
        io_part = sb("io_part", [P, 1])
        zero16 = sb("zero16", [P, EC], F16)
        wqs = [sb(f"wqs{k}", [D + 1, 2 * D]) for k in range(3)]
        wkv = [sb(f"wkv{k}", [D + DE + 1, 2 * D]) for k in range(3)]
        wgc = [sb(f"wgc{k}", [D + 1, D]) for k in range(2)]
        wpair = [sb(f"wpair{k}", [P, P]) for k in range(5)]
        bias3 = [sb(f"bias3_{k}", [D + 1, HC], BF16) for k in range(5)]
        braw = [sb(f"braw{k}", [D + 1, D]) for k in range(5)]
        bsplit = [sb(f"bsplit{k}", [D + 1, D]) for k in range(2)]
        b16 = [sb(f"b16_{k}", [D + 1, D], BF16) for k in range(3)]
        ones16 = sb("ones16", [D + 1, P], BF16)
        relu_b = [sb(f"relu_b{k}", [P, D]) for k in range(2)]
        slope = sb("slope", [P, 3])
        eps_t = sb("eps_t", [P, 1])

        mask8 = [sb(f"mask8_{d}", [P, CH, SL]) for d in range(2)]
        new = [sb(f"new_{d}", [P, EC]) for d in range(2)]
        pen16 = [sb(f"pen16_{d}", [P, CH, 2, SL]) for d in range(2)]
        fmask = [sb(f"fmask_{d}", [P, CH, SL]) for d in range(2)]
        slotm = [sb(f"slotm_{d}", [P, SL]) for d in range(2)]
        cont_all = [sb(f"cont_all_{d}", [P, 1]) for d in range(2)]
        fixed = [sb(f"fixed_{d}", [P, 2]) for d in range(2)]
        inn = [sb(f"inn_{d}", [P, EC]) for d in range(2)]
        fixi = [sb(f"fixi_{d}", [P, 4], I32) for d in range(2)]
        fixo = sb("fixo", [P, 1], I32)
        norm_e = sb("norm_e", [P, EC])
        norm_r = sb("norm_r", [P, EC])
        idx_f = sb("idx_f", [P, 3, EC])

        stage_i = [sb(f"stage_i{k}", [P, EC], I32) for k in range(4)]
        gi = [sb(f"gi{k}", [P, EC], I32) for k in range(4)]
        GI = {1: 0, 2: 1, 3: 2, 4: 1}

        qi = sb("qi", [P, EC], I32)
        offs = sb("offs", [P, 2])

        tails = sb("tails", [P, 4, D])
        ft = sb("ft", [D, 4, P])
        fd = sb("fd", [D, 2, P])
        fe = sb("fe", [D, 2, P])
        fr = sb("fr", [D, 3, P + 1])
        fc = sb("fc", [D, 3, P])
        carry = sb("carry", [P, 3, D])
        fb = sb("fb", [P, FS])
        fh = sb("fh", [P, FS])
        fx1 = sb("fx1", [P, FS])
        fxd = sb("fxd", [P, D])
        fbm = sb("fbm", [P, D, SL])
        pre = sb("pre", [P, 4, D])
        fsel = sb("fsel", [P, CH, SL])
        fsc = sb("fsc", [P, 8])
        fm2 = sb("fm2", [P, D])
        fdd = sb("fdd", [P, 2, D])
        fee = sb("fee", [P, 2, D])
        fz = sb("fz", [P, 6, D])
        fT = sb("fT", [D + 1, P])
        frow = sb("frow", [P, D])
        fln = {"xc": sb("lnf_xc", [P, 1, D]), "sq": sb("lnf_sq", [P, 1, D]),
               **{k: sb(f"lnf_{k}", [P, 1]) for k in ("sum", "ss", "std", "rstd")}}

        gs = [sb(f"gs{b}", [P, T, XW]) for b in range(2)]
        gt = [g[:, :, :].rearrange("p t f -> p (t f)")[:, 0:HC] for g in gs]
        idxb = [sb(f"idxb{b}", [P, T], I32) for b in range(2)]
        oidxb = [sb(f"oidxb{b}", [P, T], I32) for b in range(2)]
        hrow = [sb(f"hrow{b}", [P, T, D]) for b in range(2)]
        hd = [sb(f"hd{b}", [P, FS]) for b in range(2)]
        maskF = [sb(f"maskF{b}", [P, FS]) for b in range(2)]
        msgF = sb("msgF", [P, FS])
        aggF = [sb(f"aggF{b}", [P, FS]) for b in range(2)]
        hdT = sb("hdT", [D + 1, T * P])
        kvin = [sb(f"kvin{b}", [D + DE + 1, T * P]) for b in range(2)]
        alpha8 = sb("alpha8", [P, 2 * SL])
        d8 = sb("d8", [P, 2, 2 * SL])
        e8 = sb("e8", [P, 2, 2 * SL])
        r8 = sb("r8", [P, 2 * SL])
        x1b = [sb(f"x1b{b}", [P, FS]) for b in range(2)]
        xin = [sb(f"xin{b}", [P, T, D]) for b in range(2)]
        od = [sb(f"od{b}", [P, T, D]) for b in range(2)]
        mask8f = [m[:, :, :].rearrange("p c s -> p (c s)") for m in mask8]

        def ln_buffers(name):
            return {"xc": B[name + "_xc"], "sq": B[name + "_sq"],
                    **{k: sb(f"{name}_{k}", [P, T]) for k in ("sum", "ss", "std", "rstd")}}

        def ln_sems(name):
            return sems(" ".join(f"{name}_{k}" for k in "sum centred squared spread std rstd out".split()))

        lnb = {k: ln_buffers(k) for k in ("lna", "lnb", "lne")}
        LS = {k: ln_sems(k) for k in ("LA", "LB", "LE")}

        ps = [ctx.enter_context(nc.psum_tensor(f"ps{k}", [P, 1024], F32)) for k in range(4)]
        psA, psB, psC, psD = ps
        bank = lambda k: ps[k // 2][:, k % 2 * 512:(k % 2 + 1) * 512]
        trz, trd = bank(0), [bank(k) for k in (1, 2, 3)]
        mmz, mmd = bank(4), [bank(k) for k in (5, 6, 7)]

        S = sems("waits_passed idx_copied oidx_copied w_loaded edges_loaded pool_consts onehots_ready onehots_used counts_done sqrt_done "
                 "totals_ready offset_done sqrt_in deg_tail degT deg_carry deg_back "
                 "idx_made consts_stored relu_made "
                 "ext_aux gc_extract gc_maskF gc_msg gc_carry gc_agg gc_z gc_zT gc_zTc gc_mm gc_relu gc_y "
                 "pairs_cleared "
                 "d_y d_tr0 d_tr1 d_tr2 d_trc0 d_trc1 d_trc2 d_mm0 d_mm1 d_mm2 d_neg0 d_neg1 d_pre0 d_pre1 d_res "
                 "t_maskF t_hp t_hpc t_hd t_trh t_hdT t_trg t_gT t_q t_kv t_qs t_prod t_alpha t_acar t_m t_d0 t_d t_e "
                 "t_scar t_s t_r0 t_r t_av t_avc t_agg t_u1 t_u2 t_u3 t_hn t_cF t_y "
                 "fx_tail fx_tailT fx_d fx_e fx_carry fx_back fx_z fx_zT fx_zTc fx_mm fx_relu fx_row fx_hT fx_hTr fx_ho "
                 "fx_gather fx_scatter "
                 "dve_order pool_order")
        ld = {k: [sem(f"{k}{b}") for b in range(2)] for k in
              "ld_hrow ld_ea ld_x1 ld_dx ld_xin gat scat st_xd st_agg st_hn st_hd st_ext st_t1 st_t2 st_od".split()}
        st_x1 = [sem(f"st_x1_{q}") for q in range(4)]

        def settle(eng):
            if eng.engine in (mybir.EngineType.SP, mybir.EngineType.Pool, mybir.EngineType.PE):
                eng.sem_inc(S["waits_passed"], 1)

        def need(eng, s, v):
            if isinstance(v, int) and v <= 0:
                return
            eng.wait_ge(s, v)
            if not isinstance(v, int):
                settle(eng)

        def pairs(eng, n, body, tail=1):
            body(0)
            with eng.Fori(1, n - tail) as i:
                body(i)
            for i in range(n - tail, n):
                body(i)

        def quads(eng, r, step):
            def body(i):
                for j in range(4):
                    step(r, i, j)
            pairs(eng, QUADS, body)

        flat = lambda t: t[:, :, :].rearrange("p t f -> p (t f)")

        def fj(t):
            return t[:, :].rearrange("p (f s) -> p s f", s=SL)[:, 1:SL, :]

        def slot(t, s):
            return t[:, :].rearrange("p (f s) -> p f s", s=SL)[:, :, s]

        def bc(ap, n):
            return ap.unsqueeze(2).broadcast_to([ap.shape[0], ap.shape[1], n])

        def mem(ap, rev):
            return ap[:, ::-1] if rev else ap

        def col0(c, rev):
            return (EC - T) - c * T if rev else c * T

        def dense_done(eng):
            for q in range(4):
                eng.wait_ge(st_x1[q], 16 * 2 * QUADS)
            for k in ("st_t1", "st_t2", "st_od"):
                for b in range(2):
                    eng.wait_ge(ld[k][b], 2 * LB)

        block = ctx.enter_context(nc.Block())
        LB = 16 * PAIRS

        @block.sync
        def _(sp):
            e2 = dst[1:1 + EPAD].rearrange("(p c) -> p c", p=P)
            sp.dma_start(stage_i[0][:, :], src.rearrange("(p c) -> p c", p=P)).then_inc(S["edges_loaded"], 16)
            sp.dma_start(stage_i[1][:, :], e2).then_inc(S["edges_loaded"], 16)
            sp.dma_start(stage_i[2][:, :], dst[0:EPAD].rearrange("(p c) -> p c", p=P)).then_inc(S["edges_loaded"], 16)
            sp.dma_start(stage_i[3][:, :], dst[2:2 + EPAD].rearrange("(p c) -> p c", p=P)).then_inc(S["edges_loaded"], 16)
            for k, (Wq, bq, Wk, bk, Wv, bv, We, Ws, bs) in enumerate(layers):
                for t, r0, c0, w in ((wqs[k], 0, 0, Wq), (wqs[k], 0, D, Ws), (wkv[k], 0, 0, Wk), (wkv[k], 0, D, Wv),
                                     (wkv[k], D, 0, We), (wkv[k], D, D, We)):
                    sp.dma_start(t[r0:r0 + w.shape[0], c0:c0 + D], w).then_inc(S["w_loaded"], 16)
                for t, r0, c0, w in ((wqs[k], D, 0, bq), (wqs[k], D, D, bs), (wkv[k], D + DE, 0, bk), (wkv[k], D + DE, D, bv)):
                    sp.dma_start(t[r0:r0 + 1, c0:c0 + D], w.unsqueeze(0)).then_inc(S["w_loaded"], 16)
            for k, (w, bb) in enumerate(((W1, b1), (W2, b2))):
                sp.dma_start(wgc[k][0:D, :], w).then_inc(S["w_loaded"], 16)
                sp.dma_start(wgc[k][D:D + 1, :], bb.unsqueeze(0)).then_inc(S["w_loaded"], 16)
                sp.dma_start(relu_b[k][:, :], bb.unsqueeze(0).broadcast_to([P, D])).then_inc(S["w_loaded"], 16)
            sp.wait_ge(S["pairs_cleared"], 1)
            for k, (w, bb) in enumerate([(l[7], l[8]) for l in layers] + [(W1, b1), (W2, b2)]):
                for o in (0, D):
                    sp.dma_start(wpair[k][o:o + D, o:o + D], w).then_inc(S["w_loaded"], 16)
                sp.dma_start(braw[k][:, :], bb.unsqueeze(0).broadcast_to([D + 1, D])).then_inc(S["w_loaded"], 16)
            sp.dma_start(slope[:, 0:1], prelu_a.unsqueeze(0).broadcast_to([P, 1])).then_inc(S["w_loaded"], 16)

            def xd_body(i):
                for b in range(2):
                    c = 2 * i + b
                    need(sp, ld["gat"][b], 16 * T * (i + 1))
                    sp.dma_start(rows(xd_rows)[:, bass.ds(c * HC, HC)], x1b[b][:, 0:HC]).then_inc(ld["st_xd"][b], 16)

            pairs(sp, PAIRS, xd_body)

            def ext_store(eng, c, er):
                b = c % 2
                eng.wait_ge(S["ext_aux"], c + 1)
                eng.wait_ge(ld["ld_dx"][b], 16 * (c // 2 + 1))
                eng.dma_start(er[:, c * XC * XW:(c + 1) * XC * XW], extb[b][:, :, :].rearrange("p c f -> p (c f)")
                              ).then_inc(ld["st_ext"][b], 16)

            xr, er = rows(x, 0, NPAD), ext.rearrange("(p c) f -> p (c f)", p=P)
            for c in range(NN // XC):
                b = c % 2
                need(sp, ld["st_ext"][b], 16 * (c // 2))
                sp.dma_start(extb[b][:, :, 0:D], xr[:, c * XC * D:(c + 1) * XC * D].rearrange("p (c f) -> p c f", f=D)
                             ).then_inc(ld["ld_dx"][b], 16)
                if c >= 1:
                    ext_store(sp, c - 1, er)
            ext_store(sp, NN // XC - 1, er)
            sp.wait_ge(S["relu_made"], 1)
            sp.dma_start(tab_h1[EPAD:EPAD + P, :], relu_b[0][:, :]).then_inc(S["consts_stored"], 16)
            for b in range(2):
                sp.wait_ge(ld["st_ext"][b], 16 * (NN // XC // 2))
            sp.wait_ge(S["consts_stored"], 16)
            for b in range(2):
                sp.wait_ge(ld["st_xd"][b], LB)

            def gc_loads(s):
                cols = bass.ds(s.g * HC, HC)
                need(sp, S["d_y"], s.n - 2)
                sp.dma_start(flat(xin[s.b]), xr[:, cols]).then_inc(ld["ld_xin"][s.b], 16)

            def gc_load_xd(s):
                if s.r == 1:
                    need(sp, S["gc_y"], s.c - 1)
                    sp.dma_start(flat(hrow[s.b]), rows(xd_rows)[:, bass.ds(col0(s.c, True) * D, HC)]
                                 ).then_inc(ld["ld_hrow"][s.b], 16)

            def dense_store(s, table, buf, ready, done):
                need(sp, ready, s.n)
                sp.dma_start(rows(table, 0, NPAD)[:, bass.ds(s.g * HC, HC)], flat(buf)).then_inc(done, 16)

            def dense_stores(r, i, j, edges_too=None):
                a, p0, p1, o = (Step(r, i, j, lag) for lag in range(4))
                if p1.dense:
                    dense_store(p1, tab[2], t2d[p1.b], S["d_pre1"], ld["st_t2"][p1.b])
                if edges_too:
                    edges_too()
                if p0.dense:
                    dense_store(p0, tab[1], t1d[p0.b], S["d_pre0"], ld["st_t1"][p0.b])
                if a.dense:
                    dense_store(a, tab[0], x1d[a.q], LS["LA"]["LA_out"], st_x1[a.q])
                if o.dense:
                    dense_store(o, out, od[o.b], LS["LB"]["LB_out"], ld["st_od"][o.b])

            def row_stores(s):
                if not s.edges:
                    return
                if s.r == 0:
                    need(sp, S["gc_relu"], s.n)
                    sp.dma_start(rows(tab_h1)[:, bass.ds(s.c * HC, HC)], flat(hnew[s.b])).then_inc(ld["st_hn"][s.b], 16)
                else:
                    need(sp, LS["LE"]["LE_out"], s.c + 1)
                    sp.dma_start(rows(tab[0], NPAD)[:, bass.ds(col0(s.c, True) * D, HC)], flat(hnew[s.b])
                                 ).then_inc(ld["st_hn"][s.b], 16)

            def gc_step(r, i, j):
                s = Step(r, i, j)
                if not (s.fixed and i == QUADS - 1 and j >= 2):
                    gc_loads(Step(r, i, j, -2))
                dense_stores(r, i, j, lambda: agg_store(s))
                row_stores(Step(r, i, j, 1 + r))
                if not (s.fixed and i == QUADS - 1 and j == 3):
                    gc_load_xd(Step(r, i, j, -1))

            def agg_store(s):
                need(sp, S["gc_agg"], s.n)
                sp.dma_start(blocks(agg_blk)[:, bass.ds(s.c * FS, FS)], aggF[s.b][:, :]).then_inc(ld["st_agg"][s.b], 16)

            def opened(r):
                sp.wait_ge(S["fx_scatter"], 16 * r)
                for b in range(2):
                    sp.wait_ge(ld["st_hn"][b], LB * r)

            for r in range(2):
                if r:
                    opened(r)
                for b in range(2):
                    gc_loads(Step(r, 0, b))
                gc_load_xd(Step(r, 0, 0))
                quads(sp, r, gc_step)
                for lag in range(1 + r, 0, -1):
                    row_stores(Step(r, QUADS, 0, lag))
            for j in range(3):
                dense_stores(2, 0, j)

            def t_load_rows(l, i, j):
                c, b = 2 * i + j, j % 2
                need(sp, S["t_hp"], l * CH + c - 1)
                sp.dma_start(flat(hrow[b]), rows(tab[l], NPAD)[:, bass.ds(col0(c, REVERSE[2 + l]) * D, HC)]
                             ).then_inc(ld["ld_hrow"][b], 16)

            def t_loads(l, i, b):
                c = 2 * i + b
                need(sp, S["t_kv"], l * CH + c - 1)
                sp.dma_start(kvin[b][D:D + DE, :], eaT[:, bass.ds(col0(c, REVERSE[2 + l]) * P, T * P)]
                             ).then_inc(ld["ld_ea"][b], 16)
                if l == 2:
                    need(sp, S["t_y"], c - 1)
                    sp.dma_start(x1b[b][:, :], blocks(hd_blk[0])[:, bass.ds(c * FS, FS)]).then_inc(ld["ld_x1"][b], 16)

            def t_store_hd(l, i, j):
                c, b = 2 * i + j, j % 2
                need(sp, S["t_hd"], l * CH + c + 1)
                sp.dma_start(blocks(hd_blk[l])[:, bass.ds(c * FS, FS)], hd[b][:, :]).then_inc(ld["st_hd"][b], 16)

            def t_stores(l, i, b):
                c = 2 * i + b
                n = l * CH + c + 1
                need(sp, S["t_agg"], n)
                sp.dma_start(blocks(agg_blk)[:, bass.ds(c * FS, FS)], aggF[b][:, :]).then_inc(ld["st_agg"][b], 16)
                if l < 2:
                    need(sp, S["t_hn"], n)
                    sp.dma_start(rows(tab[l + 1], NPAD)[:, bass.ds(col0(c, REVERSE[2 + l]) * D, HC)], flat(hnew[b])
                                 ).then_inc(ld["st_hn"][b], 16)

            for l in range(3):
                opened(2 + l)
                t_load_rows(l, 0, 0)
                t_load_rows(l, 0, 1)
                for b in range(2):
                    t_loads(l, 0, b)
                t_load_rows(l, 0, 2)
                t_store_hd(l, 0, 0)

                def t_body(i):
                    left = CH - 2 * i if isinstance(i, int) else CH
                    for b in range(2):
                        if left > b + 3:
                            t_load_rows(l, i, b + 3)
                        if left > b + 1:
                            t_store_hd(l, i, b + 1)
                        if left > b + 2:
                            t_loads(l, i + 1, b)
                        t_stores(l, i, b)

                pairs(sp, PAIRS, t_body, tail=2)
            for b in range(2):
                sp.wait_ge(ld["st_hd"][b], 3 * LB)
                sp.wait_ge(ld["st_agg"][b], 5 * LB)
                sp.wait_ge(ld["st_hn"][b], 4 * LB)
                sp.wait_ge(ld["scat"][b], T * LB)
            dense_done(sp)
            sp.wait_ge(S["fx_scatter"], 16 * 5)

        @block.gpsimd
        def _(pool):
            order = Order(pool, S["pool_order"])
            order(pool.memset(ident[:, :], 0.0))
            order(pool.affine_select(out=ident[:, :], in_=ident[:, :], compare_op=ALU.not_equal, fill=1.0, base=0,
                                     pattern=[[-1, P]], channel_multiplier=1))
            order(pool.memset(below[:, :], 1.0))
            order(pool.affine_select(out=below[:, :], in_=below[:, :], compare_op=ALU.is_ge, fill=0.0, base=-1,
                                     pattern=[[1, P]], channel_multiplier=-1))
            loose = dict(allow_small_or_imprecise_dtypes=True)
            order(pool.iota(io_lo[:, :], [[1, NN]], base=0, channel_multiplier=0, **loose))
            order(pool.iota(io_hi[:, :], [[1, P]], base=0, channel_multiplier=0, **loose))
            order(pool.iota(io_node[:, :], [[1, NN]], base=0, channel_multiplier=NN, **loose))
            order(pool.iota(io_part[:, :], [[1, 1]], base=0, channel_multiplier=1, **loose))
            order(pool.iota(io_blk[:, :, :], [[1, CH], [0, SL]], base=0, channel_multiplier=CH, **loose))
            order(pool.iota(io_row[0][:, :, :], [[T, CH], [1, SL]], base=-1, channel_multiplier=EC, **loose))
            order(pool.iota(io_row[1][:, :, :], [[-T, CH], [-1, SL]], base=EC, channel_multiplier=EC, **loose))
            for t in (hdT, fT):
                order(pool.memset(t[D:D + 1, :], 1.0))
            for b in range(2):
                order(pool.memset(kvin[b][D + DE:D + DE + 1, :], 1.0))
            order(pool.memset(ones16[:, :], 1.0))
            for k in range(5):
                order(pool.memset(bias3[k][:, :], 0.0))
                if k < 4:
                    order(pool.memset(wpair[k][:, :], 0.0))
            pool.memset(wpair[4][:, :], 0.0).then_inc(S["pairs_cleared"], 1)
            pool.memset(eps_t[:, :], EPS).then_inc(S["pool_consts"], 1)

            def copy_idx(phase, c, b, idx, before):
                need(pool, ld["gat"][b], before)
                pool.tensor_copy(idxb[b][:, :], idx[:, bass.ds(c * T, T)]).then_inc(S["idx_copied"], 1)

            def gathers(phase, i, b, idx, table, bound, to, width):
                c = 2 * i + b
                base = phase * T * LB
                need(pool, S["idx_copied"], phase * CH + c + 1)
                for t in range(T):
                    if t == T - 1 and not (isinstance(i, int) and i == PAIRS - 1 and b == 1):
                        copy_idx(phase, c + 1, 1 - b, idx, base + 16 * T * (i + b))
                    pool.indirect_dma_start(out=to(b, t)[:, 0:width], out_offset=None, in_=table,
                                            in_offset=bass.IndirectOffsetOnAxis(ap=idxb[b][:, t:t + 1], axis=0),
                                            bounds_check=bound, oob_is_err=False).then_inc(ld["gat"][b], 16)

            def opened(r):
                for b in range(2):
                    need(pool, ld["st_hn"][b], LB * min(r, 4))
                need(pool, S["fx_scatter"], 16 * r)

            def fix_gather(r, table, bound, col, to):
                pool.indirect_dma_start(out=to, out_offset=None, in_=table,
                                        in_offset=bass.IndirectOffsetOnAxis(ap=fixi[REVERSE[r]][:, col:col + 1], axis=0),
                                        bounds_check=bound, oob_is_err=False).then_inc(S["fx_gather"], 16)

            def fix(r):
                for b in range(2):
                    pool.wait_ge(ld["st_agg"][b], LB * (r + 1))
                fix_gather(r, agg_blk, P * CH - 1, 0, fb[:, :])
                if r == 1:
                    fix_gather(r, xd_rows, EPAD - 1, 1, fxd[:, :])
                if r >= 2:
                    for b in range(2):
                        pool.wait_ge(ld["st_hd"][b], LB * (r - 1))
                    fix_gather(r, hd_blk[r - 2], P * CH - 1, 0, fh[:, :])
                if r == 4:
                    fix_gather(r, hd_blk[0], P * CH - 1, 0, fx1[:, :])
                for b in range(2):
                    pool.wait_ge(ld["st_hn"][b], LB * min(r + 1, 4))
                    need(pool, ld["scat"][b], T * LB if r == 4 else 0)
                pool.wait_ge(S["fx_row"], r + 1)
                if r == 0:
                    to, bound, at = tab_h1, EPAD + P - 1, fixi[0][:, 2:3]
                elif r < 4:
                    to, bound, at = tab[r - 1], NPAD + EPAD - 1, fixi[REVERSE[r]][:, 3:4]
                else:
                    to, bound, at = out, NPAD - 1, fixo[:, 0:1]
                pool.indirect_dma_start(out=to, out_offset=bass.IndirectOffsetOnAxis(ap=at, axis=0), in_=frow[:, :],
                                        in_offset=None, bounds_check=bound, oob_is_err=False
                                        ).then_inc(S["fx_scatter"], 16)

            pool.wait_ge(S["edges_loaded"], 64)
            copy_idx(0, 0, 0, stage_i[1], 0)

            def xd_body(i):
                for b in range(2):
                    need(pool, ld["st_xd"][b], 16 * i)
                    gathers(0, i, b, stage_i[1], x, NPAD - 1, lambda b, t: x1b[b][:, t * D:(t + 1) * D], D)

            pairs(pool, PAIRS, xd_body)

            for b in range(2):
                pool.wait_ge(ld["st_ext"][b], 16 * (NN // XC // 2))
            pool.wait_ge(S["consts_stored"], 16)
            for r in range(2):
                opened(r)
                if r:
                    pool.wait_ge(S["idx_made"], 1)
                idx = stage_i[0] if r == 0 else gi[GI[r]]
                table, bound, width = (ext, NPAD - 1, XW) if r == 0 else (tab_h1, EPAD + P - 1, D)
                copy_idx(1 + r, 0, 0, idx, (1 + r) * T * LB)

                def gc_body(i):
                    for b in range(2):
                        need(pool, S["gc_msg"], r * CH + 2 * i + b - 1)
                        gathers(1 + r, i, b, idx, table, bound, lambda b, t: gs[b][:, t, :], width)

                pairs(pool, PAIRS, gc_body)
                fix(r)

            dense_done(pool)
            for l in range(3):
                r = 2 + l
                opened(r)
                idx = gi[GI[r]]
                copy_idx(1 + r, 0, 0, idx, (1 + r) * T * LB)

                def scatters(i, b):
                    c = 2 * i + b
                    need(pool, S["oidx_copied"], c + 1)
                    need(pool, LS["LE"]["LE_out"], CH + c + 1)
                    for t in range(T):
                        pool.indirect_dma_start(out=out, out_offset=bass.IndirectOffsetOnAxis(ap=oidxb[b][:, t:t + 1], axis=0),
                                                in_=hnew[b][:, t, :], in_offset=None, bounds_check=NPAD - 1,
                                                oob_is_err=False).then_inc(ld["scat"][b], 16)

                def copy_oidx(i, b):
                    need(pool, ld["scat"][b], 16 * T * i)
                    pool.tensor_copy(oidxb[b][:, :], gi[3][:, bass.ds((2 * i + b) * T, T)]).then_inc(S["oidx_copied"], 1)

                def t_body(i):
                    for b in range(2):
                        out_too = l == 2 and not (isinstance(i, int) and i == 0)
                        if out_too:
                            copy_oidx(i - 1, b)
                        need(pool, S["t_trg"], l * CH + 2 * i + b - 1)
                        gathers(1 + r, i, b, idx, tab[l], NPAD + EPAD - 1, lambda b, t: gt[b][:, t * D:(t + 1) * D], D)
                        if out_too:
                            scatters(i - 1, b)

                pairs(pool, PAIRS, t_body)
                if l == 2:
                    for b in range(2):
                        copy_oidx(PAIRS - 1, b)
                        scatters(PAIRS - 1, b)
                fix(r)
            pool.wait_ge(S["fx_scatter"], 16 * 5)

        @block.tensor
        def _(pe):
            def onehot_products(k, b, lhs, rhs, start, stop):
                for h in range(2):
                    m = pe.matmul(ps[k][:, h * 512:h * 512 + EC], lhs, rhs(h), start=start, stop=stop,
                                  skip_group_check=True)
                return m

            pe.wait_ge(S["onehots_ready"], 1)
            for k in range(2):
                onehot_products(k, 0, zero16[:, 0:P], lambda h: zero16[:, :], True, False)

            def count(i):
                for b in range(2):
                    pe.wait_ge(S["onehots_ready"], 2 + 2 * i + b)
                    for k in range(2):
                        m = onehot_products(k, b, oh[b][k][:, 0:P],
                                            lambda h, k=k, b=b: oh[b][k][:, P + h * EC:P + (h + 1) * EC], False, False)
                    m.then_inc(S["onehots_used"], 1)

            pairs(pe, EC // 2, count)
            for k in range(2):
                m = onehot_products(k, 0, zero16[:, 0:P], lambda h: zero16[:, :], False, True)
            m.then_inc(S["counts_done"], 1)
            pe.wait_ge(S["totals_ready"], 1)
            pe.matmul(psC[:, 0:1], below[:, :], offs[:, 0:1], start=True, stop=True).then_inc(S["offset_done"], 1)

            def turn(n, src3, count, dst, rows_, done):
                for k in range(count):
                    t = pe.transpose(dst[0:src3(k).shape[1], k * rows_:(k + 1) * rows_], src3(k), ident[0:rows_, 0:rows_])
                t.then_inc(done, 1)

            for d in range(2):
                pe.wait_ge(S["deg_tail"], d + 1)
                turn(d, lambda k: tails[:, 3 * k, :], 2, psC, P, S["degT"])
                pe.wait_ge(S["deg_carry"], d + 1)
                pe.transpose(psC[:, 0:D], fc[:, 0, :], ident[0:D, 0:D]).then_inc(S["deg_back"], 1)

            pe.wait_ge(S["w_loaded"], W_LOADED)

            def fix(r):
                t_round = r >= 2
                n = r + 1
                ks = range(4) if t_round else (0, 3)
                pe.wait_ge(S["fx_tail"], n)
                for k in ks:
                    t = pe.transpose(psA[0:D, k * P:(k + 1) * P], tails[:, k, :], ident[:, :])
                t.then_inc(S["fx_tailT"], 1)
                pe.wait_ge(S["fx_carry"], n)
                for k in range(3 if t_round else 1):
                    t = pe.transpose(psA[:, k * D:(k + 1) * D], fc[:, k, :], ident[0:D, 0:D])
                t.then_inc(S["fx_back"], 1)
                pe.wait_ge(S["fx_z"], n)
                pe.transpose(psB[0:D, 0:P], fz[:, 0, :], ident[:, :]).then_inc(S["fx_zT"], 1)
                pe.wait_ge(S["fx_zTc"], n)
                w = wqs[r - 2] if t_round else wgc[r]
                pe.matmul(psC[:, 0:w.shape[1]], fT[:, :], w[:, :], start=True, stop=True).then_inc(S["fx_mm"], 1)
                if 1 <= r <= 3:
                    pe.wait_ge(S["fx_hT"], r)
                    for k in range(2):
                        t = pe.transpose(psA[0:D, k * P:(k + 1) * P], tails[:, k, :], ident[:, :])
                    t.then_inc(S["fx_hTr"], 1)
                    pe.wait_ge(S["fx_ho"], r)
                    pe.transpose(psB[:, 0:D], fc[:, 0, :], ident[0:D, 0:D]).then_inc(S["fx_hTr"], 1)

            def products(to, width, lhs, w, done):
                for t in range(T):
                    m = pe.matmul(to[:, t * width:(t + 1) * width], lhs(t), w, start=True, stop=True)
                m.then_inc(done, 1)

            def pair_transposes(to, tiles, done):
                settle(pe)
                for t in range(0, T, 2):
                    w = min(2, T - t)
                    m = pe.transpose(to[0:w * D, t // 2 * P:(t // 2 + 1) * P], tiles(t, w), ident[:, :])
                m.then_inc(done, 1)

            def pair_products(to, lhs, k, done):
                pe.matmul(to[:, 0:HC], ones16[:, :], bias3[k][:, :], start=True, stop=False, skip_group_check=True)
                for t in range(0, T, 2):
                    w = min(2, T - t) * D
                    m = pe.matmul(to[:, t * D:t * D + w], lhs[0:w, t // 2 * P:(t // 2 + 1) * P], wpair[k][0:w, 0:w],
                                  start=False, stop=t + 2 >= T, skip_group_check=True)
                m.then_inc(done, 1)

            def turn_dense(s, k, src_t, ready):
                if s.dense:
                    pe.wait_ge(ready, s.n)
                    need(pe, S[f"d_trc{k}"], s.n - 1)
                    pair_transposes(trd[k], lambda t, w: src_t[:, t:t + w, :].rearrange("p t f -> p (t f)"), S[f"d_tr{k}"])

            def multiply_dense(s, k, read):
                if s.dense:
                    pe.wait_ge(S[f"d_trc{k}"], s.n)
                    need(pe, read, s.n - 1)
                    pair_products(mmd[k], nT[k], k, S[f"d_mm{k}"])

            def gc_step(r, i, j, edges=True):
                s, p0, p1 = (Step(r, i, j, lag) for lag in range(3))
                turn_dense(p1, 2, t2d[p1.b], S["d_pre1"])
                turn_dense(p0, 1, t1d[p0.b], S["d_pre0"])
                turn_dense(s, 0, x1d[s.q], LS["LA"]["LA_out"])
                multiply_dense(p1, 2, S["d_res"])
                if edges:
                    pe.wait_ge(S["gc_z"], s.n)
                    need(pe, S["gc_zTc"], s.n - 1)
                    pair_transposes(trz, lambda t, w: u1[:, t:t + w, :].rearrange("p t f -> p (t f)"), S["gc_zT"])
                multiply_dense(p0, 1, S["d_pre1"])
                multiply_dense(s, 0, S["d_pre0"])
                if edges:
                    pe.wait_ge(S["gc_zTc"], s.n)
                    need(pe, S["gc_relu"], s.n - 1)
                    pair_products(mmz, zT, 3 + r, S["gc_mm"])

            for r in range(2):
                quads(pe, r, gc_step)
                if r == 1:
                    for j in range(3):
                        gc_step(2, 0, j, edges=False)
                fix(r)

            def t_turn(l, i, b):
                n = l * CH + 2 * i + b + 1
                pe.wait_ge(S["t_hd"], n)
                need(pe, S["t_hdT"], n - 1)
                settle(pe)
                for t in range(T):
                    m = pe.transpose(psB[0:D, t * P:(t + 1) * P], slot(hd[b], t + 1), ident[:, :])
                m.then_inc(S["t_trh"], 1)
                pe.wait_ge(ld["gat"][b], (3 + l) * T * LB + 16 * T * (i + 1))
                need(pe, S["t_gT"], n - 1)
                pair_transposes(psA, lambda t, w: gt[b][:, t * D:(t + w) * D], S["t_trg"])
                pe.wait_ge(S["t_hdT"], n)
                need(pe, S["t_qs"], n - 1)
                products(psD, 2 * D, lambda t: hdT[:, t * P:(t + 1) * P], wqs[l][:, :], S["t_q"])

            for l in range(3):
                t_turn(l, 0, 0)

                def t_body(i):
                    for b in range(2):
                        n = l * CH + 2 * i + b + 1
                        pe.wait_ge(S["t_gT"], n)
                        pe.wait_ge(ld["ld_ea"][b], l * LB + 16 * (i + 1))
                        need(pe, S["t_av"], n - 1)
                        at = (lambda t: T - 1 - t) if REVERSE[2 + l] else (lambda t: t)
                        products(psC, 2 * D, lambda t: kvin[b][:, at(t) * P:(at(t) + 1) * P], wkv[l][:, :], S["t_kv"])
                        if not (isinstance(i, int) and i == PAIRS - 1 and b):
                            t_turn(l, i + b, 1 - b)

                pairs(pe, PAIRS, t_body)
                fix(2 + l)

        @block.scalar
        def _(act):
            def ln_square(L, n, w, B):
                act.wait_ge(L[B + "_centred"], n)
                act.activation(w["sq"][:, :, :], w["xc"][:, :, :], ACT.Square).then_inc(L[B + "_squared"], 1)

            def ln_std(L, n, w, B):
                act.wait_ge(L[B + "_spread"], n)
                act.activation(w["std"][:, :], w["ss"][:, :], ACT.Sqrt, scale=1.0 / D, bias=eps_t[:, 0:1]
                               ).then_inc(L[B + "_std"], 1)

            act.wait_ge(S["sqrt_in"], 1)
            act.activation(tn[0][:, :], tn[0][:, :], ACT.Sqrt).then_inc(S["sqrt_done"], 1)
            for d in range(2):
                act.wait_ge(S["sqrt_in"], d + 2)
                act.activation(te[1][:, :], te[0][:, :], ACT.Sqrt).then_inc(S["sqrt_done"], 1)

            def fill_mask(c, b, d, done):
                act.copy(maskF[b][:, :].rearrange("p (f s) -> p f s", s=SL),
                         mask8f[d][:, bass.ds(c * SL, SL)].unsqueeze(1).broadcast_to([P, D, SL])).then_inc(done, 1)

            def fix(r):
                t_round = r >= 2
                n = r + 1
                if t_round:
                    act.wait_ge(S["fx_d"], 2 * (r - 1) - 1)
                    act.activation(fe[:, :, :], fd[:, :, :], ACT.Exp).then_inc(S["fx_e"], 1)
                    act.wait_ge(S["fx_d"], 2 * (r - 1))
                    act.activation(fee[:, :, :], fdd[:, :, :], ACT.Exp).then_inc(S["fx_e"], 1)
                act.wait_ge(S["fx_zT"], n)
                act.copy(fT[0:D, :], psB[0:D, 0:P]).then_inc(S["fx_zTc"], 1)
                if not t_round:
                    act.wait_ge(S["fx_mm"], n)
                    act.activation(fz[:, 1, :], psC[:, 0:D], ACT.Relu).then_inc(S["fx_relu"], 1)
                if r in (1, 4):
                    k = 2 * CH + (1 if r == 1 else 2)
                    ln_square(LS["LA"], k, fln, "LA")
                    ln_std(LS["LA"], k, fln, "LA")

            def dense_neg(s, k):
                if s.dense:
                    act.wait_ge(S[f"d_mm{k}"], s.n)
                    need(act, S[f"d_pre{k}"], s.n - 1)
                    act.activation(flat(neg[k]), mmd[k][:, 0:HC], ACT.Relu, scale=-1.0).then_inc(S[f"d_neg{k}"], 1)

            def dense_turned(s, k):
                if s.dense:
                    act.wait_ge(S[f"d_tr{k}"], s.n)
                    need(act, S[f"d_mm{k}"], s.n - 1)
                    copy_pairs(nT[k], trd[k], S[f"d_trc{k}"])

            def copy_pairs(to, of, done):
                act.copy(to[:, 0:3 * P], of[:, 0:3 * P])
                act.copy(to[0:D, 3 * P:4 * P], of[0:D, 3 * P:4 * P]).then_inc(done, 1)

            def gc_relu(e):
                if not e.edges:
                    return
                act.wait_ge(S["gc_mm"], e.n)
                if e.r == 0:
                    need(act, ld["st_hn"][e.b], 16 * e.h)
                    act.activation(flat(hnew[e.b]), mmz[:, 0:HC], ACT.Relu).then_inc(S["gc_relu"], 1)
                else:
                    need(act, S["gc_y"], e.c)
                    act.activation(flat(u2), mmz[:, 0:HC], ACT.Relu).then_inc(S["gc_relu"], 1)

            def row_square(e):
                if e.r == 1 and e.edges:
                    ln_square(LS["LE"], e.c + 1, lnb["lne"], "LE")

            def row_std(e):
                if e.r == 1 and e.edges:
                    ln_std(LS["LE"], e.c + 1, lnb["lne"], "LE")

            def gc_step(r, i, j, edges=True):
                s, p0, p1, o = (Step(r, i, j, lag) for lag in range(4))
                e, e2 = p0, p1
                if o.dense:
                    ln_square(LS["LB"], o.n, lnb["lnb"], "LB")
                if s.dense:
                    ln_square(LS["LA"], s.n, lnb["lna"], "LA")
                dense_neg(p1, 1)
                dense_neg(p0, 0)
                if edges:
                    need(act, S["gc_agg"], s.n - 2)
                    fill_mask(s.c, s.b, int(REVERSE[r]), S["gc_maskF"])
                if o.dense:
                    ln_std(LS["LB"], o.n, lnb["lnb"], "LB")
                if s.dense:
                    ln_std(LS["LA"], s.n, lnb["lna"], "LA")
                row_std(e2)
                if edges:
                    gc_relu(e)
                dense_turned(p1, 2)
                dense_turned(p0, 1)
                dense_turned(s, 0)
                if edges:
                    act.wait_ge(S["gc_zT"], s.n)
                    need(act, S["gc_mm"], s.n - 1)
                    copy_pairs(zT, trz, S["gc_zTc"])
                    row_square(e)

            for r in range(2):
                quads(act, r, gc_step)
                e, e2 = Step(r, QUADS, 0, 1), Step(r, QUADS, 0, 2)
                gc_relu(e)
                row_std(e2)
                row_square(e)
                row_std(e)
                if r == 1:
                    for j in range(3):
                        gc_step(2, 0, j, edges=False)
                fix(r)

            def t_mask(l, c, b, n):
                need(act, S["t_hd"], n - 2)
                fill_mask(c, b, int(REVERSE[2 + l]), S["t_maskF"])

            tiles = lambda ap: ap.rearrange("p (t e) -> p t e", e=P)

            def unpair(to, of, done):
                act.copy(to[:, 0:T:2, :], tiles(of[0:D, 0:4 * P]))
                act.copy(to[:, 1:T:2, :], tiles(of[D:2 * D, 0:3 * P])).then_inc(done, 1)

            def t_hdT(n, b):
                act.wait_ge(S["t_trh"], n)
                need(act, S["t_q"], n - 1)
                act.copy(hdT[0:D, :], psB[0:D, 0:T * P]).then_inc(S["t_hdT"], 1)

            def t_gT(l, n, b):
                act.wait_ge(S["t_trg"], n)
                need(act, S["t_kv"], n - 2)
                unpair(mem(tiles(kvin[b][0:D, :]), REVERSE[2 + l]), psA, S["t_gT"])

            def t_qs(n, b):
                act.wait_ge(S["t_q"], n)
                need(act, S["t_u2"], n - 2)
                act.copy(qs[b][:, :, :].rearrange("p t f -> p (t f)"), psD[:, 0:T * 2 * D]).then_inc(S["t_qs"], 1)

            for l in range(3):
                H = HEADS[l]
                for c in range(2):
                    t_mask(l, c, c, l * CH + c + 1)
                t_hdT(l * CH + 1, 0)
                t_gT(l, l * CH + 1, 0)
                t_qs(l * CH + 1, 0)
                t_mask(l, 2, 0, l * CH + 3)

                def t_body(i):
                    for b in range(2):
                        c = 2 * i + b
                        n = l * CH + c + 1
                        left = CH - c if isinstance(i, int) else CH
                        if left > 1:
                            t_hdT(n + 1, 1 - b)
                            t_gT(l, n + 1, 1 - b)
                        if l == 2 and not (isinstance(i, int) and c == 0):
                            ln_std(LS["LE"], CH + c, lnb["lne"], "LE")
                        act.wait_ge(S["t_d"], n)
                        act.activation(e8[:, :, 0:H * SL], d8[:, :, 0:H * SL], ACT.Exp).then_inc(S["t_e"], 1)
                        need(act, S["t_agg"], n - 1)
                        act.wait_ge(S["t_e"], n)
                        act.copy(cF[:, :].rearrange("p (h c s) -> p h c s", h=H, s=SL),
                                 e8[:, 0, 0:H * SL].rearrange("p (h s) -> p h s", h=H).unsqueeze(2)
                                 .broadcast_to([P, H, D // H, SL])).then_inc(S["t_cF"], 1)
                        if left > 1:
                            t_qs(n + 1, 1 - b)
                        if left > 3:
                            t_mask(l, c + 3, 1 - b, n + 3)
                        if l == 2:
                            ln_square(LS["LE"], CH + c + 1, lnb["lne"], "LE")

                pairs(act, PAIRS, t_body, tail=2)
                if l == 2:
                    ln_std(LS["LE"], 2 * CH, lnb["lne"], "LE")
                fix(2 + l)

        @block.vector
        def _(v):
            order = Order(v, S["dve_order"])

            def ln_sum(L, n, w, B, y):
                v.tensor_reduce(w["sum"][:, :], y, AX, ALU.add).then_inc(L[B + "_sum"], 1)

            def ln_subtract(L, n, w, B, y):
                v.wait_ge(L[B + "_sum"], n)
                v.scalar_tensor_tensor(out=w["xc"][:, :, :], in0=bc(w["sum"][:, :], D), scalar=-1.0 / D, in1=y,
                                       op0=ALU.mult, op1=ALU.add).then_inc(L[B + "_centred"], 1)

            def ln_centre(L, n, w, B, y):
                ln_sum(L, n, w, B, y)
                ln_subtract(L, n, w, B, y)

            def ln_spread(L, n, w, B):
                v.wait_ge(L[B + "_squared"], n)
                v.tensor_reduce(w["ss"][:, :], w["sq"][:, :, :], AX, ALU.add).then_inc(L[B + "_spread"], 1)

            def ln_scale(L, n, w, B, to):
                v.wait_ge(L[B + "_std"], n)
                v.reciprocal(w["rstd"][:, :], w["std"][:, :]).then_inc(L[B + "_rstd"], 1)
                v.wait_ge(L[B + "_rstd"], n)
                v.tensor_tensor(to, w["xc"][:, :, :], bc(w["rstd"][:, :], D), ALU.mult).then_inc(L[B + "_out"], 1)

            v.wait_ge(S["edges_loaded"], 64)
            v.wait_ge(S["pool_consts"], 1)
            for k in range(4):
                order(v.tensor_copy(ef[:, k, :], stage_i[k][:, :]))
            for k in range(2):
                hi, lo = hl[k][0][:, :], hl[k][1][:, :]
                e, q, t = ef[:, k, :], te[0][:, :], te[1][:, :]
                order(v.tensor_scalar(q, e, 1.0 / NN, None, ALU.mult))
                order(v.tensor_copy(qi[:, :], q))
                order(v.tensor_copy(hi, qi[:, :]))
                order(v.scalar_tensor_tensor(out=lo, in0=hi, scalar=-float(NN), in1=e, op0=ALU.mult, op1=ALU.add))
                for op, sign in ((ALU.is_lt, 1.0), (ALU.is_ge, -1.0)):
                    order(v.tensor_scalar(t, lo, 0.0 if sign > 0 else float(NN), None, op))
                    order(v.scalar_tensor_tensor(out=hi, in0=t, scalar=-sign, in1=hi, op0=ALU.mult, op1=ALU.add))
                    order(v.scalar_tensor_tensor(out=lo, in0=t, scalar=sign * NN, in1=lo, op0=ALU.mult, op1=ALU.add))
            v.memset(zero16[:, :], 0.0).then_inc(S["onehots_ready"], 1)

            def onehots(i):
                for b in range(2):
                    j = 2 * i + b
                    need(v, S["onehots_used"], j - 1)
                    for k in range(2):
                        v.tensor_scalar(oh[b][k][:, P:P + NN], io_lo[:, :], hl[k][1][:, bass.ds(j, 1)], None, ALU.is_equal)
                        m = v.tensor_scalar(oh[b][k][:, 0:P], io_hi[:, :], hl[k][0][:, bass.ds(j, 1)], None, ALU.is_equal)
                    m.then_inc(S["onehots_ready"], 1)

            pairs(v, EC // 2, onehots)

            counts = [ps[k][:, :].rearrange("p (h w) -> p h w", h=2)[:, :, 0:EC] for k in range(2)]
            two = lambda t: t[:, :].rearrange("p (h w) -> p h w", h=2)
            root, indeg, has, cum, first = tn
            v.wait_ge(S["counts_done"], 1)
            v.tensor_scalar(two(root), counts[0], 1.0, None, ALU.max).then_inc(S["sqrt_in"], 1)
            order(v.tensor_copy(two(indeg), counts[1]))
            order(v.memset(ones[:, :], 1.0))
            order(v.tensor_tensor_scan(cum[:, :], ones[:, :], indeg[:, :], 0.0, ALU.mult, ALU.add))
            v.tensor_copy(offs[:, 0:1], cum[:, NN - 1:NN]).then_inc(S["totals_ready"], 1)
            order(v.tensor_scalar(has[:, :], indeg[:, :], 0.5, None, ALU.is_ge))
            v.wait_ge(S["sqrt_done"], 1)
            order(v.reciprocal(aux[:, :, 0], root[:, :]))
            v.wait_ge(S["offset_done"], 1)
            order(v.tensor_copy(offs[:, 1:2], psC[:, 0:1]))
            order(v.tensor_scalar(cum[:, :], cum[:, :], offs[:, 1:2], -1.0, ALU.add, ALU.add))
            order(v.scalar_tensor_tensor(out=first[:, :], in0=cum[:, :], scalar=1.0, in1=indeg[:, :], op0=ALU.add, op1=ALU.subtract))
            order(v.tensor_scalar(offs[:, 0:1], io_part[:, :], float(EPAD), None, ALU.add))
            order(v.tensor_scalar(root[:, :], cum[:, :], offs[:, 0:1], None, ALU.subtract))
            order(v.tensor_tensor(root[:, :], root[:, :], has[:, :], ALU.mult))
            order(v.tensor_scalar(aux[:, :, 1], root[:, :], offs[:, 0:1], None, ALU.add))
            for k, pos in ((2, cum), (3, first)):
                order(v.scalar_tensor_tensor(out=root[:, :], in0=pos[:, :], scalar=float(NPAD), in1=io_node[:, :],
                                             op0=ALU.add, op1=ALU.subtract))
                order(v.tensor_tensor(root[:, :], root[:, :], has[:, :], ALU.mult))
                order(v.tensor_tensor(aux[:, :, k], root[:, :], io_node[:, :], ALU.add))
            for c in range(NN // XC):
                b = c % 2
                need(v, ld["st_ext"][b], 16 * (c // 2))
                v.tensor_copy(extb[b][:, :, D:XW], aux[:, c * XC:(c + 1) * XC, :]).then_inc(S["ext_aux"], 1)

            v.wait_ge(S["w_loaded"], W_LOADED)
            for l in range(3):
                order(v.tensor_scalar(wqs[l][:, 0:D], wqs[l][:, 0:D], float((D // HEADS[l]) ** -0.5), None, ALU.mult))
            for k in range(5):
                rest = braw[k]
                for p in range(3):
                    order(v.tensor_copy(b16[p][:, :], rest[:, :]))
                    if p < 2:
                        order(v.tensor_tensor(bsplit[p][:, :], rest[:, :], b16[p][:, :], ALU.subtract))
                        rest = bsplit[p]
                    at = 32 * p
                    order(v.tensor_copy(bias3[k][at:at + 1, :].rearrange("p (t f) -> p t f", f=D),
                                        b16[p][at:at + 1, :].unsqueeze(1).broadcast_to([1, T, D])))
            order(v.tensor_scalar(slope[:, 1:2], slope[:, 0:1], -1.0, None, ALU.add))
            order(v.tensor_scalar(slope[:, 2:3], slope[:, 0:1], -1.0, 1.0, ALU.mult, ALU.add))
            order(v.tensor_scalar(relu_b[1][:, :], relu_b[1][:, :], 0.0, None, ALU.max))
            v.tensor_scalar(relu_b[0][:, :], relu_b[0][:, :], 0.0, None, ALU.max).then_inc(S["relu_made"], 1)

            order(v.memset(m_all[:, :, :], 0.0))
            order(v.memset(s_all[:, :, :], 0.0))
            order(v.memset(fr[:, :, :], 0.0))
            order(v.tensor_tensor(hl[0][0][:, :], ef[:, 1, :], ef[:, 2, :], ALU.is_equal))
            order(v.tensor_tensor(hl[0][1][:, :], ef[:, 1, :], ef[:, 3, :], ALU.is_equal))
            go, end, lead = hl[1][0], hl[1][1], te[2]
            chunks = lambda t: t[:, :].rearrange("p (c t) -> p c t", t=T)
            flat8 = lambda t: t[:, :, :].rearrange("p c s -> p (c s)")

            def total(to, in0, in1):
                order(v.tensor_tensor(fsel[:, :, :], in0, in1, ALU.mult))
                order(v.tensor_reduce(to, flat8(fsel), AX, ALU.add))

            def carry_over(d, k):
                order(v.tensor_tensor_scan(fr[:, k, 1:P + 1], ft[:, 3, :], ft[:, k, :], 0.0, ALU.mult, ALU.add))

            for d in range(2):
                order(v.tensor_copy(go[:, :], mem(hl[0][d][:, :], d)))
                order(v.tensor_scalar(end[:, :], mem(hl[0][1 - d][:, :], d), -1.0, 1.0, ALU.mult, ALU.add))
                order(v.tensor_scalar(new[d][:, :], go[:, :], -1.0, 1.0, ALU.mult, ALU.add))
                order(v.memset(mask8[d][:, :, :], 0.0))
                order(v.tensor_copy(mask8[d][:, :, 1:SL], chunks(go)))
                order(v.memset(pen16[d][:, :, :, :], -BIG))
                for h in range(2):
                    order(v.tensor_scalar(pen16[d][:, :, h, 1:SL], chunks(new[d]), -BIG, None, ALU.mult))
                order(v.memset(te[0][:, :], 0.0))
                order(v.tensor_tensor_scan(lead[:, :], go[:, :], te[0][:, :], 1.0, ALU.mult, ALU.add))
                order(v.tensor_copy(cont_all[d][:, :], lead[:, EC - 1:EC]))
                order(v.memset(fmask[d][:, :, :], 0.0))
                order(v.tensor_tensor(fmask[d][:, :, 1:SL], chunks(lead), chunks(end), ALU.mult))
                order(v.tensor_reduce(fixed[d][:, 0:1], flat8(fmask[d]), AX, ALU.add))
                order(v.tensor_scalar(fixed[d][:, 1:2], fixed[d][:, 0:1], -1.0, 1.0, ALU.mult, ALU.add))
                order(v.tensor_reduce(slotm[d][:, :], fmask[d][:, :, :].rearrange("p c s -> p s c"), AX, ALU.add))
                total(fsc[:, 0:1], fmask[d][:, :, :], io_blk[:, :, :])
                total(fsc[:, 1:2], fmask[d][:, :, :], io_row[d][:, :, :])
                order(v.scalar_tensor_tensor(out=fsc[:, 2:3], in0=fixed[d][:, 1:2], scalar=float(EPAD + P), in1=fsc[:, 1:2],
                                             op0=ALU.mult, op1=ALU.add))
                order(v.scalar_tensor_tensor(out=fsc[:, 3:4], in0=fixed[d][:, 1:2], scalar=float(EPAD), in1=fsc[:, 1:2],
                                             op0=ALU.mult, op1=ALU.add))
                order(v.tensor_scalar(fsc[:, 3:4], fsc[:, 3:4], float(NPAD), None, ALU.add))
                order(v.tensor_copy(fixi[d][:, :], fsc[:, 0:4]))
                if d == 0:
                    order(v.tensor_tensor(fsel[:, :, 1:SL], fmask[0][:, :, 1:SL], ef[:, 1, :].rearrange("p (c t) -> p c t", t=T), ALU.mult))
                    order(v.memset(fsel[:, :, 0:1], 0.0))
                    order(v.tensor_reduce(fsc[:, 0:1], flat8(fsel), AX, ALU.add))
                    order(v.scalar_tensor_tensor(out=fsc[:, 0:1], in0=fixed[0][:, 1:2], scalar=float(NPAD), in1=fsc[:, 0:1],
                                                 op0=ALU.mult, op1=ALU.add))
                    order(v.tensor_copy(fixo[:, :], fsc[:, 0:1]))
                order(v.tensor_tensor_scan(te[0][:, :], go[:, :], ones[:, 0:EC], 0.0, ALU.mult, ALU.add))
                order(v.tensor_copy(tails[:, 0, :], te[0][:, EC - 1:EC].broadcast_to([P, D])))
                v.tensor_copy(tails[:, 3, :], cont_all[d][:, :].broadcast_to([P, D])).then_inc(S["deg_tail"], 1)
                v.wait_ge(S["degT"], d + 1)
                order(v.tensor_copy(ft[:, 0, :], mem(psC[0:D, 0:P], d)))
                order(v.tensor_copy(ft[:, 3, :], mem(psC[0:D, P:2 * P], d)))
                carry_over(d, 0)
                v.tensor_copy(fc[:, 0, :], mem(fr[:, 0, 0:P], d)).then_inc(S["deg_carry"], 1)
                v.wait_ge(S["deg_back"], d + 1)
                order(v.tensor_copy(carry[:, 0, :], psC[:, 0:D]))
                v.tensor_tensor_scan(te[0][:, :], go[:, :], ones[:, 0:EC], carry[:, 0, 0:1], ALU.mult, ALU.add
                                     ).then_inc(S["sqrt_in"], 1)
                v.wait_ge(S["sqrt_done"], d + 2)
                order(v.reciprocal(inn[d][:, :], te[1][:, :]))
            order(v.scalar_tensor_tensor(out=te[0][:, :], in0=hl[0][1][:, :], scalar=float(NPAD), in1=ef[:, 1, :],
                                         op0=ALU.mult, op1=ALU.add))
            order(v.tensor_copy(gi[3][:, :], te[0][:, :]))
            order(v.memset(d8[:, 0, :], -BIG))
            order(v.memset(d8[:, 1, :], 0.0))

            GATHERED = (1, 3, 5, 7, 10)

            def pick(to, blk, d, done=None):
                order(v.tensor_tensor(fbm[:, :, :], blk[:, :].rearrange("p (f s) -> p f s", s=SL),
                                      slotm[d][:, :].unsqueeze(1).broadcast_to([P, D, SL]), ALU.mult))
                m = v.tensor_reduce(to, fbm[:, :, :], AX, ALU.add)
                m.then_inc(done, 1) if done else order(m)

            def fix(r):
                d = int(REVERSE[r])
                n = r + 1
                t_round = r >= 2
                l = r - 2
                H = HEADS[l] if t_round else 1
                heads = lambda ap: bc(ap, D // H)
                hc = lambda ap: ap.rearrange("p (h c) -> p h c", h=H)
                last = lambda t: t[:, CH, 0:H * SL].rearrange("p (h s) -> p h s", s=SL)[:, :, SL - 1]
                if t_round:
                    v.wait_ge(S["t_agg"], CH * (l + 1))
                    v.wait_ge(S["t_s"], CH * (l + 1))
                    order(v.tensor_copy(hc(tails[:, 1, :]), heads(last(s_all))))
                    order(v.tensor_copy(hc(tails[:, 2, :]), heads(last(m_all))))
                else:
                    v.wait_ge(S["gc_agg"], CH * (r + 1))
                order(v.tensor_copy(tails[:, 0, :], slot(aggF[1], SL - 1)))
                v.tensor_copy(tails[:, 3, :], cont_all[d][:, :].broadcast_to([P, D])).then_inc(S["fx_tail"], 1)
                v.wait_ge(S["fx_tailT"], n)
                for k in (range(4) if t_round else (0, 3)):
                    order(v.tensor_copy(ft[:, k, :], mem(psA[0:D, k * P:(k + 1) * P], d)))
                if t_round:
                    M, Mprev = fr[:, 2, 1:P + 1], fr[:, 2, 0:P]
                    order(v.tensor_scalar(fd[:, 0, :], ft[:, 3, :], BIG, -BIG, ALU.mult, ALU.add))
                    order(v.tensor_tensor_scan(M, fd[:, 0, :], ft[:, 2, :], 0.0, ALU.add, ALU.max))
                    order(v.tensor_tensor(fd[:, 1, :], Mprev, M, ALU.subtract))
                    order(v.tensor_tensor(fd[:, 0, :], fd[:, 0, :], fd[:, 1, :], ALU.add))
                    v.tensor_tensor(fd[:, 1, :], ft[:, 2, :], M, ALU.subtract).then_inc(S["fx_d"], 1)
                    v.wait_ge(S["fx_e"], 2 * l + 1)
                    for k in range(2):
                        order(v.tensor_tensor(ft[:, k, :], ft[:, k, :], fe[:, 1, :], ALU.mult))
                        order(v.tensor_tensor_scan(fr[:, k, 1:P + 1], fe[:, 0, :], ft[:, k, :], 0.0, ALU.mult, ALU.add))
                    v.tensor_copy(fc[:, :, :], fr[:, :, 0:P][:, :, ::-1] if d else fr[:, :, 0:P]).then_inc(S["fx_carry"], 1)
                else:
                    carry_over(d, 0)
                    v.tensor_copy(fc[:, 0, :], mem(fr[:, 0, 0:P], d)).then_inc(S["fx_carry"], 1)
                v.wait_ge(S["fx_back"], n)
                nk = 3 if t_round else 1
                order(v.tensor_copy(carry[:, 0:nk, :], psA[:, 0:nk * D].rearrange("p (k f) -> p k f", f=D)))
                v.wait_ge(S["fx_gather"], 16 * GATHERED[r])
                pick(pre[:, 0, :], fb, d)
                if not t_round:
                    order(v.memset(fsel[:, :, 0:1], 0.0))
                    order(v.tensor_tensor(fsel[:, :, 1:SL], fmask[d][:, :, 1:SL], chunks(inn[d]), ALU.mult))
                    order(v.tensor_reduce(fsc[:, 0:1], flat8(fsel), AX, ALU.add))
                    order(v.tensor_tensor(fz[:, 2, :], carry[:, 0, :], pre[:, 0, :], ALU.add))
                    v.tensor_scalar(fz[:, 0, :], fz[:, 2, :], fsc[:, 0:1], None, ALU.mult).then_inc(S["fx_z"], 1)
                    v.wait_ge(S["fx_relu"], n)
                    need(v, S["fx_scatter"], 16 * r)
                    if r == 0:
                        v.tensor_copy(frow[:, :], fz[:, 1, :]).then_inc(S["fx_row"], 1)
                        v.wait_ge(S["fx_row"], 1)
                        return
                    order(v.tensor_tensor(fz[:, 2, :], fz[:, 1, :], fxd[:, :], ALU.add))
                    y = fz[:, 2:3, :]
                else:
                    pick(fz[:, 0, :], fh, d, S["fx_z"])
                    for k, t in ((1, s_all), (2, m_all)):
                        for h in range(H):
                            total(fsc[:, h:h + 1], fmask[d][:, :, :], t[:, 1:CH + 1, h * SL:(h + 1) * SL])
                        order(v.tensor_copy(hc(pre[:, k, :]), heads(fsc[:, 0:H])))
                    order(v.tensor_tensor(fm2[:, :], carry[:, 2, :], pre[:, 2, :], ALU.max))
                    order(v.tensor_tensor(fdd[:, 0, :], carry[:, 2, :], fm2[:, :], ALU.subtract))
                    v.tensor_tensor(fdd[:, 1, :], pre[:, 2, :], fm2[:, :], ALU.subtract).then_inc(S["fx_d"], 1)
                    v.wait_ge(S["fx_e"], 2 * l + 2)
                    for k in range(2):
                        order(v.tensor_tensor(fz[:, 1 + k, :], carry[:, k, :], fee[:, 0, :], ALU.mult))
                        order(v.tensor_tensor(fz[:, 3, :], pre[:, k, :], fee[:, 1, :], ALU.mult))
                        order(v.tensor_tensor(fz[:, 1 + k, :], fz[:, 1 + k, :], fz[:, 3, :], ALU.add))
                    order(v.tensor_scalar(fz[:, 2, :], fz[:, 2, :], 1e-16, None, ALU.add))
                    order(v.reciprocal(fz[:, 2, :], fz[:, 2, :]))
                    order(v.tensor_tensor(fz[:, 1, :], fz[:, 1, :], fz[:, 2, :], ALU.mult))
                    v.wait_ge(S["fx_mm"], n)
                    order(v.tensor_tensor(fz[:, 1, :], fz[:, 1, :], psC[:, D:2 * D], ALU.add))
                    need(v, S["fx_scatter"], 16 * r)
                    if l < 2:
                        order(v.tensor_scalar(fz[:, 2, :], fz[:, 1, :], 0.0, slope[:, 1:2], ALU.min, ALU.mult))
                        v.tensor_tensor(frow[:, :], fz[:, 2, :], fz[:, 1, :], ALU.add).then_inc(S["fx_row"], 1)
                        v.wait_ge(S["fx_row"], n)
                    else:
                        pick(fz[:, 3, :], fx1, d)
                        order(v.tensor_tensor(fz[:, 1, :], fz[:, 1, :], fz[:, 3, :], ALU.add))
                        y = fz[:, 1:2, :]
                if r in (1, 4):
                    k = 2 * CH + (1 if r == 1 else 2)
                    L = LS["LA"]
                    ln_centre(L, k, fln, "LA", y)
                    ln_spread(L, k, fln, "LA")
                    ln_scale(L, k, fln, "LA", fz[:, 4:5, :])
                    v.wait_ge(L["LA_out"], k)
                    v.tensor_copy(frow[:, :], fz[:, 4, :]).then_inc(S["fx_row"], 1)
                    v.wait_ge(S["fx_row"], n)
                if r == 4:
                    return
                order(v.tensor_scalar(tails[:, 0, :], frow[:, :], fixed[d][:, 0:1], None, ALU.mult))
                v.tensor_copy(tails[:, 1, :], fixed[d][:, 1:2].broadcast_to([P, D])).then_inc(S["fx_hT"], 1)
                v.wait_ge(S["fx_hTr"], 2 * r - 1)
                for k in range(2):
                    order(v.tensor_copy(ft[:, k, :], mem(psA[0:D, k * P:(k + 1) * P], not d)))
                order(v.tensor_tensor_scan(fr[:, 0, 1:P + 1], ft[:, 1, :], ft[:, 0, :], 0.0, ALU.mult, ALU.add))
                v.tensor_copy(fc[:, 0, :], mem(fr[:, 0, 0:P], not d)).then_inc(S["fx_ho"], 1)
                v.wait_ge(S["fx_hTr"], 2 * r)
                need(v, ld["st_hd"][1], LB * (r - 1))
                order(v.tensor_copy(slot(hd[1], SL - 1), psB[:, 0:D]))

            def prelu_dense(s, k, to, stored):
                if s.dense:
                    v.wait_ge(S[f"d_neg{k}"], s.n)
                    need(v, stored, 16 * s.h)
                    need(v, S[f"d_tr{k + 1}"], s.n - 2)
                    v.scalar_tensor_tensor(out=flat(to), in0=flat(neg[k]), scalar=slope[:, 2:3], in1=mmd[k][:, 0:HC],
                                           op0=ALU.mult, op1=ALU.add).then_inc(S[f"d_pre{k}"], 1)

            def row_centre(e):
                if e.r == 1 and e.edges:
                    v.wait_ge(S["gc_relu"], e.n)
                    v.wait_ge(ld["ld_hrow"][e.b], 16 * (e.h - PAIRS + 1))
                    v.tensor_tensor(u3[:, :, :], mem(u2[:, :, :], True), hrow[e.b][:, :, :], ALU.add).then_inc(S["gc_y"], 1)
                    v.wait_ge(S["gc_y"], e.c + 1)
                    ln_centre(LS["LE"], e.c + 1, lnb["lne"], "LE", u3[:, :, :])

            def row_spread(e):
                if e.r == 1 and e.edges:
                    ln_spread(LS["LE"], e.c + 1, lnb["lne"], "LE")

            def row_scale(e):
                if e.r == 1 and e.edges:
                    need(v, ld["st_hn"][e.b], 16 * e.h)
                    ln_scale(LS["LE"], e.c + 1, lnb["lne"], "LE", hnew[e.b][:, :, :])

            def gc_step(r, i, j, edges=True):
                s, p0, p1, o = (Step(r, i, j, lag) for lag in range(4))
                e, e2 = p0, p1
                c, n, b = s.c, s.n, s.b
                d = int(REVERSE[r]) if edges else 0
                cols = bass.ds(c * T, T)
                la = (LS["LA"], s.n, lnb["lna"], "LA")
                lb = (LS["LB"], o.n, lnb["lnb"], "LB")
                if o.dense:
                    v.wait_ge(S["d_mm2"], o.n)
                    v.tensor_tensor(flat(yd[1]), flat(x1d[o.q]), mmd[2][:, 0:HC], ALU.add).then_inc(S["d_res"], 1)
                if s.dense:
                    v.wait_ge(ld["ld_xin"][b], 16 * (s.h + 1))
                    v.tensor_tensor(yd[0][:, :, :], xin[b][:, :, :], relu_b[1][:, :].unsqueeze(1).broadcast_to([P, T, D]),
                                    ALU.add).then_inc(S["d_y"], 1)
                if o.dense:
                    v.wait_ge(S["d_res"], o.n)
                    ln_sum(*lb, yd[1][:, :, :])
                if s.dense:
                    v.wait_ge(S["d_y"], n)
                    ln_sum(*la, yd[0][:, :, :])
                if o.dense:
                    ln_subtract(*lb, yd[1][:, :, :])
                if s.dense:
                    ln_subtract(*la, yd[0][:, :, :])
                if edges:
                    v.wait_ge(ld["gat"][b], T * LB + 16 * T * (s.h + 1))
                    if r == 0:
                        v.tensor_copy(idx_f[:, :, cols], gs[b][:, :, D + 1:XW].rearrange("p t k -> p k t")).then_inc(S["gc_extract"], 1)
                        v.tensor_copy(norm_e[:, cols], gs[b][:, :, D]).then_inc(S["gc_extract"], 1)
                        norm = gs[b][:, :, D]
                    else:
                        norm = norm_r[:, cols]
                    v.tensor_tensor(fj(msgF), gs[b][:, :, 0:D], bc(norm, D), ALU.mult).then_inc(S["gc_msg"], 1)
                    v.tensor_copy(slot(msgF, 0), slot(aggF[1 - b], SL - 1)).then_inc(S["gc_carry"], 1)
                prelu_dense(p1, 1, t2d[p1.b], ld["st_t2"][p1.b])
                if o.dense:
                    ln_spread(*lb)
                if s.dense:
                    ln_spread(*la)
                row_spread(e2)
                if edges:
                    v.wait_ge(S["gc_maskF"], n)
                    v.wait_ge(S["gc_carry"], n)
                    need(v, ld["st_agg"][b], 16 * s.h)
                    v.tensor_tensor_scan(aggF[b][:, :], maskF[b][:, :], msgF[:, :], 0.0, ALU.mult, ALU.add
                                         ).then_inc(S["gc_agg"], 1)
                prelu_dense(p0, 0, t1d[p0.b], ld["st_t1"][p0.b])
                if s.dense:
                    need(v, st_x1[s.q], 16 * s.k)
                    ln_scale(*la, x1d[s.q][:, :, :])
                if edges:
                    v.wait_ge(S["gc_agg"], n)
                    need(v, S["gc_zT"], n - 1)
                    v.tensor_tensor(u1[:, :, :], fj(aggF[b]), bc(inn[d][:, cols], D), ALU.mult).then_inc(S["gc_z"], 1)
                if o.dense:
                    need(v, ld["st_od"][o.b], 16 * o.h)
                    ln_scale(*lb, od[o.b][:, :, :])
                row_scale(e2)
                row_centre(e)

            for r in range(2):
                if r:
                    v.wait_ge(ld["st_agg"][1], LB * r)
                order(v.memset(slot(aggF[1], SL - 1), 0.0))

                quads(v, r, gc_step)
                e, e2 = Step(r, QUADS, 0, 1), Step(r, QUADS, 0, 2)
                row_spread(e2)
                row_scale(e2)
                row_centre(e)
                row_spread(e)
                row_scale(e)
                if r == 1:
                    for j in range(3):
                        gc_step(2, 0, j, edges=False)
                if r == 0:
                    v.wait_ge(S["gc_extract"], 2 * CH)
                    order(v.tensor_copy(norm_r[:, :], norm_e[:, ::-1]))
                    order(v.tensor_copy(gi[0][:, :], idx_f[:, 0, :][:, ::-1]))
                    order(v.tensor_copy(gi[1][:, :], idx_f[:, 2, :]))
                    v.tensor_copy(gi[2][:, :], idx_f[:, 1, :][:, ::-1]).then_inc(S["idx_made"], 1)
                fix(r)

            mf = m_all[:, :, :].rearrange("p c s -> p (c s)")
            sf = s_all[:, :, :].rearrange("p c s -> p (c s)")
            k3 = psC[:, 0:T * 2 * D].rearrange("p (t f) -> p t f", f=2 * D)

            def hd_prepare(l, i, b):
                c = 2 * i + b
                d = int(REVERSE[2 + l])
                v.wait_ge(ld["ld_hrow"][b], (1 + l) * LB + 16 * (i + 1))
                need(v, S["t_hd"], l * CH + c)
                v.tensor_tensor(fj(hp), mem(hrow[b][:, :, :], d), bc(new[d][:, bass.ds(c * T, T)], D), ALU.mult
                                ).then_inc(S["t_hp"], 1)

            def hd_carry(b):
                v.tensor_copy(slot(hp, 0), slot(hd[1 - b], SL - 1)).then_inc(S["t_hpc"], 1)

            def hd_scan(l, i, b):
                n = l * CH + 2 * i + b + 1
                v.wait_ge(S["t_maskF"], n)
                v.wait_ge(S["t_hpc"], n)
                need(v, S["t_trh"], n - 2)
                need(v, ld["st_hd"][b], l * LB + 16 * i)
                v.tensor_tensor_scan(hd[b][:, :], maskF[b][:, :], hp[:, :], 0.0, ALU.mult, ALU.add).then_inc(S["t_hd"], 1)

            def row_out(c, i, b):
                need(v, ld["scat"][b], 16 * T * i)
                if isinstance(i, int) and i == 0:
                    v.wait_ge(ld["st_hn"][b], 4 * LB)
                ln_scale(LS["LE"], CH + c + 1, lnb["lne"], "LE", hnew[b][:, :, :])

            def t_step(l, i, b):
                c = 2 * i + b
                n = l * CH + c + 1
                d = int(REVERSE[2 + l])
                H = HEADS[l]
                HS = H * SL
                more = not (isinstance(i, int) and i == PAIRS - 1)
                nxt = (l, i + 1, b)
                hs = lambda ap: ap.rearrange("p (h s) -> p h s", s=SL)
                over = lambda ap: ap.unsqueeze(2).broadcast_to([P, H, D // H, T])
                wide = lambda t, lo, hi: t[:, :].rearrange("p (h c s) -> p h c s", h=H, s=SL)[:, :, :, lo:hi]
                m_old, m_new = mf[:, bass.ds(c * 2 * SL, HS)], mf[:, bass.ds((c + 1) * 2 * SL, HS)]
                s_old, s_new = sf[:, bass.ds(c * 2 * SL, HS)], sf[:, bass.ds((c + 1) * 2 * SL, HS)]
                pen = pen16[d][:, :, :, :].rearrange("p c h s -> p (c h s)")[:, bass.ds(c * 2 * SL, HS)]
                first = isinstance(i, int) and c == 0
                if l == 2 and not first:
                    ln_spread(LS["LE"], CH + c, lnb["lne"], "LE")
                v.wait_ge(S["t_qs"], n)
                v.wait_ge(S["t_kv"], n)
                v.tensor_tensor(prod[:, :, :], qs[b][:, :, 0:D], k3[:, :, 0:D], ALU.mult).then_inc(S["t_prod"], 1)
                if more:
                    hd_prepare(*nxt)
                v.wait_ge(S["t_prod"], n)
                v.tensor_reduce(hs(alpha8[:, 0:HS])[:, :, 1:SL].rearrange("p h t -> p t h"),
                                prod[:, :, :].rearrange("p t (h c) -> p t h c", h=H), AX, ALU.add).then_inc(S["t_alpha"], 1)
                v.tensor_copy(hs(alpha8[:, 0:HS])[:, :, 0], hs(m_old)[:, :, SL - 1]).then_inc(S["t_acar"], 1)
                if more:
                    hd_carry(b)
                v.wait_ge(S["t_acar"], n)
                v.tensor_tensor_scan(m_new, pen, alpha8[:, 0:HS], 0.0, ALU.add, ALU.max).then_inc(S["t_m"], 1)
                if more:
                    hd_scan(*nxt)
                if l == 2 and not first:
                    row_out(c - 1, i - 1 + b, 1 - b)
                v.wait_ge(S["t_m"], n)
                v.tensor_tensor(hs(d8[:, 0, 0:HS])[:, :, 1:SL], hs(m_new)[:, :, 0:T], hs(m_new)[:, :, 1:SL], ALU.subtract
                                ).then_inc(S["t_d0"], 1)
                v.tensor_tensor(hs(d8[:, 1, 0:HS])[:, :, 1:SL], hs(alpha8[:, 0:HS])[:, :, 1:SL], hs(m_new)[:, :, 1:SL],
                                ALU.subtract)
                v.wait_ge(S["t_d0"], n)
                v.tensor_tensor(hs(d8[:, 0, 0:HS])[:, :, 1:SL], hs(d8[:, 0, 0:HS])[:, :, 1:SL], hs(pen)[:, :, 1:SL], ALU.add
                                ).then_inc(S["t_d"], 1)
                v.tensor_copy(slot(msgF, 0), slot(aggF[1 - b], SL - 1)).then_inc(S["t_avc"], 1)
                v.wait_ge(S["t_e"], n)
                v.tensor_copy(hs(e8[:, 1, 0:HS])[:, :, 0], hs(s_old)[:, :, SL - 1]).then_inc(S["t_scar"], 1)
                v.tensor_tensor(wide(msgF, 1, SL), k3[:, :, D:2 * D].rearrange("p t (h c) -> p h c t", h=H),
                                over(hs(e8[:, 1, 0:HS])[:, :, 1:SL]), ALU.mult).then_inc(S["t_av"], 1)
                v.wait_ge(S["t_scar"], n)
                v.tensor_tensor_scan(s_new, e8[:, 0, 0:HS], e8[:, 1, 0:HS], 0.0, ALU.mult, ALU.add).then_inc(S["t_s"], 1)
                v.wait_ge(S["t_cF"], n)
                v.wait_ge(S["t_av"], n)
                v.wait_ge(S["t_avc"], n)
                need(v, ld["st_agg"][b], (2 + l) * LB + 16 * i)
                v.tensor_tensor_scan(aggF[b][:, :], cF[:, :], msgF[:, :], 0.0, ALU.mult, ALU.add).then_inc(S["t_agg"], 1)
                v.wait_ge(S["t_s"], n)
                v.tensor_scalar(r8[:, 0:HS], s_new, 1e-16, None, ALU.add).then_inc(S["t_r0"], 1)
                v.wait_ge(S["t_r0"], n)
                v.reciprocal(r8[:, 0:HS], r8[:, 0:HS]).then_inc(S["t_r"], 1)
                v.wait_ge(S["t_r"], n)
                v.wait_ge(S["t_agg"], n)
                v.tensor_tensor(u1[:, :, :].rearrange("p t (h c) -> p h c t", h=H), wide(aggF[b], 1, SL),
                                over(hs(r8[:, 0:HS])[:, :, 1:SL]), ALU.mult).then_inc(S["t_u1"], 1)
                v.wait_ge(S["t_u1"], n)
                v.tensor_tensor(u2[:, :, :], u1[:, :, :], qs[b][:, :, D:2 * D], ALU.add).then_inc(S["t_u2"], 1)
                v.wait_ge(S["t_u2"], n)
                if l < 2:
                    v.tensor_scalar(u3[:, :, :], u2[:, :, :], 0.0, slope[:, 1:2], ALU.min, ALU.mult).then_inc(S["t_u3"], 1)
                    need(v, ld["st_hn"][b], (2 + l) * LB + 16 * i)
                    v.wait_ge(S["t_u3"], n)
                    v.tensor_tensor(mem(hnew[b][:, :, :], d), u3[:, :, :], u2[:, :, :], ALU.add).then_inc(S["t_hn"], 1)
                else:
                    v.wait_ge(ld["ld_x1"][b], 16 * (i + 1))
                    v.tensor_tensor(u3[:, :, :], u2[:, :, :], fj(x1b[b]), ALU.add).then_inc(S["t_y"], 1)
                    v.wait_ge(S["t_y"], c + 1)
                    ln_centre(LS["LE"], CH + c + 1, lnb["lne"], "LE", u3[:, :, :])

            for l in range(3):
                v.wait_ge(ld["st_agg"][1], LB * (2 + l))
                order(v.memset(slot(aggF[1], SL - 1), 0.0))
                for b in range(2):
                    hd_prepare(l, 0, b)
                    hd_carry(b)
                    hd_scan(l, 0, b)

                def t_body(i):
                    for b in range(2):
                        t_step(l, i, b)

                pairs(v, PAIRS, t_body)
                if l == 2:
                    ln_spread(LS["LE"], 2 * CH, lnb["lne"], "LE")
                    row_out(CH - 1, PAIRS - 1, 1)
                fix(2 + l)


_L = [f"L1_gnn_{w}{k}" for k in range(3) for w in ("Wq", "bq", "Wk", "bk", "Wv", "bv", "We", "Ws", "bs")]
_INS = ["x", "src", "dst", "edge_attr_32", "L0_gnn_W1", "L0_gnn_b1", "L0_gnn_W2", "L0_gnn_b2", *_L, "L1_gnn_prelu_a"]


def kernel(**inputs):
    import numpy as np
    import concourse.bacc as bacc
    from concourse.bass_utils import run_bass_kernel_spmd

    given = {k: np.asarray(v) for k, v in inputs.items()}
    given["x"] = np.pad(given["x"], ((0, NPAD - N_NODES), (0, 0)))
    given["src"] = np.pad(given["src"], (0, EPAD - N_EDGES), constant_values=N_NODES)
    given["dst"] = np.pad(given["dst"], (1, EPAD - N_EDGES), constant_values=(-1, N_NODES))
    given["dst"] = np.pad(given["dst"], (0, 1), constant_values=N_NODES + 1)
    ea = np.pad(given["edge_attr_32"], ((0, EPAD - N_EDGES), (0, 0)))
    given["edge_attr_32"] = ea.reshape(P, EC, DE).transpose(2, 1, 0).reshape(DE, EC * P)
    given["L1_gnn_prelu_a"] = given["L1_gnn_prelu_a"].reshape(1)

    nc = bacc.Bacc("TRN2", target_bir_lowering=False, num_devices=1)
    arrays, aps = {}, {}
    for name in _INS:
        a = np.ascontiguousarray(given[name])
        arrays[f"in_{name}"] = a
        aps[name] = nc.dram_tensor(f"in_{name}", a.shape, mybir.dt.from_np(a.dtype), kind="ExternalInput").ap()
    out = nc.dram_tensor("out_0", (NPAD, D), F32, kind="ExternalOutput").ap()
    layers = [[aps[n] for n in _L[9 * k:9 * k + 9]] for k in range(3)]
    gnn_kernel(nc, aps["x"], aps["src"], aps["dst"], aps["edge_attr_32"], aps["L0_gnn_W1"], aps["L0_gnn_b1"],
               aps["L0_gnn_W2"], aps["L0_gnn_b2"], layers, aps["L1_gnn_prelu_a"], out)
    r = run_bass_kernel_spmd(nc, [arrays], core_ids=[0])
    return r.results[0]["out_0"][0:N_NODES]
```

```python
import math
from contextlib import ExitStack

import concourse.bass as bass
from concourse import mybir

F32 = mybir.dt.float32
F16 = mybir.dt.float16
BF16 = mybir.dt.bfloat16
I32 = mybir.dt.int32
ALU = mybir.AluOpType
ACT = mybir.ActivationFunctionType
AX = mybir.AxisListType.X

P = 128
D = 64
DE = 32
N_NODES, N_EDGES = 100000, 50000
T = 7
SL = T + 1
EC = 392
CH = EC // T
PAIRS = CH // 2
QUADS = CH // 4
NN = 2 * EC
NPAD, EPAD = P * NN, P * EC
XW = D + 4
BIG = 1.0e30
EPS = 1e-5
HC = T * D
FS = D * SL
HEADS = (2, 2, 1)
assert EC % (2 * T) == 0 and EC % 4 == 0 and NPAD % CH == 0 and NPAD > N_NODES and EPAD > N_EDGES

REVERSE = (False, True, False, True, False)


W_LOADED = 16 * (3 * 10 + 2 * 3 + 1 + 5 * 3)


class Step:

    def __init__(self, r, i, j, lag=0):
        self.r, k = r, j - lag
        self.c = 4 * i + k
        self.g = r * CH + self.c
        self.n = self.g + 1
        self.b, self.q = k % 2, k % 4
        self.h = r * PAIRS + 2 * i + k // 2
        self.k = r * QUADS + i + k // 4
        self.fixed = isinstance(i, int)
        self.edges = not self.fixed or 0 <= self.c < CH
        self.dense = not self.fixed or 0 <= self.g < 2 * CH


class Order:

    def __init__(self, eng, s):
        self.eng, self.s, self.n = eng, s, 0

    def __call__(self, instruction):
        self.n += 1
        instruction.then_inc(self.s, 1)
        self.eng.wait_ge(self.s, self.n)


def gnn_kernel(nc, x, src, dst, eaT, W1, b1, W2, b2, layers, prelu_a, out):
    with ExitStack() as ctx:
        def sb(name, shape, dt=F32):
            return ctx.enter_context(nc.sbuf_tensor(name, shape, dt))

        def sem(name):
            return ctx.enter_context(nc.semaphore(name))

        def sems(names):
            return {n: sem(n) for n in names.split()}

        def dram(name, shape, dt=F32):
            return nc.dram_tensor(name, shape, dt).ap()

        ext = dram("ext", (NPAD, XW))
        xd_rows = dram("xd_rows", (EPAD, D))
        tab_h1 = dram("tab_h1", (EPAD + P, D))
        tab = [dram(f"tab{k}", (NPAD + EPAD, D)) for k in range(3)]
        agg_blk = dram("agg_blk", (P * CH, FS))
        hd_blk = [dram(f"hd_blk{k}", (P * CH, FS)) for k in range(3)]

        def rows(t, lo=0, n=EPAD):
            return t[lo:lo + n, :].rearrange("(p c) f -> p (c f)", p=P)

        def blocks(t):
            return t.rearrange("(p c) f -> p (c f)", p=P)

        def shared(name, early, late):
            def words(spec):
                return -(-math.prod(spec[1][1:]) * (2 if spec[2:] == (F16,) else 4) // 4)

            whole = sb(name, [P, max(sum(map(words, s)) for s in (early, late))])
            got = {}
            for specs in (early, late):
                at = 0
                for spec in specs:
                    ap = whole[0:spec[1][0], at:at + words(spec)]
                    if spec[2:] == (F16,):
                        ap = ap.bitcast(F16)
                    if len(spec[1]) == 3:
                        ap = ap.rearrange("p (a b) -> p a b", b=spec[1][2])
                    got[spec[0]] = ap
                    at += words(spec)
            return got

        two_of = lambda names, shape: [(f"{n}{b}", shape) for n in names.split() for b in range(2)]
        B = shared("nodes_or_dense", [(f"tn{k}", [P, NN]) for k in range(5)], [(f"x1d{q}", [P, T, D]) for q in range(4)] + two_of("t1d t2d", [P, T, D]))
        qs = [sb(f"qs{b}", [P, T, 2 * D]) for b in range(2)]
        prod, cF, hp = sb("prod", [P, T, D]), sb("cF", [P, FS]), sb("hp", [P, FS])
        B |= shared("aux_or_rows", [("aux", [P, NN, 4])], two_of("hnew", [P, T, D]) + [(f"u{k}", [P, T, D]) for k in (1, 2, 3)])
        B |= shared("onehots_or_sums_and_output", [(f"oh{q}_{k}", [P, NN], F16) for q in range(4) for k in range(2)],
                    [("m_all", [P, CH + 1, 2 * SL]), ("s_all", [P, CH + 1, 2 * SL])] + two_of("od", [P, T, D]))
        od = [B[f"od{b}"] for b in range(2)]
        B |= shared("degrees_or_dense",
                    [(f"hl{k}_{j}", [P, EC]) for k in range(2) for j in range(2)] + [(f"te{k}", [P, EC]) for k in range(3)]
                    + [("ef", [P, 4, EC]), ("io_node", [P, NN]), ("ones", [P, NN]), ("io_blk", [P, CH, SL])]
                    + [(f"io_row{d}", [P, CH, SL]) for d in range(2)],
                    [(f"nT{k}", [P, 4 * P]) for k in range(3)] + [("zT", [P, 4 * P])] + two_of("neg yd", [P, T, D])
                    + [(f"{k}_{j}", [P, T, D]) for k in ("lna", "lnb", "lne") for j in ("xc", "sq")])
        hl = [[B[f"hl{k}_{j}"] for j in range(2)] for k in range(2)]
        te, nT = ([B[f"{n}{k}"] for k in range(3)] for n in ("te", "nT"))
        neg, yd, io_row = ([B[f"{n}{k}"] for k in range(2)] for n in ("neg", "yd", "io_row"))
        ef, io_node, ones, io_blk, zT = (B[n] for n in "ef io_node ones io_blk zT".split())
        t1d, t2d, hnew = ([B[n + "0"], B[n + "1"]] for n in "t1d t2d hnew".split())
        x1d = [B[f"x1d{q}"] for q in range(4)]
        tn = [B[f"tn{k}"] for k in range(5)]
        oh = [[B[f"oh{q}_{k}"] for k in range(2)] for q in range(4)]
        aux, u1, u2, u3, m_all, s_all = (B[n] for n in "aux u1 u2 u3 m_all s_all".split())

        ident = sb("ident", [P, P])
        below = sb("below", [P, P])
        io_lo = sb("io_lo", [P, NN], F16)
        io_hi = sb("io_hi", [P, P], F16)
        far = [sb(f"far{q}", [P, P], F16) for q in range(4)]
        oh_hi = [[sb(f"oh_hi{q}_{k}", [P, P], F16) for k in range(2)] for q in range(4)]
        one_t = sb("one_t", [P, 1])
        io_part = sb("io_part", [P, 1])
        zero16 = sb("zero16", [P, EC], F16)
        wqs = [sb(f"wqs{k}", [D + 1, 2 * D]) for k in range(3)]
        wkv = [sb(f"wkv{k}", [D + DE + 1, 2 * D]) for k in range(3)]
        wgc = [sb(f"wgc{k}", [D + 1, D]) for k in range(2)]
        wpair = [sb(f"wpair{k}", [P, P]) for k in range(5)]
        bias3 = [sb(f"bias3_{k}", [D + 1, HC], BF16) for k in range(5)]
        braw = [sb(f"braw{k}", [D + 1, D]) for k in range(5)]
        bsplit = [sb(f"bsplit{k}", [D + 1, D]) for k in range(2)]
        b16 = [sb(f"b16_{k}", [D + 1, D], BF16) for k in range(3)]
        ones16 = sb("ones16", [D + 1, P], BF16)
        relu_b = [sb(f"relu_b{k}", [P, D]) for k in range(2)]
        slope = sb("slope", [P, 3])
        eps_t = sb("eps_t", [P, 1])

        mask8 = [sb(f"mask8_{d}", [P, CH, SL]) for d in range(2)]
        new = [sb(f"new_{d}", [P, EC]) for d in range(2)]
        pen16 = [sb(f"pen16_{d}", [P, CH, 2, SL]) for d in range(2)]
        fmask = [sb(f"fmask_{d}", [P, CH, SL]) for d in range(2)]
        slotm = [sb(f"slotm_{d}", [P, SL]) for d in range(2)]
        cont_all = [sb(f"cont_all_{d}", [P, 1]) for d in range(2)]
        fixed = [sb(f"fixed_{d}", [P, 2]) for d in range(2)]
        inn = [sb(f"inn_{d}", [P, EC]) for d in range(2)]
        fixi = [sb(f"fixi_{d}", [P, 4], I32) for d in range(2)]
        fixo = sb("fixo", [P, 1], I32)
        norm_e = sb("norm_e", [P, EC])
        norm_r = sb("norm_r", [P, EC])
        idx_f = sb("idx_f", [P, 3, EC])

        stage_i = [sb(f"stage_i{k}", [P, EC], I32) for k in range(4)]
        gi = [sb(f"gi{k}", [P, EC], I32) for k in range(4)]
        GI = {1: 0, 2: 1, 3: 2, 4: 1}

        qi = sb("qi", [P, EC], I32)
        offs = sb("offs", [P, 2])

        tails = sb("tails", [P, 4, D])
        ft = sb("ft", [D, 4, P])
        fd = sb("fd", [D, 2, P])
        fe = sb("fe", [D, 2, P])
        fr = sb("fr", [D, 3, P + 1])
        fc = sb("fc", [D, 3, P])
        carry = sb("carry", [P, 3, D])
        fb = sb("fb", [P, FS])
        fh = sb("fh", [P, FS])
        fx1 = sb("fx1", [P, FS])
        fxd = sb("fxd", [P, D])
        fbm = sb("fbm", [P, D, SL])
        pre = sb("pre", [P, 4, D])
        fsel = sb("fsel", [P, CH, SL])
        fsc = sb("fsc", [P, 8])
        fm2 = sb("fm2", [P, D])
        fdd = sb("fdd", [P, 2, D])
        fee = sb("fee", [P, 2, D])
        fz = sb("fz", [P, 6, D])
        fT = sb("fT", [D + 1, P])
        frow = sb("frow", [P, D])
        fln = {"xc": sb("lnf_xc", [P, 1, D]), "sq": sb("lnf_sq", [P, 1, D]),
               **{k: sb(f"lnf_{k}", [P, 1]) for k in ("sum", "ss", "std", "rstd")}}

        gs = [sb(f"gs{b}", [P, T, XW]) for b in range(2)]
        gt = [g[:, :, :].rearrange("p t f -> p (t f)")[:, 0:HC] for g in gs]
        idxb = [sb(f"idxb{b}", [P, T], I32) for b in range(2)]
        oidxb = [sb(f"oidxb{b}", [P, T], I32) for b in range(2)]
        hrow = [sb(f"hrow{b}", [P, T, D]) for b in range(2)]
        hd = [sb(f"hd{b}", [P, FS]) for b in range(2)]
        maskF = [sb(f"maskF{b}", [P, FS]) for b in range(2)]
        msgF = sb("msgF", [P, FS])
        aggF = [sb(f"aggF{b}", [P, FS]) for b in range(2)]
        hdT = sb("hdT", [D + 1, T * P])
        kvin = [sb(f"kvin{b}", [D + DE + 1, T * P]) for b in range(2)]
        alpha8 = sb("alpha8", [P, 2 * SL])
        d8 = sb("d8", [P, 2, 2 * SL])
        e8 = sb("e8", [P, 2, 2 * SL])
        r8 = sb("r8", [P, 2 * SL])
        x1b = [sb(f"x1b{b}", [P, FS]) for b in range(2)]
        xin = [sb(f"xin{b}", [P, T, D]) for b in range(2)]
        vs = yd
        mask8f = [m[:, :, :].rearrange("p c s -> p (c s)") for m in mask8]

        def ln_buffers(name):
            return {"xc": B[name + "_xc"], "sq": B[name + "_sq"],
                    **{k: sb(f"{name}_{k}", [P, T]) for k in ("sum", "ss", "std", "rstd")}}

        def ln_sems(name):
            return sems(" ".join(f"{name}_{k}" for k in "sum centred squared spread std rstd out".split()))

        lnb = {k: ln_buffers(k) for k in ("lna", "lnb", "lne")}
        LS = {k: ln_sems(k) for k in ("LA", "LB", "LE")}

        ps = [ctx.enter_context(nc.psum_tensor(f"ps{k}", [P, 1024], F32)) for k in range(4)]
        psA, psB, psC, psD = ps
        bank = lambda k: ps[k // 2][:, k % 2 * 512:(k % 2 + 1) * 512]
        trz, trd = bank(0), [bank(k) for k in (1, 2, 3)]
        mmz, mmd = bank(4), [bank(k) for k in (5, 6, 7)]

        S = sems("waits_passed idx_copied oidx_copied w_loaded edges_loaded pool_consts onehots_ready onehots_used hi_far hi_ready prepared counts_done sqrt_done "
                 "totals_ready offset_done sqrt_in deg_tail degT deg_carry deg_back "
                 "idx_made consts_stored relu_made "
                 "aux_two aux_done ext_stored gc_extract gc_maskF gc_msg gc_carry gc_agg gc_z gc_zT gc_zTc gc_mm gc_relu gc_y "
                 "pairs_cleared "
                 "d_y d_tr0 d_tr1 d_tr2 d_trc0 d_trc1 d_trc2 d_mm0 d_mm1 d_mm2 d_neg0 d_neg1 d_pre0 d_pre1 d_res "
                 "t_maskF t_hp t_hpc t_hd t_trh t_hdT t_trg t_gT t_q t_kv t_qs t_prod t_alpha t_acar t_m t_d0 t_d t_e "
                 "t_scar t_s t_r0 t_r t_av t_avc t_v t_agg t_u1 t_u2 t_u3 t_hn t_cF t_y "
                 "fx_tail fx_tailT fx_d fx_e fx_carry fx_back fx_z fx_zT fx_zTc fx_mm fx_relu fx_row fx_hT fx_hTr fx_ho "
                 "fx_gather fx_scatter "
                 "dve_order pool_order")
        ld = {k: [sem(f"{k}{b}") for b in range(2)] for k in
              "ld_hrow ld_ea ld_x1 ld_xin gat scat st_xd st_agg st_hn st_hd st_t1 st_t2 st_od".split()}
        st_x1 = [sem(f"st_x1_{q}") for q in range(4)]

        def settle(eng):
            if eng.engine in (mybir.EngineType.SP, mybir.EngineType.Pool, mybir.EngineType.PE):
                eng.sem_inc(S["waits_passed"], 1)

        def need(eng, s, v):
            if isinstance(v, int) and v <= 0:
                return
            eng.wait_ge(s, v)
            if not isinstance(v, int):
                settle(eng)

        def pairs(eng, n, body, tail=1):
            body(0)
            with eng.Fori(1, n - tail) as i:
                body(i)
            for i in range(n - tail, n):
                body(i)

        def quads(eng, r, step):
            def body(i):
                for j in range(4):
                    step(r, i, j)
            pairs(eng, QUADS, body)

        flat = lambda t: t[:, :, :].rearrange("p t f -> p (t f)")

        def fj(t):
            return t[:, :].rearrange("p (f s) -> p s f", s=SL)[:, 1:SL, :]

        def slot(t, s):
            return t[:, :].rearrange("p (f s) -> p f s", s=SL)[:, :, s]

        def bc(ap, n):
            return ap.unsqueeze(2).broadcast_to([ap.shape[0], ap.shape[1], n])

        def mem(ap, rev):
            return ap[:, ::-1] if rev else ap

        def col0(c, rev):
            return (EC - T) - c * T if rev else c * T

        def dense_done(eng):
            for q in range(4):
                eng.wait_ge(st_x1[q], 16 * 2 * QUADS)
            for k in ("st_t1", "st_t2", "st_od"):
                for b in range(2):
                    eng.wait_ge(ld[k][b], 2 * LB)

        k3 = psC[:, 0:T * 2 * D].rearrange("p (t f) -> p t f", f=2 * D)

        block = ctx.enter_context(nc.Block())
        LB = 16 * PAIRS

        @block.sync
        def _(sp):
            e2 = dst[1:1 + EPAD].rearrange("(p c) -> p c", p=P)
            sp.dma_start(stage_i[0][:, :], src.rearrange("(p c) -> p c", p=P)).then_inc(S["edges_loaded"], 16)
            sp.dma_start(stage_i[1][:, :], e2).then_inc(S["edges_loaded"], 16)
            sp.dma_start(stage_i[2][:, :], dst[0:EPAD].rearrange("(p c) -> p c", p=P)).then_inc(S["edges_loaded"], 16)
            sp.dma_start(stage_i[3][:, :], dst[2:2 + EPAD].rearrange("(p c) -> p c", p=P)).then_inc(S["edges_loaded"], 16)
            for k, (Wq, bq, Wk, bk, Wv, bv, We, Ws, bs) in enumerate(layers):
                for t, r0, c0, w in ((wqs[k], 0, 0, Wq), (wqs[k], 0, D, Ws), (wkv[k], 0, 0, Wk), (wkv[k], 0, D, Wv),
                                     (wkv[k], D, 0, We), (wkv[k], D, D, We)):
                    sp.dma_start(t[r0:r0 + w.shape[0], c0:c0 + D], w).then_inc(S["w_loaded"], 16)
                for t, r0, c0, w in ((wqs[k], D, 0, bq), (wqs[k], D, D, bs), (wkv[k], D + DE, 0, bk), (wkv[k], D + DE, D, bv)):
                    sp.dma_start(t[r0:r0 + 1, c0:c0 + D], w.unsqueeze(0)).then_inc(S["w_loaded"], 16)
            for k, (w, bb) in enumerate(((W1, b1), (W2, b2))):
                sp.dma_start(wgc[k][0:D, :], w).then_inc(S["w_loaded"], 16)
                sp.dma_start(wgc[k][D:D + 1, :], bb.unsqueeze(0)).then_inc(S["w_loaded"], 16)
                sp.dma_start(relu_b[k][:, :], bb.unsqueeze(0).broadcast_to([P, D])).then_inc(S["w_loaded"], 16)
            sp.wait_ge(S["pairs_cleared"], 1)
            for k, (w, bb) in enumerate([(l[7], l[8]) for l in layers] + [(W1, b1), (W2, b2)]):
                for o in (0, D):
                    sp.dma_start(wpair[k][o:o + D, o:o + D], w).then_inc(S["w_loaded"], 16)
                sp.dma_start(braw[k][:, :], bb.unsqueeze(0).broadcast_to([D + 1, D])).then_inc(S["w_loaded"], 16)
            sp.dma_start(slope[:, 0:1], prelu_a.unsqueeze(0).broadcast_to([P, 1])).then_inc(S["w_loaded"], 16)

            def xd_body(i):
                for b in range(2):
                    c = 2 * i + b
                    part = bass.ds(c * (NPAD // CH), NPAD // CH)
                    sp.dma_start(ext[part, 0:D], x[part, :]).then_inc(S["ext_stored"], 16)
                    need(sp, ld["gat"][b], 16 * T * (i + 1))
                    sp.dma_start(rows(xd_rows)[:, bass.ds(c * HC, HC)], x1b[b][:, 0:HC]).then_inc(ld["st_xd"][b], 16)

            pairs(sp, PAIRS, xd_body)

            xr = rows(x, 0, NPAD)
            for b in range(2):
                sp.wait_ge(ld["st_xd"][b], LB)

            def gc_loads(s):
                cols = bass.ds(s.g * HC, HC)
                need(sp, S["d_y"], s.n - 2)
                sp.dma_start(flat(xin[s.b]), xr[:, cols]).then_inc(ld["ld_xin"][s.b], 16)

            def gc_load_xd(s):
                if s.r == 1:
                    need(sp, S["gc_y"], s.c - 1)
                    sp.dma_start(flat(hrow[s.b]), rows(xd_rows)[:, bass.ds(col0(s.c, True) * D, HC)]
                                 ).then_inc(ld["ld_hrow"][s.b], 16)

            def dense_store(s, table, buf, ready, done):
                need(sp, ready, s.n)
                sp.dma_start(rows(table, 0, NPAD)[:, bass.ds(s.g * HC, HC)], flat(buf)).then_inc(done, 16)

            def dense_stores(r, i, j, edges_too=None):
                a, p0, p1, o = (Step(r, i, j, lag) for lag in range(4))
                if p1.dense:
                    dense_store(p1, tab[2], t2d[p1.b], S["d_pre1"], ld["st_t2"][p1.b])
                if edges_too:
                    edges_too()
                if p0.dense:
                    dense_store(p0, tab[1], t1d[p0.b], S["d_pre0"], ld["st_t1"][p0.b])
                if a.dense:
                    dense_store(a, tab[0], x1d[a.q], LS["LA"]["LA_out"], st_x1[a.q])
                if o.dense:
                    dense_store(o, out, od[o.b], LS["LB"]["LB_out"], ld["st_od"][o.b])

            def row_stores(s):
                if not s.edges:
                    return
                if s.r == 0:
                    need(sp, S["gc_relu"], s.n)
                    sp.dma_start(rows(tab_h1)[:, bass.ds(s.c * HC, HC)], flat(hnew[s.b])).then_inc(ld["st_hn"][s.b], 16)
                else:
                    need(sp, LS["LE"]["LE_out"], s.c + 1)
                    sp.dma_start(rows(tab[0], NPAD)[:, bass.ds(col0(s.c, True) * D, HC)], flat(hnew[s.b])
                                 ).then_inc(ld["st_hn"][s.b], 16)

            def gc_step(r, i, j):
                s = Step(r, i, j)
                if not (s.fixed and i == QUADS - 1 and j >= 2):
                    gc_loads(Step(r, i, j, -2))
                dense_stores(r, i, j, lambda: agg_store(s))
                row_stores(Step(r, i, j, 1 + r))
                if not (s.fixed and i == QUADS - 1 and j == 3):
                    gc_load_xd(Step(r, i, j, -1))

            def agg_store(s):
                need(sp, S["gc_agg"], s.n)
                sp.dma_start(blocks(agg_blk)[:, bass.ds(s.c * FS, FS)], aggF[s.b][:, :]).then_inc(ld["st_agg"][s.b], 16)

            def opened(r):
                sp.wait_ge(S["fx_scatter"], 16 * r)
                for b in range(2):
                    sp.wait_ge(ld["st_hn"][b], LB * r)

            for r in range(2):
                if r:
                    opened(r)
                for b in range(2):
                    gc_loads(Step(r, 0, b))
                gc_load_xd(Step(r, 0, 0))
                quads(sp, r, gc_step)
                for lag in range(1 + r, 0, -1):
                    row_stores(Step(r, QUADS, 0, lag))
            for j in range(3):
                dense_stores(2, 0, j)

            def t_load_rows(l, i, j):
                c, b = 2 * i + j, j % 2
                need(sp, S["t_hp"], l * CH + c - 1)
                sp.dma_start(flat(hrow[b]), rows(tab[l], NPAD)[:, bass.ds(col0(c, REVERSE[2 + l]) * D, HC)]
                             ).then_inc(ld["ld_hrow"][b], 16)

            def t_loads(l, i, b):
                c = 2 * i + b
                need(sp, S["t_kv"], l * CH + c - 1)
                sp.dma_start(kvin[b][D:D + DE, :], eaT[:, bass.ds(col0(c, REVERSE[2 + l]) * P, T * P)]
                             ).then_inc(ld["ld_ea"][b], 16)
                if l == 2:
                    need(sp, S["t_y"], c - 1)
                    sp.dma_start(x1b[b][:, :], blocks(hd_blk[0])[:, bass.ds(c * FS, FS)]).then_inc(ld["ld_x1"][b], 16)

            def t_store_hd(l, i, j):
                c, b = 2 * i + j, j % 2
                need(sp, S["t_hd"], l * CH + c + 1)
                sp.dma_start(blocks(hd_blk[l])[:, bass.ds(c * FS, FS)], hd[b][:, :]).then_inc(ld["st_hd"][b], 16)

            def t_stores(l, i, b):
                c = 2 * i + b
                n = l * CH + c + 1
                need(sp, S["t_agg"], n)
                sp.dma_start(blocks(agg_blk)[:, bass.ds(c * FS, FS)], aggF[b][:, :]).then_inc(ld["st_agg"][b], 16)

            def t_store_rows(l, i, b):
                c = 2 * i + b
                need(sp, S["t_hn"], l * CH + c + 1)
                sp.dma_start(rows(tab[l + 1], NPAD)[:, bass.ds(col0(c, REVERSE[2 + l]) * D, HC)], flat(hnew[b])
                             ).then_inc(ld["st_hn"][b], 16)

            for l in range(3):
                opened(2 + l)
                t_load_rows(l, 0, 0)
                t_load_rows(l, 0, 1)
                for b in range(2):
                    t_loads(l, 0, b)
                t_load_rows(l, 0, 2)
                t_store_hd(l, 0, 0)

                def t_body(i):
                    left = CH - 2 * i if isinstance(i, int) else CH
                    for b in range(2):
                        if left > b + 3:
                            t_load_rows(l, i, b + 3)
                        if left > b + 1:
                            t_store_hd(l, i, b + 1)
                        if left > b + 2:
                            t_loads(l, i + 1, b)
                        t_stores(l, i, b)
                        if l < 2 and not (isinstance(i, int) and 2 * i + b == 0):
                            t_store_rows(l, i - 1 + b, 1 - b)

                pairs(sp, PAIRS, t_body, tail=2)
                if l < 2:
                    t_store_rows(l, PAIRS - 1, 1)
            for b in range(2):
                sp.wait_ge(ld["st_hd"][b], 3 * LB)
                sp.wait_ge(ld["st_agg"][b], 5 * LB)
                sp.wait_ge(ld["st_hn"][b], 4 * LB)
                sp.wait_ge(ld["scat"][b], T * LB)
            dense_done(sp)
            sp.wait_ge(S["fx_scatter"], 16 * 5)

        @block.gpsimd
        def _(pool):
            order = Order(pool, S["pool_order"])
            order(pool.memset(ident[:, :], 0.0))
            order(pool.affine_select(out=ident[:, :], in_=ident[:, :], compare_op=ALU.not_equal, fill=1.0, base=0,
                                     pattern=[[-1, P]], channel_multiplier=1))
            order(pool.memset(below[:, :], 1.0))
            order(pool.affine_select(out=below[:, :], in_=below[:, :], compare_op=ALU.is_ge, fill=0.0, base=-1,
                                     pattern=[[1, P]], channel_multiplier=-1))
            loose = dict(allow_small_or_imprecise_dtypes=True)
            order(pool.iota(io_lo[:, :], [[1, NN]], base=0, channel_multiplier=0, **loose))
            order(pool.iota(io_hi[:, :], [[1, P]], base=0, channel_multiplier=0, **loose))
            order(pool.iota(io_node[:, :], [[1, NN]], base=0, channel_multiplier=NN, **loose))
            order(pool.iota(io_part[:, :], [[1, 1]], base=0, channel_multiplier=1, **loose))
            order(pool.iota(io_blk[:, :, :], [[1, CH], [0, SL]], base=0, channel_multiplier=CH, **loose))
            order(pool.iota(io_row[0][:, :, :], [[T, CH], [1, SL]], base=-1, channel_multiplier=EC, **loose))
            order(pool.iota(io_row[1][:, :, :], [[-T, CH], [-1, SL]], base=EC, channel_multiplier=EC, **loose))
            for t in (hdT, fT):
                order(pool.memset(t[D:D + 1, :], 1.0))
            for b in range(2):
                order(pool.memset(kvin[b][D + DE:D + DE + 1, :], 1.0))
            order(pool.memset(ones16[:, :], 1.0))
            for k in range(5):
                order(pool.memset(bias3[k][:, :], 0.0))
                if k < 4:
                    order(pool.memset(wpair[k][:, :], 0.0))
            pool.memset(wpair[4][:, :], 0.0).then_inc(S["pairs_cleared"], 1)
            order(pool.memset(one_t[:, :], 1.0))
            pool.memset(eps_t[:, :], EPS).then_inc(S["pool_consts"], 1)

            def copy_idx(phase, c, b, idx, before):
                need(pool, ld["gat"][b], before)
                pool.tensor_copy(idxb[b][:, :], idx[:, bass.ds(c * T, T)]).then_inc(S["idx_copied"], 1)

            def gathers(phase, i, b, idx, table, bound, to, width, between=None):
                c = 2 * i + b
                base = phase * T * LB
                need(pool, S["idx_copied"], phase * CH + c + 1)
                for t in range(T):
                    if t == T // 2 and between:
                        between()
                    if t == T - 1 and not (isinstance(i, int) and i == PAIRS - 1 and b == 1):
                        copy_idx(phase, c + 1, 1 - b, idx, base + 16 * T * (i + b))
                    pool.indirect_dma_start(out=to(b, t)[:, 0:width], out_offset=None, in_=table,
                                            in_offset=bass.IndirectOffsetOnAxis(ap=idxb[b][:, t:t + 1], axis=0),
                                            bounds_check=bound, oob_is_err=False).then_inc(ld["gat"][b], 16)

            def opened(r):
                for b in range(2):
                    need(pool, ld["st_hn"][b], LB * min(r, 4))
                need(pool, S["fx_scatter"], 16 * r)

            def fix_gather(r, table, bound, col, to):
                pool.indirect_dma_start(out=to, out_offset=None, in_=table,
                                        in_offset=bass.IndirectOffsetOnAxis(ap=fixi[REVERSE[r]][:, col:col + 1], axis=0),
                                        bounds_check=bound, oob_is_err=False).then_inc(S["fx_gather"], 16)

            def fix(r):
                for b in range(2):
                    pool.wait_ge(ld["st_agg"][b], LB * (r + 1))
                fix_gather(r, agg_blk, P * CH - 1, 0, fb[:, :])
                if r == 1:
                    fix_gather(r, xd_rows, EPAD - 1, 1, fxd[:, :])
                if r >= 2:
                    for b in range(2):
                        pool.wait_ge(ld["st_hd"][b], LB * (r - 1))
                    fix_gather(r, hd_blk[r - 2], P * CH - 1, 0, fh[:, :])
                if r == 4:
                    fix_gather(r, hd_blk[0], P * CH - 1, 0, fx1[:, :])
                for b in range(2):
                    pool.wait_ge(ld["st_hn"][b], LB * min(r + 1, 4))
                    need(pool, ld["scat"][b], T * LB if r == 4 else 0)
                pool.wait_ge(S["fx_row"], r + 1)
                if r == 0:
                    to, bound, at = tab_h1, EPAD + P - 1, fixi[0][:, 2:3]
                elif r < 4:
                    to, bound, at = tab[r - 1], NPAD + EPAD - 1, fixi[REVERSE[r]][:, 3:4]
                else:
                    to, bound, at = out, NPAD - 1, fixo[:, 0:1]
                pool.indirect_dma_start(out=to, out_offset=bass.IndirectOffsetOnAxis(ap=at, axis=0), in_=frow[:, :],
                                        in_offset=None, bounds_check=bound, oob_is_err=False
                                        ).then_inc(S["fx_scatter"], 16)

            pool.wait_ge(S["edges_loaded"], 64)
            copy_idx(0, 0, 0, stage_i[1], 0)

            def xd_body(i):
                for b in range(2):
                    need(pool, ld["st_xd"][b], 16 * i)
                    gathers(0, i, b, stage_i[1], x, NPAD - 1, lambda b, t: x1b[b][:, t * D:(t + 1) * D], D)

            pairs(pool, PAIRS, xd_body)

            pool.wait_ge(S["ext_stored"], 16 * (CH + 2))
            pool.wait_ge(S["consts_stored"], 16)
            for r in range(2):
                opened(r)
                if r:
                    pool.wait_ge(S["idx_made"], 1)
                idx = stage_i[0] if r == 0 else gi[GI[r]]
                table, bound, width = (ext, NPAD - 1, XW) if r == 0 else (tab_h1, EPAD + P - 1, D)
                copy_idx(1 + r, 0, 0, idx, (1 + r) * T * LB)

                def dense_in(i, b):
                    need(pool, ld["ld_xin"][b], 16 * (r * PAIRS + i + 1))
                    need(pool, LS["LA"]["LA_centred"], r * CH + 2 * i + b)
                    pool.tensor_tensor(yd[0][:, :, :], xin[b][:, :, :], relu_b[1][:, :].unsqueeze(1).broadcast_to([P, T, D]),
                                       ALU.add).then_inc(S["d_y"], 1)

                def gc_body(i):
                    for b in range(2):
                        first = isinstance(i, int) and i == 0 and b == 0
                        need(pool, S["gc_msg"], r * CH + 2 * i + b - 1)
                        gathers(1 + r, i, b, idx, table, bound, lambda b, t: gs[b][:, t, :], width,
                                None if first else lambda: dense_in(i - 1 + b, 1 - b))

                if r == 0:
                    pool.wait_ge(S["prepared"], 1)
                pairs(pool, PAIRS, gc_body)
                dense_in(PAIRS - 1, 1)
                fix(r)

            for l in range(3):
                r = 2 + l
                if l == 0:
                    for q in range(4):
                        pool.wait_ge(st_x1[q], 16 * 2 * QUADS)
                elif l == 1:
                    dense_done(pool)
                opened(r)
                idx = gi[GI[r]]
                copy_idx(1 + r, 0, 0, idx, (1 + r) * T * LB)

                def scatters(i, b):
                    c = 2 * i + b
                    need(pool, S["oidx_copied"], c + 1)
                    need(pool, LS["LE"]["LE_out"], CH + c + 1)
                    for t in range(T):
                        pool.indirect_dma_start(out=out, out_offset=bass.IndirectOffsetOnAxis(ap=oidxb[b][:, t:t + 1], axis=0),
                                                in_=hnew[b][:, t, :], in_offset=None, bounds_check=NPAD - 1,
                                                oob_is_err=False).then_inc(ld["scat"][b], 16)

                def copy_oidx(i, b):
                    need(pool, ld["scat"][b], 16 * T * i)
                    pool.tensor_copy(oidxb[b][:, :], gi[3][:, bass.ds((2 * i + b) * T, T)]).then_inc(S["oidx_copied"], 1)

                def t_body(i):
                    for b in range(2):
                        out_too = l == 2 and not (isinstance(i, int) and i == 0)
                        if out_too:
                            copy_oidx(i - 1, b)
                        need(pool, S["t_trg"], l * CH + 2 * i + b - 1)
                        gathers(1 + r, i, b, idx, tab[l], NPAD + EPAD - 1, lambda b, t: gt[b][:, t * D:(t + 1) * D], D)
                        if out_too:
                            scatters(i - 1, b)

                pairs(pool, PAIRS, t_body)
                if l == 2:
                    for b in range(2):
                        copy_oidx(PAIRS - 1, b)
                        scatters(PAIRS - 1, b)
                fix(r)
            pool.wait_ge(S["fx_scatter"], 16 * 5)

        @block.tensor
        def _(pe):
            def onehot_products(k, b, lhs, rhs, start, stop):
                for h in range(2):
                    m = pe.matmul(ps[k][:, h * 512:h * 512 + EC], lhs, rhs(h), start=start, stop=stop,
                                  skip_group_check=True)
                return m

            pe.wait_ge(S["onehots_ready"], 1)
            for k in range(2):
                onehot_products(k, 0, zero16[:, 0:P], lambda h: zero16[:, :], True, False)

            def count(i):
                for q in range(4):
                    pe.wait_ge(S["onehots_ready"], 2 + 4 * i + q)
                    pe.wait_ge(S["hi_ready"], 1 + 4 * i + q)
                    for k in range(2):
                        m = onehot_products(k, q, oh_hi[q][k][:, :],
                                            lambda h, k=k, q=q: oh[q][k][:, h * EC:(h + 1) * EC], False, False)
                    m.then_inc(S["onehots_used"], 1)

            pairs(pe, EC // 4, count)
            for k in range(2):
                m = onehot_products(k, 0, zero16[:, 0:P], lambda h: zero16[:, :], False, True)
            m.then_inc(S["counts_done"], 1)
            pe.wait_ge(S["totals_ready"], 1)
            pe.matmul(psC[:, 0:1], below[:, :], offs[:, 0:1], start=True, stop=True).then_inc(S["offset_done"], 1)

            def turn(n, src3, count, dst, rows_, done):
                for k in range(count):
                    t = pe.transpose(dst[0:src3(k).shape[1], k * rows_:(k + 1) * rows_], src3(k), ident[0:rows_, 0:rows_])
                t.then_inc(done, 1)

            for d in range(2):
                pe.wait_ge(S["deg_tail"], d + 1)
                turn(d, lambda k: tails[:, 3 * k, :], 2, psC, P, S["degT"])
                pe.wait_ge(S["deg_carry"], d + 1)
                pe.transpose(psC[:, 0:D], fc[:, 0, :], ident[0:D, 0:D]).then_inc(S["deg_back"], 1)

            pe.wait_ge(S["w_loaded"], W_LOADED)

            def fix(r):
                t_round = r >= 2
                n = r + 1
                ks = range(4) if t_round else (0, 3)
                pe.wait_ge(S["fx_tail"], n)
                for k in ks:
                    t = pe.transpose(psA[0:D, k * P:(k + 1) * P], tails[:, k, :], ident[:, :])
                t.then_inc(S["fx_tailT"], 1)
                pe.wait_ge(S["fx_carry"], n)
                for k in range(3 if t_round else 1):
                    t = pe.transpose(psA[:, k * D:(k + 1) * D], fc[:, k, :], ident[0:D, 0:D])
                t.then_inc(S["fx_back"], 1)
                pe.wait_ge(S["fx_z"], n)
                pe.transpose(psB[0:D, 0:P], fz[:, 0, :], ident[:, :]).then_inc(S["fx_zT"], 1)
                pe.wait_ge(S["fx_zTc"], n)
                w = wqs[r - 2] if t_round else wgc[r]
                pe.matmul(psC[:, 0:w.shape[1]], fT[:, :], w[:, :], start=True, stop=True).then_inc(S["fx_mm"], 1)
                if 1 <= r <= 3:
                    pe.wait_ge(S["fx_hT"], r)
                    for k in range(2):
                        t = pe.transpose(psA[0:D, k * P:(k + 1) * P], tails[:, k, :], ident[:, :])
                    t.then_inc(S["fx_hTr"], 1)
                    pe.wait_ge(S["fx_ho"], r)
                    pe.transpose(psB[:, 0:D], fc[:, 0, :], ident[0:D, 0:D]).then_inc(S["fx_hTr"], 1)

            def products(to, width, lhs, w, done):
                for t in range(T):
                    m = pe.matmul(to[:, t * width:(t + 1) * width], lhs(t), w, start=True, stop=True)
                m.then_inc(done, 1)

            def pair_transposes(to, tiles, done):
                settle(pe)
                for t in range(0, T, 2):
                    w = min(2, T - t)
                    m = pe.transpose(to[0:w * D, t // 2 * P:(t // 2 + 1) * P], tiles(t, w), ident[:, :])
                m.then_inc(done, 1)

            def pair_products(to, lhs, k, done):
                pe.matmul(to[:, 0:HC], ones16[:, :], bias3[k][:, :], start=True, stop=False, skip_group_check=True)
                for t in range(0, T, 2):
                    w = min(2, T - t) * D
                    m = pe.matmul(to[:, t * D:t * D + w], lhs[0:w, t // 2 * P:(t // 2 + 1) * P], wpair[k][0:w, 0:w],
                                  start=False, stop=t + 2 >= T, skip_group_check=True)
                m.then_inc(done, 1)

            def turn_dense(s, k, src_t, ready):
                if s.dense:
                    pe.wait_ge(ready, s.n)
                    need(pe, S[f"d_trc{k}"], s.n - 1)
                    pair_transposes(trd[k], lambda t, w: src_t[:, t:t + w, :].rearrange("p t f -> p (t f)"), S[f"d_tr{k}"])

            def multiply_dense(s, k, read):
                if s.dense:
                    pe.wait_ge(S[f"d_trc{k}"], s.n)
                    need(pe, read, s.n - 1)
                    pair_products(mmd[k], nT[k], k, S[f"d_mm{k}"])

            def gc_step(r, i, j, edges=True):
                s, p0, p1 = (Step(r, i, j, lag) for lag in range(3))
                turn_dense(p1, 2, t2d[p1.b], S["d_pre1"])
                turn_dense(p0, 1, t1d[p0.b], S["d_pre0"])
                turn_dense(s, 0, x1d[s.q], LS["LA"]["LA_out"])
                multiply_dense(p1, 2, S["d_res"])
                if edges:
                    pe.wait_ge(S["gc_z"], s.n)
                    need(pe, S["gc_zTc"], s.n - 1)
                    pair_transposes(trz, lambda t, w: u1[:, t:t + w, :].rearrange("p t f -> p (t f)"), S["gc_zT"])
                multiply_dense(p0, 1, S["d_pre1"])
                multiply_dense(s, 0, S["d_pre0"])
                if edges:
                    pe.wait_ge(S["gc_zTc"], s.n)
                    need(pe, S["gc_relu"], s.n - 1)
                    pair_products(mmz, zT, 3 + r, S["gc_mm"])

            for r in range(2):
                quads(pe, r, gc_step)
                fix(r)
                if r == 1:
                    for j in range(3):
                        gc_step(2, 0, j, edges=False)

            def t_turn(l, i, b):
                n = l * CH + 2 * i + b + 1
                pe.wait_ge(S["t_hd"], n)
                need(pe, S["t_hdT"], n - 1)
                settle(pe)
                for t in range(T):
                    m = pe.transpose(psB[0:D, t * P:(t + 1) * P], slot(hd[b], t + 1), ident[:, :])
                m.then_inc(S["t_trh"], 1)
                pe.wait_ge(ld["gat"][b], (3 + l) * T * LB + 16 * T * (i + 1))
                need(pe, S["t_gT"], n - 1)
                pair_transposes(psA, lambda t, w: gt[b][:, t * D:(t + w) * D], S["t_trg"])
                pe.wait_ge(S["t_hdT"], n)
                need(pe, S["t_qs"], n - 1)
                products(psD, 2 * D, lambda t: hdT[:, t * P:(t + 1) * P], wqs[l][:, :], S["t_q"])

            for l in range(3):
                t_turn(l, 0, 0)

                def t_body(i):
                    for b in range(2):
                        n = l * CH + 2 * i + b + 1
                        pe.wait_ge(S["t_gT"], n)
                        pe.wait_ge(ld["ld_ea"][b], l * LB + 16 * (i + 1))
                        need(pe, S["t_prod"], n - 1)
                        need(pe, S["t_v"], n - 1)
                        at = (lambda t: T - 1 - t) if REVERSE[2 + l] else (lambda t: t)
                        products(psC, 2 * D, lambda t: kvin[b][:, at(t) * P:(at(t) + 1) * P], wkv[l][:, :], S["t_kv"])
                        if not (isinstance(i, int) and i == PAIRS - 1 and b):
                            t_turn(l, i + b, 1 - b)

                pairs(pe, PAIRS, t_body)
                fix(2 + l)

        @block.scalar
        def _(act):
            def ln_square(L, n, w, B):
                act.wait_ge(L[B + "_centred"], n)
                act.activation(w["sq"][:, :, :], w["xc"][:, :, :], ACT.Square).then_inc(L[B + "_squared"], 1)

            def ln_squares_summed(L, n, w, B):
                act.wait_ge(L[B + "_centred"], n)
                for t in range(T):
                    m = act.activation(w["sq"][:, t, :], w["xc"][:, t, :], ACT.Square, accum_out=w["ss"][:, t:t + 1])
                m.then_inc(L[B + "_spread"], 1)

            def ln_std(L, n, w, B):
                act.wait_ge(L[B + "_spread"], n)
                act.activation(w["std"][:, :], w["ss"][:, :], ACT.Sqrt, scale=1.0 / D, bias=eps_t[:, 0:1]
                               ).then_inc(L[B + "_std"], 1)

            act.wait_ge(S["onehots_ready"], 1)

            def measure(i, q):
                need(act, S["hi_ready"], 4 * i + q - 3)
                act.activation(far[q][:, :], io_hi[:, :], ACT.Abs, bias=te[1][:, bass.ds(4 * i + q, 1)]
                               ).then_inc(S["hi_far"], 1)

            measure(0, 0)

            def his(i):
                for q in range(4):
                    j = 4 * i + q
                    if not (isinstance(i, int) and j == EC - 1):
                        measure(i + (q + 1) // 4, (q + 1) % 4)
                    act.wait_ge(S["hi_far"], j + 1)
                    need(act, S["onehots_used"], j - 3)
                    act.activation(oh_hi[q][0][:, :], far[q][:, :], ACT.Relu, scale=-1.0, bias=one_t[:, 0:1]
                                   ).then_inc(S["hi_ready"], 1)

            pairs(act, EC // 4, his)

            act.wait_ge(S["sqrt_in"], 1)
            act.activation(tn[0][:, :], tn[0][:, :], ACT.Sqrt).then_inc(S["sqrt_done"], 1)
            act.wait_ge(S["aux_done"], 1)
            for k in range(2):
                cols = slice(k * EC, (k + 1) * EC)
                act.dma_start(ext.rearrange("(p c) f -> p c f", p=P)[:, cols, D:XW], aux[:, cols, :]).then_inc(S["ext_stored"], 16)
            act.wait_ge(S["relu_made"], 1)
            act.dma_start(tab_h1[EPAD:EPAD + P, :], relu_b[0][:, :]).then_inc(S["consts_stored"], 16)
            for d in range(2):
                act.wait_ge(S["sqrt_in"], d + 2)
                act.activation(te[1][:, :], te[0][:, :], ACT.Sqrt).then_inc(S["sqrt_done"], 1)

            def fill_mask(c, b, d, done):
                act.copy(maskF[b][:, :].rearrange("p (f s) -> p f s", s=SL),
                         mask8f[d][:, bass.ds(c * SL, SL)].unsqueeze(1).broadcast_to([P, D, SL])).then_inc(done, 1)

            def fix(r):
                t_round = r >= 2
                n = r + 1
                if t_round:
                    act.wait_ge(S["fx_d"], 2 * (r - 1) - 1)
                    act.activation(fe[:, :, :], fd[:, :, :], ACT.Exp).then_inc(S["fx_e"], 1)
                    act.wait_ge(S["fx_d"], 2 * (r - 1))
                    act.activation(fee[:, :, :], fdd[:, :, :], ACT.Exp).then_inc(S["fx_e"], 1)
                act.wait_ge(S["fx_zT"], n)
                act.copy(fT[0:D, :], psB[0:D, 0:P]).then_inc(S["fx_zTc"], 1)
                if not t_round:
                    act.wait_ge(S["fx_mm"], n)
                    act.activation(fz[:, 1, :], psC[:, 0:D], ACT.Relu).then_inc(S["fx_relu"], 1)
                if r in (1, 4):
                    k = 2 * CH + (1 if r == 1 else 2)
                    ln_square(LS["LA"], k, fln, "LA")
                    ln_std(LS["LA"], k, fln, "LA")

            def dense_neg(s, k):
                if s.dense:
                    act.wait_ge(S[f"d_mm{k}"], s.n)
                    need(act, S[f"d_pre{k}"], s.n - 1)
                    act.activation(flat(neg[k]), mmd[k][:, 0:HC], ACT.Relu, scale=-1.0).then_inc(S[f"d_neg{k}"], 1)

            def dense_turned(s, k):
                if s.dense:
                    act.wait_ge(S[f"d_tr{k}"], s.n)
                    need(act, S[f"d_mm{k}"], s.n - 1)
                    copy_pairs(nT[k], trd[k], S[f"d_trc{k}"])

            def copy_pairs(to, of, done):
                act.copy(to[:, 0:3 * P], of[:, 0:3 * P])
                act.copy(to[0:D, 3 * P:4 * P], of[0:D, 3 * P:4 * P]).then_inc(done, 1)

            def gc_relu(e):
                if not e.edges:
                    return
                act.wait_ge(S["gc_mm"], e.n)
                if e.r == 0:
                    need(act, ld["st_hn"][e.b], 16 * e.h)
                    act.activation(flat(hnew[e.b]), mmz[:, 0:HC], ACT.Relu).then_inc(S["gc_relu"], 1)
                else:
                    need(act, S["gc_y"], e.c)
                    act.activation(flat(u2), mmz[:, 0:HC], ACT.Relu).then_inc(S["gc_relu"], 1)

            def row_square(e):
                if e.r == 1 and e.edges:
                    ln_squares_summed(LS["LE"], e.c + 1, lnb["lne"], "LE")

            def row_std(e):
                if e.r == 1 and e.edges:
                    ln_std(LS["LE"], e.c + 1, lnb["lne"], "LE")

            def gc_step(r, i, j, edges=True):
                s, p0, p1, o = (Step(r, i, j, lag) for lag in range(4))
                e, e2 = p0, p1
                dense_neg(p1, 1)
                if s.dense:
                    ln_squares_summed(LS["LA"], s.n, lnb["lna"], "LA")
                dense_neg(p0, 0)
                if edges:
                    need(act, S["gc_agg"], s.n - 2)
                    fill_mask(s.c, s.b, int(REVERSE[r]), S["gc_maskF"])
                if s.dense:
                    ln_std(LS["LA"], s.n, lnb["lna"], "LA")
                if edges:
                    gc_relu(e)
                dense_turned(p1, 2)
                if o.dense:
                    ln_square(LS["LB"], o.n, lnb["lnb"], "LB")
                dense_turned(p0, 1)
                row_std(e2)
                if o.dense:
                    ln_std(LS["LB"], o.n, lnb["lnb"], "LB")
                dense_turned(s, 0)
                if edges:
                    act.wait_ge(S["gc_zT"], s.n)
                    need(act, S["gc_mm"], s.n - 1)
                    copy_pairs(zT, trz, S["gc_zTc"])
                    row_square(e)

            for r in range(2):
                quads(act, r, gc_step)
                e, e2 = Step(r, QUADS, 0, 1), Step(r, QUADS, 0, 2)
                gc_relu(e)
                row_std(e2)
                row_square(e)
                row_std(e)
                fix(r)
                if r == 1:
                    for j in range(3):
                        gc_step(2, 0, j, edges=False)

            def t_mask(l, c, b, n):
                need(act, S["t_hd"], n - 2)
                fill_mask(c, b, int(REVERSE[2 + l]), S["t_maskF"])

            tiles = lambda ap: ap.rearrange("p (t e) -> p t e", e=P)

            def unpair(to, of, done):
                act.copy(to[:, 0:T:2, :], tiles(of[0:D, 0:4 * P]))
                act.copy(to[:, 1:T:2, :], tiles(of[D:2 * D, 0:3 * P])).then_inc(done, 1)

            def t_hdT(n, b):
                act.wait_ge(S["t_trh"], n)
                need(act, S["t_q"], n - 1)
                act.copy(hdT[0:D, :], psB[0:D, 0:T * P]).then_inc(S["t_hdT"], 1)

            def t_gT(l, n, b):
                act.wait_ge(S["t_trg"], n)
                need(act, S["t_kv"], n - 2)
                unpair(mem(tiles(kvin[b][0:D, :]), REVERSE[2 + l]), psA, S["t_gT"])

            def t_qs(n, b):
                act.wait_ge(S["t_q"], n)
                need(act, S["t_u2"], n - 2)
                act.copy(qs[b][:, :, :].rearrange("p t f -> p (t f)"), psD[:, 0:T * 2 * D]).then_inc(S["t_qs"], 1)

            for l in range(3):
                H = HEADS[l]
                for c in range(2):
                    t_mask(l, c, c, l * CH + c + 1)
                t_hdT(l * CH + 1, 0)
                t_gT(l, l * CH + 1, 0)
                t_qs(l * CH + 1, 0)
                t_mask(l, 2, 0, l * CH + 3)

                def t_body(i):
                    for b in range(2):
                        c = 2 * i + b
                        n = l * CH + c + 1
                        left = CH - c if isinstance(i, int) else CH
                        if left > 1:
                            t_hdT(n + 1, 1 - b)
                        act.wait_ge(S["t_prod"], n)
                        need(act, S["t_av"], n - 2)
                        act.copy(vs[b][:, :, :], k3[:, :, D:2 * D]).then_inc(S["t_v"], 1)
                        if left > 1:
                            t_gT(l, n + 1, 1 - b)
                        act.wait_ge(S["t_d"], n)
                        act.activation(e8[:, :, 0:H * SL], d8[:, :, 0:H * SL], ACT.Exp).then_inc(S["t_e"], 1)
                        need(act, S["t_agg"], n - 1)
                        act.wait_ge(S["t_e"], n)
                        act.copy(cF[:, :].rearrange("p (h c s) -> p h c s", h=H, s=SL),
                                 e8[:, 0, 0:H * SL].rearrange("p (h s) -> p h s", h=H).unsqueeze(2)
                                 .broadcast_to([P, H, D // H, SL])).then_inc(S["t_cF"], 1)
                        if left > 1:
                            t_qs(n + 1, 1 - b)
                        if left > 3:
                            t_mask(l, c + 3, 1 - b, n + 3)
                        if l == 2:
                            ln_squares_summed(LS["LE"], CH + c + 1, lnb["lne"], "LE")
                            ln_std(LS["LE"], CH + c + 1, lnb["lne"], "LE")

                pairs(act, PAIRS, t_body, tail=2)
                fix(2 + l)

        @block.vector
        def _(v):
            order = Order(v, S["dve_order"])

            def ln_sum(L, n, w, B, y):
                v.tensor_reduce(w["sum"][:, :], y, AX, ALU.add).then_inc(L[B + "_sum"], 1)

            def ln_subtract(L, n, w, B, y):
                v.wait_ge(L[B + "_sum"], n)
                v.scalar_tensor_tensor(out=w["xc"][:, :, :], in0=bc(w["sum"][:, :], D), scalar=-1.0 / D, in1=y,
                                       op0=ALU.mult, op1=ALU.add).then_inc(L[B + "_centred"], 1)

            def ln_centre(L, n, w, B, y):
                ln_sum(L, n, w, B, y)
                ln_subtract(L, n, w, B, y)

            def ln_spread(L, n, w, B, squared=None):
                v.wait_ge(L[B + "_squared"], squared or n)
                v.tensor_reduce(w["ss"][:, :], w["sq"][:, :, :], AX, ALU.add).then_inc(L[B + "_spread"], 1)

            def ln_scale(L, n, w, B, to):
                v.wait_ge(L[B + "_std"], n)
                v.reciprocal(w["rstd"][:, :], w["std"][:, :]).then_inc(L[B + "_rstd"], 1)
                v.wait_ge(L[B + "_rstd"], n)
                v.tensor_tensor(to, w["xc"][:, :, :], bc(w["rstd"][:, :], D), ALU.mult).then_inc(L[B + "_out"], 1)

            v.wait_ge(S["edges_loaded"], 64)
            v.wait_ge(S["pool_consts"], 1)
            for k in range(4):
                order(v.tensor_copy(ef[:, k, :], stage_i[k][:, :]))
            for k in range(2):
                hi, lo = hl[k][0][:, :], hl[k][1][:, :]
                e, q, t = ef[:, k, :], te[0][:, :], te[1][:, :]
                order(v.tensor_scalar(q, e, 1.0 / NN, None, ALU.mult))
                order(v.tensor_copy(qi[:, :], q))
                order(v.tensor_copy(hi, qi[:, :]))
                order(v.scalar_tensor_tensor(out=lo, in0=hi, scalar=-float(NN), in1=e, op0=ALU.mult, op1=ALU.add))
                for op, sign in ((ALU.is_lt, 1.0), (ALU.is_ge, -1.0)):
                    order(v.tensor_scalar(t, lo, 0.0 if sign > 0 else float(NN), None, op))
                    order(v.scalar_tensor_tensor(out=hi, in0=t, scalar=-sign, in1=hi, op0=ALU.mult, op1=ALU.add))
                    order(v.scalar_tensor_tensor(out=lo, in0=t, scalar=sign * NN, in1=lo, op0=ALU.mult, op1=ALU.add))
            order(v.tensor_scalar(te[1][:, :], hl[0][0][:, :], -1.0, None, ALU.mult))
            v.memset(zero16[:, :], 0.0).then_inc(S["onehots_ready"], 1)

            def onehots(i):
                for q in range(4):
                    j = 4 * i + q
                    need(v, S["onehots_used"], j - 3)
                    for k in range(2):
                        v.tensor_scalar(oh[q][k][:, :], io_lo[:, :], hl[k][1][:, bass.ds(j, 1)], None, ALU.is_equal)
                    v.tensor_scalar(oh_hi[q][1][:, :], io_hi[:, :], hl[1][0][:, bass.ds(j, 1)], None, ALU.is_equal
                                    ).then_inc(S["onehots_ready"], 1)

            pairs(v, EC // 4, onehots)

            counts = [ps[k][:, :].rearrange("p (h w) -> p h w", h=2)[:, :, 0:EC] for k in range(2)]
            two = lambda t: t[:, :].rearrange("p (h w) -> p h w", h=2)
            root, indeg, has, cum, first = tn
            v.wait_ge(S["counts_done"], 1)
            v.tensor_scalar(two(root), counts[0], 1.0, None, ALU.max).then_inc(S["sqrt_in"], 1)
            order(v.tensor_copy(two(indeg), counts[1]))
            order(v.memset(ones[:, :], 1.0))
            order(v.tensor_tensor_scan(cum[:, :], ones[:, :], indeg[:, :], 0.0, ALU.mult, ALU.add))
            v.tensor_copy(offs[:, 0:1], cum[:, NN - 1:NN]).then_inc(S["totals_ready"], 1)
            order(v.tensor_scalar(has[:, :], indeg[:, :], 0.5, None, ALU.is_ge))
            v.wait_ge(S["sqrt_done"], 1)
            order(v.reciprocal(aux[:, :, 0], root[:, :]))
            v.wait_ge(S["offset_done"], 1)
            order(v.tensor_copy(offs[:, 1:2], psC[:, 0:1]))
            order(v.tensor_scalar(cum[:, :], cum[:, :], offs[:, 1:2], -1.0, ALU.add, ALU.add))
            order(v.scalar_tensor_tensor(out=first[:, :], in0=cum[:, :], scalar=1.0, in1=indeg[:, :], op0=ALU.add, op1=ALU.subtract))
            order(v.tensor_scalar(offs[:, 0:1], io_part[:, :], float(EPAD), None, ALU.add))
            order(v.tensor_scalar(root[:, :], cum[:, :], offs[:, 0:1], None, ALU.subtract))
            order(v.tensor_tensor(root[:, :], root[:, :], has[:, :], ALU.mult))
            order(v.tensor_scalar(aux[:, :, 1], root[:, :], offs[:, 0:1], None, ALU.add))
            for k, pos in ((2, cum), (3, first)):
                order(v.scalar_tensor_tensor(out=root[:, :], in0=pos[:, :], scalar=float(NPAD), in1=io_node[:, :],
                                             op0=ALU.add, op1=ALU.subtract))
                order(v.tensor_tensor(root[:, :], root[:, :], has[:, :], ALU.mult))
                v.tensor_tensor(aux[:, :, k], root[:, :], io_node[:, :], ALU.add).then_inc(S["aux_done" if k == 3 else "aux_two"], 1)
                v.wait_ge(S["aux_done" if k == 3 else "aux_two"], 1)
            v.wait_ge(S["w_loaded"], W_LOADED)
            for l in range(3):
                order(v.tensor_scalar(wqs[l][:, 0:D], wqs[l][:, 0:D], float((D // HEADS[l]) ** -0.5), None, ALU.mult))
            for k in range(5):
                rest = braw[k]
                for p in range(3):
                    order(v.tensor_copy(b16[p][:, :], rest[:, :]))
                    if p < 2:
                        order(v.tensor_tensor(bsplit[p][:, :], rest[:, :], b16[p][:, :], ALU.subtract))
                        rest = bsplit[p]
                    at = 32 * p
                    order(v.tensor_copy(bias3[k][at:at + 1, :].rearrange("p (t f) -> p t f", f=D),
                                        b16[p][at:at + 1, :].unsqueeze(1).broadcast_to([1, T, D])))
            order(v.tensor_scalar(slope[:, 1:2], slope[:, 0:1], -1.0, None, ALU.add))
            order(v.tensor_scalar(slope[:, 2:3], slope[:, 0:1], -1.0, 1.0, ALU.mult, ALU.add))
            order(v.tensor_scalar(relu_b[1][:, :], relu_b[1][:, :], 0.0, None, ALU.max))
            v.tensor_scalar(relu_b[0][:, :], relu_b[0][:, :], 0.0, None, ALU.max).then_inc(S["relu_made"], 1)

            order(v.memset(m_all[:, :, :], 0.0))
            order(v.memset(s_all[:, :, :], 0.0))
            order(v.memset(fr[:, :, :], 0.0))
            order(v.tensor_tensor(hl[0][0][:, :], ef[:, 1, :], ef[:, 2, :], ALU.is_equal))
            order(v.tensor_tensor(hl[0][1][:, :], ef[:, 1, :], ef[:, 3, :], ALU.is_equal))
            go, end, lead = hl[1][0], hl[1][1], te[2]
            chunks = lambda t: t[:, :].rearrange("p (c t) -> p c t", t=T)
            flat8 = lambda t: t[:, :, :].rearrange("p c s -> p (c s)")

            def total(to, in0, in1):
                order(v.tensor_tensor(fsel[:, :, :], in0, in1, ALU.mult))
                order(v.tensor_reduce(to, flat8(fsel), AX, ALU.add))

            def carry_over(d, k):
                order(v.tensor_tensor_scan(fr[:, k, 1:P + 1], ft[:, 3, :], ft[:, k, :], 0.0, ALU.mult, ALU.add))

            for d in range(2):
                order(v.tensor_copy(go[:, :], mem(hl[0][d][:, :], d)))
                order(v.tensor_scalar(end[:, :], mem(hl[0][1 - d][:, :], d), -1.0, 1.0, ALU.mult, ALU.add))
                order(v.tensor_scalar(new[d][:, :], go[:, :], -1.0, 1.0, ALU.mult, ALU.add))
                order(v.memset(mask8[d][:, :, :], 0.0))
                order(v.tensor_copy(mask8[d][:, :, 1:SL], chunks(go)))
                order(v.memset(pen16[d][:, :, :, :], -BIG))
                for h in range(2):
                    order(v.tensor_scalar(pen16[d][:, :, h, 1:SL], chunks(new[d]), -BIG, None, ALU.mult))
                order(v.memset(te[0][:, :], 0.0))
                order(v.tensor_tensor_scan(lead[:, :], go[:, :], te[0][:, :], 1.0, ALU.mult, ALU.add))
                order(v.tensor_copy(cont_all[d][:, :], lead[:, EC - 1:EC]))
                order(v.memset(fmask[d][:, :, :], 0.0))
                order(v.tensor_tensor(fmask[d][:, :, 1:SL], chunks(lead), chunks(end), ALU.mult))
                order(v.tensor_reduce(fixed[d][:, 0:1], flat8(fmask[d]), AX, ALU.add))
                order(v.tensor_scalar(fixed[d][:, 1:2], fixed[d][:, 0:1], -1.0, 1.0, ALU.mult, ALU.add))
                order(v.tensor_reduce(slotm[d][:, :], fmask[d][:, :, :].rearrange("p c s -> p s c"), AX, ALU.add))
                total(fsc[:, 0:1], fmask[d][:, :, :], io_blk[:, :, :])
                total(fsc[:, 1:2], fmask[d][:, :, :], io_row[d][:, :, :])
                order(v.scalar_tensor_tensor(out=fsc[:, 2:3], in0=fixed[d][:, 1:2], scalar=float(EPAD + P), in1=fsc[:, 1:2],
                                             op0=ALU.mult, op1=ALU.add))
                order(v.scalar_tensor_tensor(out=fsc[:, 3:4], in0=fixed[d][:, 1:2], scalar=float(EPAD), in1=fsc[:, 1:2],
                                             op0=ALU.mult, op1=ALU.add))
                order(v.tensor_scalar(fsc[:, 3:4], fsc[:, 3:4], float(NPAD), None, ALU.add))
                order(v.tensor_copy(fixi[d][:, :], fsc[:, 0:4]))
                if d == 0:
                    order(v.tensor_tensor(fsel[:, :, 1:SL], fmask[0][:, :, 1:SL], ef[:, 1, :].rearrange("p (c t) -> p c t", t=T), ALU.mult))
                    order(v.memset(fsel[:, :, 0:1], 0.0))
                    order(v.tensor_reduce(fsc[:, 0:1], flat8(fsel), AX, ALU.add))
                    order(v.scalar_tensor_tensor(out=fsc[:, 0:1], in0=fixed[0][:, 1:2], scalar=float(NPAD), in1=fsc[:, 0:1],
                                                 op0=ALU.mult, op1=ALU.add))
                    order(v.tensor_copy(fixo[:, :], fsc[:, 0:1]))
                order(v.tensor_tensor_scan(te[0][:, :], go[:, :], ones[:, 0:EC], 0.0, ALU.mult, ALU.add))
                order(v.tensor_copy(tails[:, 0, :], te[0][:, EC - 1:EC].broadcast_to([P, D])))
                v.tensor_copy(tails[:, 3, :], cont_all[d][:, :].broadcast_to([P, D])).then_inc(S["deg_tail"], 1)
                v.wait_ge(S["degT"], d + 1)
                order(v.tensor_copy(ft[:, 0, :], mem(psC[0:D, 0:P], d)))
                order(v.tensor_copy(ft[:, 3, :], mem(psC[0:D, P:2 * P], d)))
                carry_over(d, 0)
                v.tensor_copy(fc[:, 0, :], mem(fr[:, 0, 0:P], d)).then_inc(S["deg_carry"], 1)
                v.wait_ge(S["deg_back"], d + 1)
                order(v.tensor_copy(carry[:, 0, :], psC[:, 0:D]))
                v.tensor_tensor_scan(te[0][:, :], go[:, :], ones[:, 0:EC], carry[:, 0, 0:1], ALU.mult, ALU.add
                                     ).then_inc(S["sqrt_in"], 1)
                v.wait_ge(S["sqrt_done"], d + 2)
                order(v.reciprocal(inn[d][:, :], te[1][:, :]))
            order(v.scalar_tensor_tensor(out=te[0][:, :], in0=hl[0][1][:, :], scalar=float(NPAD), in1=ef[:, 1, :],
                                         op0=ALU.mult, op1=ALU.add))
            order(v.tensor_copy(gi[3][:, :], te[0][:, :]))
            order(v.memset(d8[:, 0, :], -BIG))
            order(v.memset(d8[:, 1, :], 0.0))
            v.memset(e8[:, 1, :], 0.0).then_inc(S["prepared"], 1)

            GATHERED = (1, 3, 5, 7, 10)

            def pick(to, blk, d, done=None):
                order(v.tensor_tensor(fbm[:, :, :], blk[:, :].rearrange("p (f s) -> p f s", s=SL),
                                      slotm[d][:, :].unsqueeze(1).broadcast_to([P, D, SL]), ALU.mult))
                m = v.tensor_reduce(to, fbm[:, :, :], AX, ALU.add)
                m.then_inc(done, 1) if done else order(m)

            def fix(r):
                d = int(REVERSE[r])
                n = r + 1
                t_round = r >= 2
                l = r - 2
                H = HEADS[l] if t_round else 1
                heads = lambda ap: bc(ap, D // H)
                hc = lambda ap: ap.rearrange("p (h c) -> p h c", h=H)
                last = lambda t: t[:, CH, 0:H * SL].rearrange("p (h s) -> p h s", s=SL)[:, :, SL - 1]
                if t_round:
                    v.wait_ge(S["t_agg"], CH * (l + 1))
                    v.wait_ge(S["t_s"], CH * (l + 1))
                    order(v.tensor_copy(hc(tails[:, 1, :]), heads(last(s_all))))
                    order(v.tensor_copy(hc(tails[:, 2, :]), heads(last(m_all))))
                else:
                    v.wait_ge(S["gc_agg"], CH * (r + 1))
                order(v.tensor_copy(tails[:, 0, :], slot(aggF[1], SL - 1)))
                v.tensor_copy(tails[:, 3, :], cont_all[d][:, :].broadcast_to([P, D])).then_inc(S["fx_tail"], 1)
                v.wait_ge(S["fx_tailT"], n)
                for k in (range(4) if t_round else (0, 3)):
                    order(v.tensor_copy(ft[:, k, :], mem(psA[0:D, k * P:(k + 1) * P], d)))
                if t_round:
                    M, Mprev = fr[:, 2, 1:P + 1], fr[:, 2, 0:P]
                    order(v.tensor_scalar(fd[:, 0, :], ft[:, 3, :], BIG, -BIG, ALU.mult, ALU.add))
                    order(v.tensor_tensor_scan(M, fd[:, 0, :], ft[:, 2, :], 0.0, ALU.add, ALU.max))
                    order(v.tensor_tensor(fd[:, 1, :], Mprev, M, ALU.subtract))
                    order(v.tensor_tensor(fd[:, 0, :], fd[:, 0, :], fd[:, 1, :], ALU.add))
                    v.tensor_tensor(fd[:, 1, :], ft[:, 2, :], M, ALU.subtract).then_inc(S["fx_d"], 1)
                    v.wait_ge(S["fx_e"], 2 * l + 1)
                    for k in range(2):
                        order(v.tensor_tensor(ft[:, k, :], ft[:, k, :], fe[:, 1, :], ALU.mult))
                        order(v.tensor_tensor_scan(fr[:, k, 1:P + 1], fe[:, 0, :], ft[:, k, :], 0.0, ALU.mult, ALU.add))
                    v.tensor_copy(fc[:, :, :], fr[:, :, 0:P][:, :, ::-1] if d else fr[:, :, 0:P]).then_inc(S["fx_carry"], 1)
                else:
                    carry_over(d, 0)
                    v.tensor_copy(fc[:, 0, :], mem(fr[:, 0, 0:P], d)).then_inc(S["fx_carry"], 1)
                v.wait_ge(S["fx_back"], n)
                nk = 3 if t_round else 1
                order(v.tensor_copy(carry[:, 0:nk, :], psA[:, 0:nk * D].rearrange("p (k f) -> p k f", f=D)))
                v.wait_ge(S["fx_gather"], 16 * GATHERED[r])
                pick(pre[:, 0, :], fb, d)
                if not t_round:
                    order(v.memset(fsel[:, :, 0:1], 0.0))
                    order(v.tensor_tensor(fsel[:, :, 1:SL], fmask[d][:, :, 1:SL], chunks(inn[d]), ALU.mult))
                    order(v.tensor_reduce(fsc[:, 0:1], flat8(fsel), AX, ALU.add))
                    order(v.tensor_tensor(fz[:, 2, :], carry[:, 0, :], pre[:, 0, :], ALU.add))
                    v.tensor_scalar(fz[:, 0, :], fz[:, 2, :], fsc[:, 0:1], None, ALU.mult).then_inc(S["fx_z"], 1)
                    v.wait_ge(S["fx_relu"], n)
                    need(v, S["fx_scatter"], 16 * r)
                    if r == 0:
                        v.tensor_copy(frow[:, :], fz[:, 1, :]).then_inc(S["fx_row"], 1)
                        v.wait_ge(S["fx_row"], 1)
                        return
                    order(v.tensor_tensor(fz[:, 2, :], fz[:, 1, :], fxd[:, :], ALU.add))
                    y = fz[:, 2:3, :]
                else:
                    pick(fz[:, 0, :], fh, d, S["fx_z"])
                    for k, t in ((1, s_all), (2, m_all)):
                        for h in range(H):
                            total(fsc[:, h:h + 1], fmask[d][:, :, :], t[:, 1:CH + 1, h * SL:(h + 1) * SL])
                        order(v.tensor_copy(hc(pre[:, k, :]), heads(fsc[:, 0:H])))
                    order(v.tensor_tensor(fm2[:, :], carry[:, 2, :], pre[:, 2, :], ALU.max))
                    order(v.tensor_tensor(fdd[:, 0, :], carry[:, 2, :], fm2[:, :], ALU.subtract))
                    v.tensor_tensor(fdd[:, 1, :], pre[:, 2, :], fm2[:, :], ALU.subtract).then_inc(S["fx_d"], 1)
                    v.wait_ge(S["fx_e"], 2 * l + 2)
                    for k in range(2):
                        order(v.tensor_tensor(fz[:, 1 + k, :], carry[:, k, :], fee[:, 0, :], ALU.mult))
                        order(v.tensor_tensor(fz[:, 3, :], pre[:, k, :], fee[:, 1, :], ALU.mult))
                        order(v.tensor_tensor(fz[:, 1 + k, :], fz[:, 1 + k, :], fz[:, 3, :], ALU.add))
                    order(v.tensor_scalar(fz[:, 2, :], fz[:, 2, :], 1e-16, None, ALU.add))
                    order(v.reciprocal(fz[:, 2, :], fz[:, 2, :]))
                    order(v.tensor_tensor(fz[:, 1, :], fz[:, 1, :], fz[:, 2, :], ALU.mult))
                    v.wait_ge(S["fx_mm"], n)
                    order(v.tensor_tensor(fz[:, 1, :], fz[:, 1, :], psC[:, D:2 * D], ALU.add))
                    need(v, S["fx_scatter"], 16 * r)
                    if l < 2:
                        order(v.tensor_scalar(fz[:, 2, :], fz[:, 1, :], 0.0, slope[:, 1:2], ALU.min, ALU.mult))
                        v.tensor_tensor(frow[:, :], fz[:, 2, :], fz[:, 1, :], ALU.add).then_inc(S["fx_row"], 1)
                        v.wait_ge(S["fx_row"], n)
                    else:
                        pick(fz[:, 3, :], fx1, d)
                        order(v.tensor_tensor(fz[:, 1, :], fz[:, 1, :], fz[:, 3, :], ALU.add))
                        y = fz[:, 1:2, :]
                if r in (1, 4):
                    k = 2 * CH + (1 if r == 1 else 2)
                    L = LS["LA"]
                    ln_centre(L, k, fln, "LA", y)
                    ln_spread(L, k, fln, "LA", squared=k - 2 * CH)
                    ln_scale(L, k, fln, "LA", fz[:, 4:5, :])
                    v.wait_ge(L["LA_out"], k)
                    v.tensor_copy(frow[:, :], fz[:, 4, :]).then_inc(S["fx_row"], 1)
                    v.wait_ge(S["fx_row"], n)
                if r == 4:
                    return
                order(v.tensor_scalar(tails[:, 0, :], frow[:, :], fixed[d][:, 0:1], None, ALU.mult))
                v.tensor_copy(tails[:, 1, :], fixed[d][:, 1:2].broadcast_to([P, D])).then_inc(S["fx_hT"], 1)
                v.wait_ge(S["fx_hTr"], 2 * r - 1)
                for k in range(2):
                    order(v.tensor_copy(ft[:, k, :], mem(psA[0:D, k * P:(k + 1) * P], not d)))
                order(v.tensor_tensor_scan(fr[:, 0, 1:P + 1], ft[:, 1, :], ft[:, 0, :], 0.0, ALU.mult, ALU.add))
                v.tensor_copy(fc[:, 0, :], mem(fr[:, 0, 0:P], not d)).then_inc(S["fx_ho"], 1)
                v.wait_ge(S["fx_hTr"], 2 * r)
                need(v, ld["st_hd"][1], LB * (r - 1))
                order(v.tensor_copy(slot(hd[1], SL - 1), psB[:, 0:D]))

            def prelu_dense(s, k, to, stored):
                if s.dense:
                    v.wait_ge(S[f"d_neg{k}"], s.n)
                    need(v, stored, 16 * s.h)
                    need(v, S[f"d_tr{k + 1}"], s.n - 2)
                    v.scalar_tensor_tensor(out=flat(to), in0=flat(neg[k]), scalar=slope[:, 2:3], in1=mmd[k][:, 0:HC],
                                           op0=ALU.mult, op1=ALU.add).then_inc(S[f"d_pre{k}"], 1)

            def row_centre(e):
                if e.r == 1 and e.edges:
                    v.wait_ge(S["gc_relu"], e.n)
                    v.wait_ge(ld["ld_hrow"][e.b], 16 * (e.h - PAIRS + 1))
                    v.tensor_tensor(u3[:, :, :], mem(u2[:, :, :], True), hrow[e.b][:, :, :], ALU.add).then_inc(S["gc_y"], 1)
                    v.wait_ge(S["gc_y"], e.c + 1)
                    ln_centre(LS["LE"], e.c + 1, lnb["lne"], "LE", u3[:, :, :])

            def row_scale(e):
                if e.r == 1 and e.edges:
                    need(v, ld["st_hn"][e.b], 16 * e.h)
                    ln_scale(LS["LE"], e.c + 1, lnb["lne"], "LE", hnew[e.b][:, :, :])

            def gc_step(r, i, j, edges=True):
                s, p0, p1, o = (Step(r, i, j, lag) for lag in range(4))
                e, e2 = p0, p1
                c, n, b = s.c, s.n, s.b
                d = int(REVERSE[r]) if edges else 0
                cols = bass.ds(c * T, T)
                la = (LS["LA"], s.n, lnb["lna"], "LA")
                lb = (LS["LB"], o.n, lnb["lnb"], "LB")
                if edges:
                    v.wait_ge(ld["gat"][b], T * LB + 16 * T * (s.h + 1))
                    if r == 0:
                        v.tensor_copy(idx_f[:, :, cols], gs[b][:, :, D + 1:XW].rearrange("p t k -> p k t")).then_inc(S["gc_extract"], 1)
                        v.tensor_copy(norm_e[:, cols], gs[b][:, :, D]).then_inc(S["gc_extract"], 1)
                        norm = gs[b][:, :, D]
                    else:
                        norm = norm_r[:, cols]
                if s.dense:
                    v.wait_ge(S["d_y"], n)
                    ln_sum(*la, yd[0][:, :, :])
                if edges:
                    v.tensor_tensor(fj(msgF), gs[b][:, :, 0:D], bc(norm, D), ALU.mult).then_inc(S["gc_msg"], 1)
                    v.tensor_copy(slot(msgF, 0), slot(aggF[1 - b], SL - 1)).then_inc(S["gc_carry"], 1)
                if s.dense:
                    ln_subtract(*la, yd[0][:, :, :])
                if o.dense:
                    v.wait_ge(S["d_mm2"], o.n)
                    v.tensor_tensor(flat(yd[1]), flat(x1d[o.q]), mmd[2][:, 0:HC], ALU.add).then_inc(S["d_res"], 1)
                prelu_dense(p1, 1, t2d[p1.b], ld["st_t2"][p1.b])
                if o.dense:
                    v.wait_ge(S["d_res"], o.n)
                    ln_sum(*lb, yd[1][:, :, :])
                if o.dense:
                    ln_subtract(*lb, yd[1][:, :, :])
                prelu_dense(p0, 0, t1d[p0.b], ld["st_t1"][p0.b])
                if edges:
                    v.wait_ge(S["gc_maskF"], n)
                    v.wait_ge(S["gc_carry"], n)
                    need(v, ld["st_agg"][b], 16 * s.h)
                    v.tensor_tensor_scan(aggF[b][:, :], maskF[b][:, :], msgF[:, :], 0.0, ALU.mult, ALU.add
                                         ).then_inc(S["gc_agg"], 1)
                if s.dense:
                    need(v, st_x1[s.q], 16 * s.k)
                    ln_scale(*la, x1d[s.q][:, :, :])
                if o.dense:
                    ln_spread(*lb)
                if edges:
                    v.wait_ge(S["gc_agg"], n)
                    need(v, S["gc_zT"], n - 1)
                    v.tensor_tensor(u1[:, :, :], fj(aggF[b]), bc(inn[d][:, cols], D), ALU.mult).then_inc(S["gc_z"], 1)
                row_scale(e2)
                row_centre(e)
                if o.dense:
                    need(v, ld["st_od"][o.b], 16 * o.h)
                    ln_scale(*lb, od[o.b][:, :, :])

            for r in range(2):
                if r:
                    v.wait_ge(ld["st_agg"][1], LB * r)
                order(v.memset(slot(aggF[1], SL - 1), 0.0))

                quads(v, r, gc_step)
                e, e2 = Step(r, QUADS, 0, 1), Step(r, QUADS, 0, 2)
                row_scale(e2)
                row_centre(e)
                row_scale(e)
                if r == 0:
                    v.wait_ge(S["gc_extract"], 2 * CH)
                    order(v.tensor_copy(norm_r[:, :], norm_e[:, ::-1]))
                    order(v.tensor_copy(gi[0][:, :], idx_f[:, 0, :][:, ::-1]))
                    order(v.tensor_copy(gi[1][:, :], idx_f[:, 2, :]))
                    v.tensor_copy(gi[2][:, :], idx_f[:, 1, :][:, ::-1]).then_inc(S["idx_made"], 1)
                fix(r)
                if r == 1:
                    for j in range(3):
                        gc_step(2, 0, j, edges=False)

            mf = m_all[:, :, :].rearrange("p c s -> p (c s)")
            sf = s_all[:, :, :].rearrange("p c s -> p (c s)")

            def hd_prepare(l, i, b):
                c = 2 * i + b
                d = int(REVERSE[2 + l])
                v.wait_ge(ld["ld_hrow"][b], (1 + l) * LB + 16 * (i + 1))
                need(v, S["t_hd"], l * CH + c)
                v.tensor_tensor(fj(hp), mem(hrow[b][:, :, :], d), bc(new[d][:, bass.ds(c * T, T)], D), ALU.mult
                                ).then_inc(S["t_hp"], 1)

            def hd_carry(b):
                v.tensor_copy(slot(hp, 0), slot(hd[1 - b], SL - 1)).then_inc(S["t_hpc"], 1)

            def hd_scan(l, i, b):
                n = l * CH + 2 * i + b + 1
                v.wait_ge(S["t_maskF"], n)
                v.wait_ge(S["t_hpc"], n)
                need(v, S["t_trh"], n - 2)
                need(v, ld["st_hd"][b], l * LB + 16 * i)
                v.tensor_tensor_scan(hd[b][:, :], maskF[b][:, :], hp[:, :], 0.0, ALU.mult, ALU.add).then_inc(S["t_hd"], 1)

            def t_step(l, i, b):
                c = 2 * i + b
                n = l * CH + c + 1
                H = HEADS[l]
                HS = H * SL
                first = isinstance(i, int) and c == 0
                more = not (isinstance(i, int) and i == PAIRS - 1)
                nxt = (l, i + 1, b)
                mix = l < 2 and not first
                before = TOut(l, i - 1 + b, 1 - b) if mix else None
                hs = lambda ap: ap.rearrange("p (h s) -> p h s", s=SL)
                over = lambda ap: ap.unsqueeze(2).broadcast_to([P, H, D // H, T])
                m_old, m_new = mf[:, bass.ds(c * 2 * SL, HS)], mf[:, bass.ds((c + 1) * 2 * SL, HS)]
                s_old, s_new = sf[:, bass.ds(c * 2 * SL, HS)], sf[:, bass.ds((c + 1) * 2 * SL, HS)]
                pen = pen16[int(REVERSE[2 + l])][:, :, :, :].rearrange("p c h s -> p (c h s)")[:, bass.ds(c * 2 * SL, HS)]
                v.wait_ge(S["t_qs"], n)
                v.wait_ge(S["t_kv"], n)
                v.tensor_tensor(prod[:, :, :], qs[b][:, :, 0:D], k3[:, :, 0:D], ALU.mult).then_inc(S["t_prod"], 1)
                if mix:
                    before.guard()
                if more:
                    hd_prepare(*nxt)
                if mix:
                    before.invert()
                v.wait_ge(S["t_prod"], n)
                v.tensor_reduce(hs(alpha8[:, 0:HS])[:, :, 1:SL].rearrange("p h t -> p t h"),
                                prod[:, :, :].rearrange("p t (h c) -> p t h c", h=H), AX, ALU.add).then_inc(S["t_alpha"], 1)
                v.tensor_copy(hs(alpha8[:, 0:HS])[:, :, 0], hs(m_old)[:, :, SL - 1]).then_inc(S["t_acar"], 1)
                if more:
                    hd_carry(b)
                if mix:
                    before.divide()
                v.wait_ge(S["t_acar"], n)
                v.tensor_tensor_scan(m_new, pen, alpha8[:, 0:HS], 0.0, ALU.add, ALU.max).then_inc(S["t_m"], 1)
                if more:
                    hd_scan(*nxt)
                v.wait_ge(S["t_m"], n)
                v.tensor_tensor(hs(d8[:, 0, 0:HS])[:, :, 1:SL], hs(m_new)[:, :, 0:T], hs(m_new)[:, :, 1:SL], ALU.subtract
                                ).then_inc(S["t_d0"], 1)
                v.tensor_tensor(hs(d8[:, 1, 0:HS])[:, :, 1:SL], hs(alpha8[:, 0:HS])[:, :, 1:SL], hs(m_new)[:, :, 1:SL],
                                ALU.subtract)
                v.tensor_copy(slot(msgF, 0), slot(aggF[1 - b], SL - 1)).then_inc(S["t_avc"], 1)
                v.wait_ge(S["t_d0"], n)
                v.tensor_tensor(hs(d8[:, 0, 0:HS])[:, :, 1:SL], hs(d8[:, 0, 0:HS])[:, :, 1:SL], hs(pen)[:, :, 1:SL], ALU.add
                                ).then_inc(S["t_d"], 1)
                if mix:
                    before.skip()
                v.wait_ge(S["t_e"], n)
                v.tensor_copy(hs(e8[:, 1, 0:HS])[:, :, 0], hs(s_old)[:, :, SL - 1]).then_inc(S["t_scar"], 1)
                v.wait_ge(S["t_v"], n)
                v.tensor_tensor(wide(msgF, H, 1, SL), vs[b][:, :, :].rearrange("p t (h c) -> p h c t", h=H),
                                over(hs(e8[:, 1, 0:HS])[:, :, 1:SL]), ALU.mult).then_inc(S["t_av"], 1)
                if mix:
                    before.prelu()
                v.wait_ge(S["t_scar"], n)
                v.tensor_tensor_scan(s_new, e8[:, 0, 0:HS], e8[:, 1, 0:HS], 0.0, ALU.mult, ALU.add).then_inc(S["t_s"], 1)
                v.wait_ge(S["t_cF"], n)
                v.wait_ge(S["t_av"], n)
                v.wait_ge(S["t_avc"], n)
                need(v, ld["st_agg"][b], (2 + l) * LB + 16 * i)
                v.tensor_tensor_scan(aggF[b][:, :], cF[:, :], msgF[:, :], 0.0, ALU.mult, ALU.add).then_inc(S["t_agg"], 1)
                if mix:
                    before.add()
                if l == 2 or not more and b == 1:
                    TOut(l, i, b).all()

            def wide(t, H, lo, hi):
                return t[:, :].rearrange("p (h c s) -> p h c s", h=H, s=SL)[:, :, :, lo:hi]

            class TOut:

                def __init__(self, l, i, b):
                    self.l, self.i, self.b, self.c = l, i, b, 2 * i + b
                    self.n, self.H = l * CH + self.c + 1, HEADS[l]
                    self.HS = self.H * SL

                def guard(self):
                    v.wait_ge(S["t_s"], self.n)
                    v.tensor_scalar(r8[:, 0:self.HS], sf[:, bass.ds((self.c + 1) * 2 * SL, self.HS)], 1e-16, None, ALU.add
                                    ).then_inc(S["t_r0"], 1)

                def invert(self):
                    v.wait_ge(S["t_r0"], self.n)
                    v.reciprocal(r8[:, 0:self.HS], r8[:, 0:self.HS]).then_inc(S["t_r"], 1)

                def divide(self):
                    v.wait_ge(S["t_r"], self.n)
                    v.wait_ge(S["t_agg"], self.n)
                    rs = r8[:, 0:self.HS].rearrange("p (h s) -> p h s", s=SL)[:, :, 1:SL]
                    v.tensor_tensor(u1[:, :, :].rearrange("p t (h c) -> p h c t", h=self.H), wide(aggF[self.b], self.H, 1, SL),
                                    rs.unsqueeze(2).broadcast_to([P, self.H, D // self.H, T]), ALU.mult).then_inc(S["t_u1"], 1)

                def skip(self):
                    v.wait_ge(S["t_u1"], self.n)
                    v.tensor_tensor(u2[:, :, :], u1[:, :, :], qs[self.b][:, :, D:2 * D], ALU.add).then_inc(S["t_u2"], 1)

                def prelu(self):
                    v.wait_ge(S["t_u2"], self.n)
                    v.tensor_scalar(u3[:, :, :], u2[:, :, :], 0.0, slope[:, 1:2], ALU.min, ALU.mult).then_inc(S["t_u3"], 1)

                def add(self):
                    need(v, ld["st_hn"][self.b], (2 + self.l) * LB + 16 * self.i)
                    v.wait_ge(S["t_u3"], self.n)
                    v.tensor_tensor(mem(hnew[self.b][:, :, :], REVERSE[2 + self.l]), u3[:, :, :], u2[:, :, :], ALU.add
                                    ).then_inc(S["t_hn"], 1)

                def norm(self):
                    b, i, k = self.b, self.i, CH + self.c + 1
                    v.wait_ge(ld["ld_x1"][b], 16 * (i + 1))
                    v.wait_ge(S["t_u2"], self.n)
                    v.tensor_tensor(u3[:, :, :], u2[:, :, :], fj(x1b[b]), ALU.add).then_inc(S["t_y"], 1)
                    v.wait_ge(S["t_y"], self.c + 1)
                    ln_centre(LS["LE"], k, lnb["lne"], "LE", u3[:, :, :])
                    need(v, ld["scat"][b], 16 * T * i)
                    if isinstance(i, int) and i == 0:
                        v.wait_ge(ld["st_hn"][b], 4 * LB)
                    ln_scale(LS["LE"], k, lnb["lne"], "LE", hnew[b][:, :, :])

                def all(self):
                    self.guard()
                    self.invert()
                    self.divide()
                    self.skip()
                    if self.l == 2:
                        self.norm()
                    else:
                        self.prelu()
                        self.add()

            for l in range(3):
                v.wait_ge(ld["st_agg"][1], LB * (2 + l))
                order(v.memset(slot(aggF[1], SL - 1), 0.0))
                for b in range(2):
                    hd_prepare(l, 0, b)
                    hd_carry(b)
                    hd_scan(l, 0, b)

                def t_body(i):
                    for b in range(2):
                        t_step(l, i, b)

                pairs(v, PAIRS, t_body)
                fix(2 + l)


_L = [f"L1_gnn_{w}{k}" for k in range(3) for w in ("Wq", "bq", "Wk", "bk", "Wv", "bv", "We", "Ws", "bs")]
_INS = ["x", "src", "dst", "edge_attr_32", "L0_gnn_W1", "L0_gnn_b1", "L0_gnn_W2", "L0_gnn_b2", *_L, "L1_gnn_prelu_a"]


def kernel(**inputs):
    import numpy as np
    import concourse.bacc as bacc
    from concourse.bass_utils import run_bass_kernel_spmd

    given = {k: np.asarray(v) for k, v in inputs.items()}
    given["x"] = np.pad(given["x"], ((0, NPAD - N_NODES), (0, 0)))
    given["src"] = np.pad(given["src"], (0, EPAD - N_EDGES), constant_values=N_NODES)
    given["dst"] = np.pad(given["dst"], (1, EPAD - N_EDGES), constant_values=(-1, N_NODES))
    given["dst"] = np.pad(given["dst"], (0, 1), constant_values=N_NODES + 1)
    ea = np.pad(given["edge_attr_32"], ((0, EPAD - N_EDGES), (0, 0)))
    given["edge_attr_32"] = ea.reshape(P, EC, DE).transpose(2, 1, 0).reshape(DE, EC * P)
    given["L1_gnn_prelu_a"] = given["L1_gnn_prelu_a"].reshape(1)

    nc = bacc.Bacc("TRN2", target_bir_lowering=False, num_devices=1)
    arrays, aps = {}, {}
    for name in _INS:
        a = np.ascontiguousarray(given[name])
        arrays[f"in_{name}"] = a
        aps[name] = nc.dram_tensor(f"in_{name}", a.shape, mybir.dt.from_np(a.dtype), kind="ExternalInput").ap()
    out = nc.dram_tensor("out_0", (NPAD, D), F32, kind="ExternalOutput").ap()
    layers = [[aps[n] for n in _L[9 * k:9 * k + 9]] for k in range(3)]
    gnn_kernel(nc, aps["x"], aps["src"], aps["dst"], aps["edge_attr_32"], aps["L0_gnn_W1"], aps["L0_gnn_b1"],
               aps["L0_gnn_W2"], aps["L0_gnn_b2"], layers, aps["L1_gnn_prelu_a"], out)
    r = run_bass_kernel_spmd(nc, [arrays], core_ids=[0])
    return r.results[0]["out_0"][0:N_NODES]
```
